# Optimizing a Trainium2 kernel written in Bass

```python
import numpy as np
import jax
import jax.numpy as jnp

def _softmax(x, axis=-1):
    return jax.nn.softmax(x, axis=axis)

def _gelu(x):
    return jax.nn.gelu(x, approximate=True)

def _silu(x):
    return jax.nn.silu(x)

def _sigmoid(x):
    return jax.nn.sigmoid(x)

def _layernorm(x, axis=-1, eps=1e-05):
    m = jnp.mean(x, axis=axis, keepdims=True)
    v = jnp.var(x, axis=axis, keepdims=True)
    return (x - m) / jnp.sqrt(v + eps)

def _scatter_add(tgt, idx, src, axis=0):
    return tgt.at[idx].add(src)

def _segment_sum(src, seg, n):
    return jax.ops.segment_sum(src, seg, n)
kernel_name = 'mk_perceiver_d1_seqx_r4_ca8263'

def setup_inputs(seed: int=0):
    np.random.seed(seed)
    _w = jnp.asarray

    def _rec_inputs():
        import jax
        import jax.numpy as jnp
        _rk = jax.random.key(seed)
        x = -0.0005207 + 1.001 * jax.random.normal(jax.random.fold_in(_rk, 1), (1, 256, 1024), jnp.float32)
        _lenS = 256 - jax.random.randint(jax.random.fold_in(_rk, 7), (1,), 0, max(1, 256 // 4) + 1, jnp.int32)
        _lenS2 = 4096 - jax.random.randint(jax.random.fold_in(_rk, 8), (1,), 0, max(1, 4096 // 4) + 1, jnp.int32)
        _ctx_4096P = jax.random.normal(jax.random.fold_in(_rk, 11), (1, 16, 1024), jnp.float32)
        _ctx_4096c = jax.random.dirichlet(jax.random.fold_in(_rk, 511), 0.3 * jnp.ones((16,), jnp.float32), (1, 4096))
        _ctx_4096t = jnp.einsum('bsk,bkd->bsd', _ctx_4096c, _ctx_4096P)
        _ctx_4096t = _ctx_4096t * jax.lax.rsqrt(jnp.mean(jnp.square(_ctx_4096t)) + 1e-12) * 0.953939
        ctx_4096 = -0.00010331 + 0.999899 * (_ctx_4096t + 0.3 * jax.random.normal(jax.random.fold_in(_rk, 611), (1, 4096, 1024), jnp.float32))
        return (x, ctx_4096)
    x, ctx_4096 = _rec_inputs()

    def _L0_xattn_setup():
        import jax, jax.numpy as jnp
        import numpy as np
        HEADS = 32
        KV_HEADS = 8
        HEAD_DIM = 128
        EPS = 1e-06

        def rms_norm(x, w):
            var = jnp.mean(jnp.square(x.astype(jnp.float32)), axis=-1, keepdims=True)
            return (x.astype(jnp.float32) * jax.lax.rsqrt(var + EPS)).astype(x.dtype) * w
        key = jax.random.key(seed)
        ks = jax.random.split(key, 6)
        bsz, n_lat, seq, hidden = (8, 64, 1024, 1024)
        return {'latents': jax.random.normal(ks[0], (bsz, n_lat, hidden), jnp.float32), 'context': jax.random.normal(ks[1], (bsz, seq, hidden), jnp.float32), 'Wq': jax.random.normal(ks[2], (hidden, HEADS * HEAD_DIM), jnp.float32) * 0.02, 'Wk': jax.random.normal(ks[3], (hidden, KV_HEADS * HEAD_DIM), jnp.float32) * 0.02, 'Wv': jax.random.normal(ks[4], (hidden, KV_HEADS * HEAD_DIM), jnp.float32) * 0.02, 'Wo': jax.random.normal(ks[5], (HEADS * HEAD_DIM, hidden), jnp.float32) * 0.02, 'q_norm_w': jnp.ones((HEAD_DIM,), jnp.float32), 'k_norm_w': jnp.ones((HEAD_DIM,), jnp.float32)}
    _L0_xattn_all = _L0_xattn_setup()
    _L0_xattn_in = {k: v for k, v in _L0_xattn_all.items() if k in ('Wq', 'Wk', 'Wv', 'Wo', 'q_norm_w', 'k_norm_w')}
    del _L0_xattn_all

    def _L0_attn_setup():
        import jax, jax.numpy as jnp
        import numpy as np
        D = 1024
        NH = 64
        HD = 128
        RD = 64
        QLR = 256
        OLR = 256
        OG = 8
        EPS = 1e-06
        B, S = (1, 256)
        THETA = 10000.0

        def _rope(x, cos, sin, inverse=False):
            xf = x.astype(jnp.float32)
            x1, x2 = (xf[..., 0::2], xf[..., 1::2])
            sn = -sin if inverse else sin
            o1 = x1 * cos - x2 * sn
            o2 = x1 * sn + x2 * cos
            return jnp.stack([o1, o2], axis=-1).reshape(x.shape).astype(x.dtype)
        key = jax.random.key(seed)
        ks = jax.random.split(key, 8)
        bf = jnp.bfloat16

        def w(k, shape, fan_in):
            return (jax.random.normal(k, shape, jnp.float32) / np.sqrt(fan_in)).astype(bf)
        inv = 1.0 / THETA ** (np.arange(0, RD, 2, dtype=np.float32) / RD)
        ang = np.outer(np.arange(S, dtype=np.float32), inv)
        return {'x': jax.random.normal(ks[0], (B, S, D), jnp.float32).astype(bf), 'wq_a': w(ks[1], (QLR, D), D), 'q_norm_w': jnp.ones((QLR,), bf), 'wq_b': w(ks[2], (NH * HD, QLR), QLR), 'wkv': w(ks[3], (HD, D), D), 'kv_norm_w': jnp.ones((HD,), bf), 'wo_a': w(ks[4], (OG * OLR, NH * HD // OG), NH * HD // OG), 'wo_b': w(ks[5], (D, OG * OLR), OG * OLR), 'attn_sink': jax.random.normal(ks[6], (NH,), jnp.float32) * 0.1, 'cos': jnp.asarray(np.cos(ang)), 'sin': jnp.asarray(np.sin(ang))}
    _L0_attn_all = _L0_attn_setup()
    _L0_attn_in = {k: v for k, v in _L0_attn_all.items() if k in ('wq_a', 'q_norm_w', 'wq_b', 'wkv', 'kv_norm_w', 'wo_a', 'wo_b', 'attn_sink', 'cos', 'sin')}
    del _L0_attn_all

    def _L0_ffn_setup():
        import jax, jax.numpy as jnp
        import numpy as np
        IN_F = 1024
        OUT_F = 1024
        N_CLUSTERS = 64
        THRESHOLD = 0.01
        TEMPERATURE = 0.1
        BATCH, SEQ = (4, 512)
        key = jax.random.key(seed)
        k1, k2, k3, k4, k5 = jax.random.split(key, 5)
        s = 1.0 / np.sqrt(IN_F)
        return {'input': jax.random.normal(k1, (BATCH, SEQ, IN_F), dtype=jnp.float32), 'weight': jax.random.normal(k2, (OUT_F, IN_F), dtype=jnp.float32) * s, 'bias': jax.random.uniform(k3, (OUT_F,), dtype=jnp.float32, minval=-s, maxval=s), 'centroids': jax.random.normal(k4, (N_CLUSTERS, IN_F), dtype=jnp.float32) * s, 'assignments': jax.random.randint(k5, (OUT_F,), 0, N_CLUSTERS, dtype=jnp.int32)}
    _L0_ffn_all = _L0_ffn_setup()
    _L0_ffn_in = {k: v for k, v in _L0_ffn_all.items() if k in ('weight', 'bias', 'centroids', 'assignments')}
    del _L0_ffn_all
    return {'x': x, 'ctx_4096': ctx_4096, 'L0_xattn_Wq': _L0_xattn_in['Wq'], 'L0_xattn_Wk': _L0_xattn_in['Wk'], 'L0_xattn_Wv': _L0_xattn_in['Wv'], 'L0_xattn_Wo': _L0_xattn_in['Wo'], 'L0_xattn_q_norm_w': _L0_xattn_in['q_norm_w'], 'L0_xattn_k_norm_w': _L0_xattn_in['k_norm_w'], 'L0_attn_wq_a': _L0_attn_in['wq_a'], 'L0_attn_q_norm_w': _L0_attn_in['q_norm_w'], 'L0_attn_wq_b': _L0_attn_in['wq_b'], 'L0_attn_wkv': _L0_attn_in['wkv'], 'L0_attn_kv_norm_w': _L0_attn_in['kv_norm_w'], 'L0_attn_wo_a': _L0_attn_in['wo_a'], 'L0_attn_wo_b': _L0_attn_in['wo_b'], 'L0_attn_attn_sink': _L0_attn_in['attn_sink'], 'L0_attn_cos': _L0_attn_in['cos'], 'L0_attn_sin': _L0_attn_in['sin'], 'L0_ffn_weight': _L0_ffn_in['weight'], 'L0_ffn_bias': _L0_ffn_in['bias'], 'L0_ffn_centroids': _L0_ffn_in['centroids'], 'L0_ffn_assignments': _L0_ffn_in['assignments']}

def reference(x, ctx_4096, L0_xattn_Wq, L0_xattn_Wk, L0_xattn_Wv, L0_xattn_Wo, L0_xattn_q_norm_w, L0_xattn_k_norm_w, L0_attn_wq_a, L0_attn_q_norm_w, L0_attn_wq_b, L0_attn_wkv, L0_attn_kv_norm_w, L0_attn_wo_a, L0_attn_wo_b, L0_attn_attn_sink, L0_attn_cos, L0_attn_sin, L0_ffn_weight, L0_ffn_bias, L0_ffn_centroids, L0_ffn_assignments):
    import jax
    import jax.numpy as jnp

    def _L0_xattn_ref(latents, context, Wq, Wk, Wv, Wo, q_norm_w, k_norm_w):
        import jax, jax.numpy as jnp
        import numpy as np
        HEADS = 32
        KV_HEADS = 8
        HEAD_DIM = 128
        EPS = 1e-06

        def rms_norm(x, w):
            var = jnp.mean(jnp.square(x.astype(jnp.float32)), axis=-1, keepdims=True)
            return (x.astype(jnp.float32) * jax.lax.rsqrt(var + EPS)).astype(x.dtype) * w
        bsz, q_len, hidden = latents.shape
        kv = jnp.concatenate([context, latents], axis=1)
        kv_len = kv.shape[1]
        groups = HEADS // KV_HEADS
        q = (latents @ Wq).reshape(bsz, q_len, HEADS, HEAD_DIM).transpose(0, 2, 1, 3)
        k = (kv @ Wk).reshape(bsz, kv_len, KV_HEADS, HEAD_DIM).transpose(0, 2, 1, 3)
        v = (kv @ Wv).reshape(bsz, kv_len, KV_HEADS, HEAD_DIM).transpose(0, 2, 1, 3)
        q = rms_norm(q, q_norm_w)
        k = rms_norm(k, k_norm_w)
        qg = q.reshape(bsz, KV_HEADS, groups, q_len, HEAD_DIM)
        scale = 1.0 / np.sqrt(HEAD_DIM)
        scores = jnp.einsum('bhgqd,bhkd->bhgqk', qg, k) * scale
        probs = jax.nn.softmax(scores.astype(jnp.float32), axis=-1).astype(q.dtype)
        out = jnp.einsum('bhgqk,bhkd->bhgqd', probs, v)
        out = out.reshape(bsz, HEADS, q_len, HEAD_DIM).transpose(0, 2, 1, 3)
        out = out.reshape(bsz, q_len, HEADS * HEAD_DIM)
        return out @ Wo

    def _L0_attn_ref(x, wq_a, q_norm_w, wq_b, wkv, kv_norm_w, wo_a, wo_b, attn_sink, cos, sin):
        import jax, jax.numpy as jnp
        import numpy as np
        D = 1024
        NH = 64
        HD = 128
        RD = 64
        QLR = 256
        OLR = 256
        OG = 8
        EPS = 1e-06
        B, S = (1, 256)
        THETA = 10000.0

        def _rope(x, cos, sin, inverse=False):
            xf = x.astype(jnp.float32)
            x1, x2 = (xf[..., 0::2], xf[..., 1::2])
            sn = -sin if inverse else sin
            o1 = x1 * cos - x2 * sn
            o2 = x1 * sn + x2 * cos
            return jnp.stack([o1, o2], axis=-1).reshape(x.shape).astype(x.dtype)
        b, s, _ = x.shape

        def rms(v, wgt):
            vf = v.astype(jnp.float32)
            n = vf * jax.lax.rsqrt(jnp.mean(vf * vf, -1, keepdims=True) + EPS)
            return n.astype(v.dtype) * wgt
        qr = rms(x @ wq_a.T, q_norm_w)
        q = (qr @ wq_b.T).reshape(b, s, NH, HD).transpose(0, 2, 1, 3)
        qf = q.astype(jnp.float32)
        q = (qf * jax.lax.rsqrt(jnp.mean(qf * qf, -1, keepdims=True) + EPS)).astype(q.dtype)
        q = q.at[..., HD - RD:].set(_rope(q[..., HD - RD:], cos, sin))
        kv = rms(x @ wkv.T, kv_norm_w)
        kv = kv.at[..., HD - RD:].set(_rope(kv[..., HD - RD:], cos, sin))
        scale = HD ** (-0.5)
        scores = jnp.einsum('bhqd,bkd->bhqk', q, kv) * scale
        causal = jnp.tril(jnp.ones((s, s), bool))
        scores = jnp.where(causal, scores, jnp.asarray(-jnp.inf, scores.dtype))
        sink = jnp.broadcast_to(attn_sink.astype(scores.dtype)[None, :, None, None], (b, NH, s, 1))
        attn = jax.nn.softmax(jnp.concatenate([sink, scores], axis=-1), axis=-1)[..., 1:]
        attn = attn.astype(kv.dtype)
        o = jnp.einsum('bhqk,bkd->bhqd', attn, kv)
        o = o.at[..., HD - RD:].set(_rope(o[..., HD - RD:], cos, sin, inverse=True))
        o = o.transpose(0, 2, 1, 3).reshape(b, s, OG, NH * HD // OG)
        og = jnp.einsum('bsgd,grd->bsgr', o, wo_a.reshape(OG, OLR, NH * HD // OG))
        return og.reshape(b, s, OG * OLR) @ wo_b.T

    def _L0_ffn_ref(input, weight, bias, centroids, assignments):
        import jax, jax.numpy as jnp
        import numpy as np
        IN_F = 1024
        OUT_F = 1024
        N_CLUSTERS = 64
        THRESHOLD = 0.01
        TEMPERATURE = 0.1
        BATCH, SEQ = (4, 512)
        shape = input.shape
        x = input.reshape(-1, shape[-1])
        dots = jax.nn.softmax(x @ centroids.T / TEMPERATURE, axis=-1)
        hits = dots > THRESHOLD
        query_sel = jnp.any(hits, axis=1)
        cluster_sel = jnp.any(hits, axis=0)
        row_sel = cluster_sel[assignments]
        dense = x @ weight.T + bias
        out = jnp.where(query_sel[:, None] & row_sel[None, :], dense, jnp.zeros((), dense.dtype))
        return out.reshape(*shape[:-1], -1)
    x = x + _L0_xattn_ref(_layernorm(x, axis=-1), ctx_4096, L0_xattn_Wq, L0_xattn_Wk, L0_xattn_Wv, L0_xattn_Wo, L0_xattn_q_norm_w, L0_xattn_k_norm_w)
    x = x + _L0_attn_ref(_layernorm(x, axis=-1), L0_attn_wq_a, L0_attn_q_norm_w, L0_attn_wq_b, L0_attn_wkv, L0_attn_kv_norm_w, L0_attn_wo_a, L0_attn_wo_b, L0_attn_attn_sink, L0_attn_cos, L0_attn_sin)
    x = x + _L0_ffn_ref(_layernorm(x, axis=-1), L0_ffn_weight, L0_ffn_bias, L0_ffn_centroids, L0_ffn_assignments)
    return x

_drawn_inputs = setup_inputs


def setup_inputs(seed=0):
    import zlib

    import numpy as np

    out = dict(_drawn_inputs(seed))
    spreads = {'L0_xattn_q_norm_w': (1.0, 0.6), 'L0_xattn_k_norm_w': (1.0, 0.6)}
    factors = {'L0_attn_attn_sink': 32.36, 'L0_ffn_bias': 5.471}
    for name, (base, spread) in spreads.items():
        noise = np.random.default_rng([zlib.crc32(name.encode()), seed]).standard_normal(out[name].shape)
        drawn = base * np.exp(spread * noise) if base else spread * noise
        out[name] = jnp.asarray(drawn.astype(out[name].dtype))
    for name, factor in factors.items():
        out[name] = (out[name] * factor).astype(out[name].dtype)
    return out
```

```python
from contextlib import ExitStack

import concourse.bass as bass
from concourse import mybir

F32 = mybir.dt.float32
F32R = mybir.dt.float32r
BF16 = mybir.dt.bfloat16
I32 = mybir.dt.int32
ALU = mybir.AluOpType
ACT = mybir.ActivationFunctionType
AX = mybir.AxisListType

P = 128
BANK = 512

D = 1024
KT = D // P
NQ = 256
QT = NQ // P
NCTX = 4096
NK = NCTX + NQ
HD = 128

XH = 32
XKV = 8
XG = XH // XKV
XQ = XG * NQ
XQT = XQ // P
RT = NK // P
CT = NCTX // P
HALF = RT // 2

LN_EPS = 1e-5
RMS_EPS = 1e-6
SCALE = float(HD) ** -0.5


START = 1


class Scope:

    def __init__(self, nc, stack, tag):
        self.nc, self.stack, self.tag = nc, stack, tag

    def sb(self, name, shape, dt=F32):
        return self.stack.enter_context(self.nc.sbuf_tensor(f"{self.tag}_{name}", shape, dt))

    def ps(self, name, shape, dt=F32):
        return self.stack.enter_context(self.nc.psum_tensor(f"{self.tag}_{name}", shape, dt))


class Semaphores:

    def __init__(self, nc):
        self.nc, self.handles = nc, []

    def new(self, name):
        self.handles.append(self.nc.alloc_semaphore(name=name))
        return self.handles[-1]

    def credit(self, *handles):
        for handle in handles:
            self.nc.gpsimd.sem_inc(handle, START)

    def release(self):
        self.nc.clear_and_free_semaphores(self.handles)
        self.handles = []
        self.nc.all_engine_barrier()


def make_sem(nc, sems, tag):
    return lambda name: sems.new(f"{tag}_{name}")


def pipeline(eng, pairs, stages):
    groups, far = 2 * pairs, max(lead for lead, _ in stages)
    full = (groups - far) // 2

    def written_out(steps):
        for g in steps:
            for lead, stage in stages:
                if 0 <= g + lead < groups:
                    stage((g + lead) // 2, (g + lead) % 2)

    written_out(range(-far, 0))
    with eng.Fori(0, full) as pair:
        for s in range(2):
            for lead, stage in stages:
                stage(pair + (s + lead) // 2, (s + lead) % 2)
    written_out(range(2 * full, groups))


def broadcast_inner(ap, n):
    return ap.unsqueeze(2).to_broadcast([ap.shape[0], ap.shape[1], n])


def broadcast_outer(ap, n):
    return ap.unsqueeze(1).to_broadcast([ap.shape[0], n, ap.shape[1]])


def constants(nc, sems, ident, ident_bf, ones):
    sem = make_sem(nc, sems, "const")
    cleared, made = sem("cleared"), sem("made")
    with nc.Block() as block:
        @block.gpsimd
        def _(pool):
            pool.memset(ones[:], 1.0)
            pool.memset(ident[:], 0.0).then_inc(cleared, 1)
            pool.wait_ge(cleared, 1)
            pool.affine_select(out=ident[:], in_=ident[:], compare_op=ALU.not_equal, fill=1.0, base=0,
                               pattern=[[-1, P]], channel_multiplier=1).then_inc(made, 1)

        @block.vector
        def _(dve):
            dve.wait_ge(made, 1)
            dve.tensor_copy(ident_bf[:], ident[:])


def layernorm_transposed(nc, sems, tag, rows, ident, yT_high, yT_low):
    with ExitStack() as stack:
        m = Scope(nc, stack, tag)
        sem = make_sem(nc, sems, tag)
        x = m.sb("x", [P, QT, D])
        y = m.sb("y", [P, QT, D])
        stats = m.sb("stats", [P, QT, 2, 6])
        mean_var = m.sb("mean_var", [P, QT, 2])
        var_eps = m.sb("var_eps", [P, QT])
        rstd = m.sb("rstd", [P, QT])
        power = m.sb("power", [P, QT])
        psT = m.ps("psT", [P, KT, NQ])
        loaded, half_stats, aggregated, eps_added, rstd_ready, normed, transposed, high, power_set = map(sem, (
            "loaded", "half_stats", "aggregated", "eps_added", "rstd_ready", "normed", "transposed", "high", "power_set"))
        with nc.Block() as block:
            @block.sync
            def _(sp):
                sp.dma_start(x[:], rows.rearrange("(t p) d -> p t d", p=P)).then_inc(loaded, 16)

            @block.vector
            def _(dve):
                dve.wait_ge(loaded, 16)
                for t in range(QT):
                    for c in range(2):
                        last = dve.bn_stats(stats[:, t, c, :], x[:, t, c * 512:(c + 1) * 512])
                last.then_inc(half_stats, 1)
                dve.wait_ge(half_stats, 1)
                for t in range(QT):
                    last = dve.bn_aggr(mean_var[:, t, :], stats[:, t, :, :].rearrange("p a b -> p (a b)"))
                last.then_inc(aggregated, 1)
                dve.wait_ge(rstd_ready, 1)
                for t in range(QT):
                    last = dve.tensor_scalar(y[:, t, :], x[:, t, :], mean_var[:, t, 0:1], rstd[:, t:t + 1],
                                             ALU.subtract, ALU.mult)
                last.then_inc(normed, 1)
                dve.wait_ge(high, 1)
                dve.tensor_tensor(yT_low[:], psT[:], yT_high[:].bitcast(F32), ALU.subtract)

            @block.gpsimd
            def _(pool):
                pool.memset(power[:], -0.5).then_inc(power_set, 1)
                pool.wait_ge(aggregated, 1)
                pool.tensor_scalar(var_eps[:], mean_var[:, :, 1], 1.0, LN_EPS, ALU.mult, ALU.add).then_inc(eps_added, 1)
                pool.wait_ge(power_set, 1)
                pool.wait_ge(eps_added, 1)
                pool.tensor_tensor(rstd[:], var_eps[:], power[:], ALU.pow).then_inc(rstd_ready, 1)

            @block.tensor
            def _(pe):
                pe.wait_ge(normed, 1)
                for t in range(QT):
                    for k in range(KT):
                        last = pe.transpose(psT[:, k, t * P:(t + 1) * P], y[:, t, k * P:(k + 1) * P], ident[:])
                last.then_inc(transposed, 1)

            @block.scalar
            def _(act):
                act.wait_ge(transposed, 1)
                act.copy(yT_high[:], psT[:]).then_inc(high, 1)


def project_keys_values(nc, sems, context, Wk, Wv, ident, yT_high, yT_low, keyT_high, keyT_low, val_high, val_low):
    with ExitStack() as stack:
        m = Scope(nc, stack, "kv")
        sem = make_sem(nc, sems, "kv")
        row = [m.sb(f"row{s}", [P, D]) for s in range(2)]
        xT_high = [m.sb(f"xT_high{s}", [P, KT, P], F32R) for s in range(2)]
        xT_low = [m.sb(f"xT_low{s}", [P, KT, P], F32R) for s in range(2)]
        W_high = m.sb("W_high", [P, KT, 2 * D], F32R)
        W_low = m.sb("W_low", [P, KT, 2 * D], F32R)
        key = m.sb("key", [P, D])
        v_hi = [m.sb(f"v_hi{s}", [P, D], F32R) for s in range(2)]
        v_lo = [m.sb(f"v_lo{s}", [P, D], F32R) for s in range(2)]
        kT_hi = [m.sb(f"kT_hi{s}", [P, XKV, P], F32R) for s in range(2)]
        kT_lo = [m.sb(f"kT_lo{s}", [P, XKV, P], F32R) for s in range(2)]
        squares = m.sb("squares", [P, XKV])
        var = m.sb("var", [P, XKV])
        rstd = m.sb("rstd", [P, XKV])
        power = m.sb("power", [P, XKV])
        psX = m.ps("psX", [P, KT, P])
        psK = m.ps("psK", [P, D])
        psV = m.ps("psV", [P, D])
        psT = m.ps("psT", [P, XKV, P])

        row_loaded = [sem(f"row_loaded{s}") for s in range(2)]
        (w_high, w_low, x_transposed, x_high, x_low, k_projected, k_squared, k_var, k_rstd, k_scaled, v_projected,
         v_high, v_lowed, k_transposed, k_high, k_lowed, power_set) = map(sem, (
            "w_high", "w_low", "x_transposed", "x_high", "x_low", "k_projected", "k_squared", "k_var", "k_rstd",
            "k_scaled", "v_projected", "v_high", "v_lowed", "k_transposed", "k_high", "k_lowed", "power_set"))
        v_stored = [sem(f"v_stored{s}") for s in range(2)]
        k_stored = [sem(f"k_stored{s}") for s in range(2)]

        WCH = 2 * KT
        WLOADS = 16 * WCH // 2
        PAIRS = CT // 2

        def tiles(eng, step):
            with eng.Fori(0, PAIRS - 1) as pair:
                step(pair * 2, pair, 0, True)
                step(pair * 2 + 1, pair, 1, True)
            for r in range(CT - 2, RT):
                step(r, r // 2, r % 2, r + 1 < CT)

        sems.credit(k_lowed, k_var, *v_stored, *k_stored, k_transposed, k_scaled, v_lowed, x_low)
        with nc.Block() as block:
            @block.sync
            def _(sp):
                for c in range(WCH):
                    W, k = (Wk, Wv)[c % 2], c // 2
                    if c >= 2:
                        sp.wait_ge(w_low, c - 1)
                    sp.dma_start(row[c % 2][:], W[k * P:(k + 1) * P, :]).then_inc(row_loaded[c % 2], 16)
                for r in range(2):
                    sp.wait_ge(w_low, WCH - 1 + r)
                    sp.dma_start(row[r][:], context[r * P:(r + 1) * P, :]).then_inc(row_loaded[r], 16)

                def step(r, pair, s, load):
                    if load:
                        sp.wait_ge(x_transposed, r + 1)
                        sp.dma_start(row[s][:], context[bass.ds((r + 2) * P, P), :]).then_inc(row_loaded[s], 16)
                    sp.wait_ge(v_lowed, START + r + 1)
                    for src, dst in ((v_hi, val_high), (v_lo, val_low)):
                        sp.dma_start(dst[:, :, bass.ds(r, 1), :].rearrange("e p t d -> p (e t) d"),
                                     src[s][:].bitcast(F32).rearrange("p (e d) -> p e d", e=XKV)).then_inc(v_stored[s], 16)
                    sp.wait_ge(k_lowed, START + r + 1)
                    for src, dst in ((kT_hi, keyT_high), (kT_lo, keyT_low)):
                        sp.dma_start(dst[:, :, bass.ds(r * P, P)].rearrange("e d k -> d e k"),
                                     src[s][:].bitcast(F32)).then_inc(k_stored[s], 16)

                with sp.Fori(0, PAIRS - 1) as pair:
                    step(pair * 2, pair, 0, True)
                    step(pair * 2 + 1, pair, 1, True)
                for r in range(CT - 2, RT):
                    step(r, r // 2, r % 2, False)
                for s in range(2):
                    sp.wait_ge(v_stored[s], START + 32 * (RT // 2))
                    sp.wait_ge(k_stored[s], START + 32 * (RT // 2))

            @block.scalar
            def _(act):
                for c in range(WCH):
                    act.wait_ge(row_loaded[c % 2], 16 * (c // 2 + 1))
                    act.copy(W_high[:, c // 2, (c % 2) * D:(c % 2 + 1) * D], row[c % 2][:]).then_inc(w_high, 1)

                def rows_high(r, s):
                    act.wait_ge(x_transposed, r + 1)
                    act.copy(xT_high[s][:], psX[:]).then_inc(x_high, 1)

                def step(r, pair, s, has_next):
                    act.wait_ge(k_projected, r + 1)
                    act.wait_ge(k_lowed, START + r)
                    act.wait_ge(k_var, START + r)
                    for e in range(XKV):
                        last = act.activation(psT[:, e, :], psK[:, e * HD:(e + 1) * HD], ACT.Square,
                                              accum_out=squares[:, e:e + 1])
                    last.then_inc(k_squared, 1)
                    if has_next:
                        rows_high(r + 1, 1 - s)
                    act.wait_ge(v_projected, r + 1)
                    act.wait_ge(v_stored[s], START + 32 * pair)
                    act.copy(v_hi[s][:], psV[:]).then_inc(v_high, 1)
                    act.wait_ge(k_transposed, START + r + 1)
                    act.wait_ge(k_stored[s], START + 32 * pair)
                    act.copy(kT_hi[s][:], psT[:]).then_inc(k_high, 1)

                rows_high(0, 0)
                tiles(act, step)

            @block.vector
            def _(dve):
                for c in range(WCH):
                    dve.wait_ge(w_high, c + 1)
                    part = slice((c % 2) * D, (c % 2 + 1) * D)
                    dve.tensor_tensor(W_low[:, c // 2, part], row[c % 2][:], W_high[:, c // 2, part].bitcast(F32),
                                      ALU.subtract).then_inc(w_low, 1)

                def rows_low(r, s):
                    dve.wait_ge(x_high, r + 1)
                    dve.tensor_tensor(xT_low[s][:], psX[:], xT_high[s][:].bitcast(F32), ALU.subtract).then_inc(x_low, 1)

                def step(r, pair, s, has_next):
                    dve.wait_ge(k_squared, r + 1)
                    dve.tensor_scalar(var[:], squares[:], 1.0 / HD, RMS_EPS, ALU.mult, ALU.add).then_inc(k_var, 1)
                    dve.wait_ge(k_rstd, r + 1)
                    dve.wait_ge(k_transposed, START + r)
                    dve.tensor_tensor(key[:].rearrange("p (e d) -> p e d", e=XKV),
                                      psK[:].rearrange("p (e d) -> p e d", e=XKV),
                                      broadcast_inner(rstd[:], HD), ALU.mult).then_inc(k_scaled, 1)
                    if has_next:
                        rows_low(r + 1, 1 - s)
                    dve.wait_ge(v_high, r + 1)
                    dve.tensor_tensor(v_lo[s][:], psV[:], v_hi[s][:].bitcast(F32), ALU.subtract).then_inc(v_lowed, 1)
                    dve.wait_ge(k_high, r + 1)
                    dve.tensor_tensor(kT_lo[s][:], psT[:], kT_hi[s][:].bitcast(F32), ALU.subtract).then_inc(k_lowed, 1)

                rows_low(0, 0)
                tiles(dve, step)

            @block.gpsimd
            def _(pool):
                pool.memset(power[:], -0.5).then_inc(power_set, 1)
                pool.wait_ge(power_set, 1)

                def step(r, pair, s, has_next):
                    pool.wait_ge(k_var, START + r + 1)
                    pool.tensor_tensor(rstd[:], var[:], power[:], ALU.pow).then_inc(k_rstd, 1)

                tiles(pool, step)

            @block.tensor
            def _(pe):
                def transpose_rows(r, pair, s):
                    pe.wait_ge(row_loaded[s], pair * 16 + (WLOADS + 16))
                    pe.wait_ge(x_low, START + r)
                    for k in range(KT):
                        last = pe.transpose(psX[:, k, :], row[s][:, k * P:(k + 1) * P], ident[:])
                    last.then_inc(x_transposed, 1)

                def project(ps, x_hi, x_lo, first):
                    for k in range(KT):
                        for n, (x, W) in enumerate(((x_hi, W_high), (x_hi, W_low), (x_lo, W_high))):
                            for c in range(D // BANK):
                                last = pe.matmul(ps[:, c * BANK:(c + 1) * BANK], x(k),
                                                 W[:, k, first + c * BANK:first + (c + 1) * BANK],
                                                 start=(k == 0 and n == 0), stop=(k == KT - 1 and n == 2))
                    return last

                def step(r, pair, s, has_next):
                    if isinstance(r, int) and r >= CT:
                        t = slice((r - CT) * P, (r - CT + 1) * P)
                        x_hi, x_lo = (lambda k: yT_high[:, k, t]), (lambda k: yT_low[:, k, t])
                    else:
                        x_hi, x_lo = (lambda k: xT_high[s][:, k, :]), (lambda k: xT_low[s][:, k, :])
                        pe.wait_ge(x_low, START + r + 1)
                    pe.wait_ge(k_scaled, START + r)
                    project(psK, x_hi, x_lo, 0).then_inc(k_projected, 1)
                    if has_next:
                        transpose_rows(r + 1, pair + s, 1 - s)
                    pe.wait_ge(v_lowed, START + r)
                    project(psV, x_hi, x_lo, D).then_inc(v_projected, 1)
                    pe.wait_ge(k_scaled, START + r + 1)
                    for e in range(XKV):
                        last = pe.transpose(psT[:, e, :], key[:, e * HD:(e + 1) * HD], ident[:])
                    last.then_inc(k_transposed, 1)

                pe.wait_ge(w_low, WCH)
                transpose_rows(0, 0, 0)
                tiles(pe, step)


def project_queries(nc, sems, Wq, q_norm_w, k_norm_w, ident, yT_high, yT_low, qT_high, qT_low):
    with ExitStack() as stack:
        m = Scope(nc, stack, "q")
        sem = make_sem(nc, sems, "q")
        GC = XG * HD
        w_raw = [m.sb(f"w_raw{s}", [P, KT, GC]) for s in range(2)]
        w_hi = [m.sb(f"w_hi{s}", [P, KT, GC], F32R) for s in range(2)]
        w_lo = [m.sb(f"w_lo{s}", [P, KT, GC], F32R) for s in range(2)]
        q = [m.sb(f"q{s}", [P, QT * XG, HD]) for s in range(2)]
        q_hi = [m.sb(f"q_hi{s}", [P, XQ], F32R) for s in range(2)]
        q_lo = [m.sb(f"q_lo{s}", [P, XQ], F32R) for s in range(2)]
        squares = [m.sb(f"squares{s}", [P, QT * XG]) for s in range(2)]
        var = [m.sb(f"var{s}", [P, QT * XG]) for s in range(2)]
        rstd = [m.sb(f"rstd{s}", [P, QT * XG]) for s in range(2)]
        power = m.sb("power", [P, QT * XG])
        norm_w = m.sb("norm_w", [P, 2])
        weight = m.sb("weight", [P, 1])
        psQ = [m.ps(f"psQ{s}", [P, QT * XG, HD]) for s in range(2)]
        psT = [m.ps(f"psT{s}", [P, XG, QT, P]) for s in range(2)]
        (norm_loaded, weight_ready, power_set) = map(sem, ("norm_loaded", "weight_ready", "power_set"))
        two = lambda name: [sem(f"{name}{s}") for s in range(2)]
        w_loaded, w_high, w_low, projected, squared, var_ready, rstd_ready, scaled, transposed, high, low, stored = map(
            two, ("w_loaded", "w_high", "w_low", "projected", "squared", "var_ready", "rstd_ready", "scaled",
                  "transposed", "high", "low", "stored"))
        PAIRS = XKV // 2
        Wq_v = Wq.rearrange("(k p) n -> p k n", p=P)

        sems.credit(*w_low, *projected, *var_ready, *low, *stored, *scaled)
        with nc.Block() as block:
            @block.sync
            def _(sp):
                def load(pair, s):
                    sp.wait_ge(w_low[s], START + pair)
                    sp.dma_start(w_raw[s][:], Wq_v[:, :, bass.ds((pair * 2 + s) * GC, GC)]).then_inc(w_loaded[s], 16)

                def store(pair, s):
                    sp.wait_ge(low[s], START + pair + 1)
                    for src, dst in ((q_hi, qT_high), (q_lo, qT_low)):
                        sp.dma_start(dst[bass.ds(pair * 2 + s, 1), :, :].rearrange("e d q -> d (e q)"),
                                     src[s][:].bitcast(F32)).then_inc(stored[s], 16)

                sp.dma_start(norm_w[:, 0:1], q_norm_w.rearrange("(d a) -> d a", a=1)).then_inc(norm_loaded, 16)
                sp.dma_start(norm_w[:, 1:2], k_norm_w.rearrange("(d a) -> d a", a=1)).then_inc(norm_loaded, 16)
                pipeline(sp, PAIRS, [(3, load), (0, store)])
                for s in range(2):
                    sp.wait_ge(stored[s], START + 32 * PAIRS)

            @block.scalar
            def _(act):
                def split_weights(pair, s):
                    act.wait_ge(w_loaded[s], pair * 16 + 16)
                    act.wait_ge(projected[s], START + pair)
                    act.copy(w_hi[s][:], w_raw[s][:]).then_inc(w_high[s], 1)

                def square(pair, s):
                    act.wait_ge(projected[s], START + pair + 1)
                    act.wait_ge(var_ready[s], START + pair)
                    act.wait_ge(low[s], START + pair)
                    for g in range(QT * XG):
                        last = act.activation(psT[s][:, g % XG, g // XG, :], psQ[s][:, g, :], ACT.Square,
                                              accum_out=squares[s][:, g:g + 1])
                    last.then_inc(squared[s], 1)

                def split(pair, s):
                    act.wait_ge(transposed[s], pair + 1)
                    act.wait_ge(stored[s], START + pair * 32)
                    act.activation(q_hi[s][:], psT[s][:].rearrange("p g t q -> p (g t q)"), ACT.Copy,
                                   scale=weight[:, 0:1]).then_inc(high[s], 1)

                act.wait_ge(weight_ready, 1)
                pipeline(act, PAIRS, [(0, square), (2, split_weights), (0, split)])

            @block.vector
            def _(dve):
                def split_weights(pair, s):
                    dve.wait_ge(w_high[s], pair + 1)
                    dve.tensor_tensor(w_lo[s][:], w_raw[s][:], w_hi[s][:].bitcast(F32), ALU.subtract).then_inc(w_low[s], 1)

                def normalise(pair, s):
                    dve.wait_ge(squared[s], pair + 1)
                    dve.tensor_scalar(var[s][:], squares[s][:], 1.0 / HD, RMS_EPS, ALU.mult, ALU.add).then_inc(var_ready[s], 1)
                    dve.wait_ge(rstd_ready[s], pair + 1)
                    dve.tensor_tensor(q[s][:], psQ[s][:], broadcast_inner(rstd[s][:], HD), ALU.mult).then_inc(scaled[s], 1)

                def split(pair, s):
                    dve.wait_ge(high[s], pair + 1)
                    dve.scalar_tensor_tensor(q_lo[s][:], psT[s][:].rearrange("p g t q -> p (g t q)"), weight[:, 0:1],
                                             q_hi[s][:].bitcast(F32), ALU.mult, ALU.subtract).then_inc(low[s], 1)

                dve.wait_ge(norm_loaded, 32)
                dve.scalar_tensor_tensor(weight[:], norm_w[:, 0:1], SCALE, norm_w[:, 1:2], ALU.mult, ALU.mult).then_inc(weight_ready, 1)
                dve.wait_ge(weight_ready, 1)
                pipeline(dve, PAIRS, [(0, normalise), (2, split_weights), (0, split)])

            @block.gpsimd
            def _(pool):
                def root(pair, s):
                    pool.wait_ge(var_ready[s], START + pair + 1)
                    pool.tensor_tensor(rstd[s][:], var[s][:], power[:], ALU.pow).then_inc(rstd_ready[s], 1)

                pool.memset(power[:], -0.5).then_inc(power_set, 1)
                pool.wait_ge(power_set, 1)
                pipeline(pool, PAIRS, [(0, root)])

            @block.tensor
            def _(pe):
                def project(pair, s):
                    pe.wait_ge(w_low[s], START + pair + 1)
                    pe.wait_ge(scaled[s], START + pair)
                    for t in range(QT):
                        rows = slice(t * P, (t + 1) * P)
                        for k in range(KT):
                            for n, (y, w) in enumerate(((yT_high, w_hi), (yT_high, w_lo), (yT_low, w_hi))):
                                last = pe.matmul(psQ[s][:, t * XG:(t + 1) * XG, :].rearrange("p g d -> p (g d)"),
                                                 y[:, k, rows], w[s][:, k, :],
                                                 start=(k == 0 and n == 0), stop=(k == KT - 1 and n == 2))
                    last.then_inc(projected[s], 1)

                def transpose(pair, s):
                    pe.wait_ge(scaled[s], START + pair + 1)
                    for t in range(QT):
                        for g in range(XG):
                            last = pe.transpose(psT[s][:, g, t, :], q[s][:, t * XG + g, :], ident[:])
                    last.then_inc(transposed[s], 1)

                pipeline(pe, PAIRS, [(1, project), (0, transpose)])
def cross_attention(nc, sems, ident, ones, keyT_high, keyT_low, val_high, val_low, qT_high, qT_low, outT_high, outT_low):
    with ExitStack() as stack:
        m = Scope(nc, stack, "xa")
        sem = make_sem(nc, sems, "xa")
        two = lambda name: [sem(f"{name}{s}") for s in range(2)]
        PIECE = BANK * 2 // P
        PIECES = [(c * PIECE, (c + 1) * PIECE) for c in range(3)] + [(3 * PIECE, RT)]
        WIDE = RT // PIECE
        REST = RT * P - WIDE * PIECE * P
        PER = BANK * 2 // REST
        UNITS = WIDE * XQT + XQT // PER
        assert UNITS == RT

        kT_hi = [m.sb(f"kT_hi{s}", [P, NK], F32R) for s in range(2)]
        kT_lo = [m.sb(f"kT_lo{s}", [P, NK], F32R) for s in range(2)]
        v_hi = [m.sb(f"v_hi{s}", [P, HALF, HD], F32R) for s in range(2)]
        v_lo = [m.sb(f"v_lo{s}", [P, HALF, HD], F32R) for s in range(2)]
        q_hi = [m.sb(f"q_hi{s}", [P, XQ], F32R) for s in range(2)]
        q_lo = [m.sb(f"q_lo{s}", [P, XQ], F32R) for s in range(2)]
        q_max = [m.sb(f"q_max{s}", [P, XQ], F32R) for s in range(2)]
        prob = [m.sb(f"prob{s}", [P, XQ]) for s in range(2)]
        p_hi = [m.sb(f"p_hi{s}", [P, XQ], F32R) for s in range(2)]
        p_lo = [m.sb(f"p_lo{s}", [P, XQ], F32R) for s in range(2)]
        shift = [m.sb(f"shift{s}", [P, XQ]) for s in range(2)]
        total = [m.sb(f"total{s}", [P, XQ]) for s in range(2)]
        zeros = m.sb("zeros", [P, 1])
        part_max = m.sb("part_max", [P, XQT, WIDE + 1])
        query_max = m.sb("query_max", [P, XQT])
        diag = m.sb("diag", [P, XQT, P], F32R)
        ones_r = m.sb("ones_r", [P, P], F32R)
        inverse = m.sb("inverse", [P, XQT])
        diag_inv = m.sb("diag_inv", [P, XQT, P])
        raw = m.sb("raw", [P, XQ])
        out = m.sb("out", [P, XQ])
        o_hi = m.sb("o_hi", [P, XQ], F32R)
        o_lo = m.sb("o_lo", [P, XQ], F32R)
        psS = [m.ps(f"psS{s}", [P, XQ]) for s in range(2)]
        psO = m.ps("psO", [P, XQ])
        psM = m.ps("psM", [P, XQ])

        setup, scores, exps, p_high, o_normed, o_high, o_lowed = map(sem, (
            "setup", "scores", "exps", "p_high", "o_normed", "o_high", "o_lowed"))
        shifted, summed, p_low, pv = map(two, ("shifted", "summed", "p_low", "pv"))
        qm_loaded, v_loaded = map(two, ("qm_loaded", "v_loaded"))
        q_loaded = two("q_loaded")
        k_loaded = [[sem(f"k_loaded{s}_{c}") for c in range(len(PIECES))] for s in range(2)]
        (mx_scores, mx_reduced, query_max_ready, diag_ready, shift_ps, shift_ready, o_raw, total_ps, inverse_ready,
         diag_inv_ready, inv_ps, o_stored) = map(sem, (
             "mx_scores", "mx_reduced", "query_max_ready", "diag_ready", "shift_ps", "shift_ready", "o_raw", "total_ps",
             "inverse_ready", "diag_inv_ready", "inv_ps", "o_stored"))
        PAIRS = XKV // 2

        def unit(u):
            if u < WIDE * XQT:
                c, t = u // XQT, u % XQT
                return ([(t, c * PIECE * P + i * BANK, BANK, i * BANK) for i in range(2)],
                        part_max[:, t:t + 1, c], psM[:].rearrange("p (a n) -> p a n", a=1))
            t = (u - WIDE * XQT) * PER
            return ([(t + i, WIDE * PIECE * P, REST, i * REST) for i in range(PER)],
                    part_max[:, t:t + PER, WIDE], psM[:].rearrange("p (a n) -> p a n", a=PER))

        sems.credit(scores, total_ps, *pv, o_normed, o_stored, *p_low, *summed, inv_ps, o_lowed, *shifted, o_raw)
        with nc.Block() as block:
            @block.sync
            def _(sp):
                def load_qmax(e, s):
                    sp.dma_start(q_max[s][:].bitcast(F32), qT_high[bass.ds(e, 1), :, :].rearrange("e d q -> d (e q)")).then_inc(qm_loaded[s], 16)

                def load_q(e, s):
                    for dst, src in ((q_hi, qT_high), (q_lo, qT_low)):
                        sp.dma_start(dst[s][:].bitcast(F32), src[bass.ds(e, 1), :, :].rearrange("e d q -> d (e q)")).then_inc(q_loaded[s], 16)

                def load_keys(e, s, c):
                    a, b = (x * P for x in PIECES[c])
                    for dst, src in ((kT_hi, keyT_high), (kT_lo, keyT_low)):
                        sp.dma_start(dst[s][:, a:b].bitcast(F32),
                                     src[bass.ds(e, 1), :, a:b].rearrange("e d k -> d (e k)")).then_inc(k_loaded[s][c], 16)

                def load_values(e, half):
                    for dst, src in ((v_hi, val_high), (v_lo, val_low)):
                        sp.dma_start(dst[half][:].bitcast(F32),
                                     src[bass.ds(e, 1), :, half * HALF:(half + 1) * HALF, :].rearrange("e p t d -> p (e t) d")).then_inc(v_loaded[half], 16)

                def store(e):
                    sp.wait_ge(o_lowed, START + e + 1)
                    for src, dst in ((o_hi, outT_high), (o_lo, outT_low)):
                        sp.dma_start(dst[bass.ds(e, 1), :, :].rearrange("e d q -> d (e q)"), src[:].bitcast(F32)).then_inc(o_stored, 16)

                def head(e, s, last):
                    if not last:
                        sp.wait_ge(shift_ready, e + 1)
                        load_qmax(e + 2, s)
                    if not (last and s):
                        sp.wait_ge(scores, START + e * RT)
                        load_q(e + 1, 1 - s)
                    for c, (_, b) in enumerate(PIECES):
                        if c == 1 and s:
                            store(e - 1)
                        if not last:
                            sp.wait_ge(scores, START + e * RT + b)
                            load_keys(e + 2, s, c)
                        if c == 2 and not (last and s):
                            sp.wait_ge(pv[(HALF - 1) % 2], START + e * HALF + (HALF - 1) // 2 + 1)
                            load_values(e + 1, 0)
                    if not (last and s):
                        sp.wait_ge(pv[(RT - 1) % 2], START + e * HALF + HALF)
                        load_values(e + 1, 1)
                    if s:
                        store(e)

                load_qmax(0, 0)
                for c in range(len(PIECES)):
                    load_keys(0, 0, c)
                load_q(0, 0)
                load_values(0, 0)
                load_qmax(1, 1)
                load_keys(1, 1, 0)
                load_values(0, 1)
                for c in range(1, len(PIECES)):
                    load_keys(1, 1, c)
                with sp.Fori(0, PAIRS - 1) as pair:
                    head(pair * 2, 0, False)
                    head(pair * 2 + 1, 1, False)
                head(XKV - 2, 0, True)
                head(XKV - 1, 1, True)
                sp.wait_ge(o_stored, START + 32 * XKV)

            @block.gpsimd
            def _(pool):
                pool.memset(zeros[:], 0.0).then_inc(setup, 1)
                pool.wait_ge(setup, 2)

                def split_out(e):
                    pool.wait_ge(o_high, e + 1)
                    pool.tensor_tensor(o_lo[:], out[:], o_hi[:].bitcast(F32), ALU.subtract).then_inc(o_lowed, 1)

                with pool.Fori(0, PAIRS) as pair:
                    for s in range(2):
                        e = pair * 2 + s
                        for j in range(RT):
                            pool.wait_ge(exps, e * RT + j + 1)
                            if j:
                                pool.wait_ge(summed[(j - 1) % 2], START + e * HALF + (j - 1) // 2 + 1)
                            else:
                                pool.wait_ge(total_ps, START + pair * 2)
                            pool.tensor_tensor(total[s][:], total[s][:] if j else zeros[:].to_broadcast([P, XQ]), prob[j % 2][:],
                                               ALU.add).then_inc(summed[j % 2], 1)
                            if s and j == 2:
                                split_out(e - 1)
                    split_out(pair * 2 + 1)

            @block.scalar
            def _(act):
                def head(pair, s, last):
                    e = pair * 2 + s
                    for j in range(RT):
                        act.wait_ge(shifted[j % 2], START + e * HALF + j // 2 + 1)
                        act.activation(prob[j % 2][:], prob[j % 2][:], ACT.Exp).then_inc(exps, 1)
                        act.wait_ge(exps, e * RT + j + 1)
                        act.wait_ge(pv[j % 2], START + e * HALF + j // 2)
                        act.copy(p_hi[j % 2][:], prob[j % 2][:]).then_inc(p_high, 1)
                        if s and j == 1:
                            take_out(e - 1)
                        if s and j == 2:
                            split_out(e - 1)
                    if not (last and s):
                        act.wait_ge(shift_ps, e + 2)
                        act.copy(shift[1 - s][:], psM[:]).then_inc(shift_ready, 1)
                    if s:
                        take_out(e)
                        split_out(e)

                def take_out(e):
                    act.wait_ge(pv[(RT - 1) % 2], START + e * HALF + HALF)
                    act.wait_ge(o_normed, START + e)
                    act.copy(raw[:], psO[:]).then_inc(o_raw, 1)

                def split_out(e):
                    act.wait_ge(o_normed, START + e + 1)
                    act.wait_ge(o_stored, START + e * 32)
                    act.copy(o_hi[:], out[:]).then_inc(o_high, 1)

                act.wait_ge(shift_ps, 1)
                act.copy(shift[0][:], psM[:]).then_inc(shift_ready, 1)
                with act.Fori(0, PAIRS - 1) as pair:
                    head(pair, 0, False)
                    head(pair, 1, False)
                head(PAIRS - 1, 0, True)
                head(PAIRS - 1, 1, True)

            @block.vector
            def _(dve):
                dve.tensor_copy(ones_r[:], ones[:]).then_inc(setup, 1)

                def reduce_unit(e, u):
                    dve.wait_ge(mx_scores, e * UNITS + u + 1)
                    _, dst, src = unit(u)
                    dve.tensor_reduce(dst, src, AX.X, ALU.max).then_inc(mx_reduced, 1)

                def finish_max(e):
                    dve.wait_ge(mx_reduced, (e + 1) * UNITS)
                    dve.tensor_reduce(query_max[:], part_max[:], AX.X, ALU.max).then_inc(query_max_ready, 1)
                    dve.wait_ge(query_max_ready, e + 1)
                    dve.wait_ge(shift_ps, e)
                    dve.tensor_tensor(diag[:], broadcast_outer(ident[:], XQT), broadcast_inner(query_max[:], P),
                                      ALU.mult).then_inc(diag_ready, 1)

                def low(e, j):
                    dve.wait_ge(p_high, e * RT + j + 1)
                    dve.tensor_tensor(p_lo[j % 2][:], prob[j % 2][:], p_hi[j % 2][:].bitcast(F32), ALU.subtract).then_inc(p_low[j % 2], 1)

                def invert_total(e):
                    dve.wait_ge(total_ps, START + e + 1)
                    dve.reciprocal(inverse[:], psM[:, 0:XQT]).then_inc(inverse_ready, 1)
                    dve.wait_ge(inverse_ready, e + 1)
                    dve.wait_ge(inv_ps, START + e)
                    dve.tensor_tensor(diag_inv[:], broadcast_outer(ident[:], XQT), broadcast_inner(inverse[:], P),
                                      ALU.mult).then_inc(diag_inv_ready, 1)

                def normalise(e):
                    dve.wait_ge(inv_ps, START + e + 1)
                    dve.wait_ge(o_raw, START + e + 1)
                    dve.wait_ge(o_lowed, START + e)
                    dve.tensor_tensor(out[:], psM[:], raw[:], ALU.mult).then_inc(o_normed, 1)

                def head(pair, s, last):
                    e = pair * 2 + s
                    for j in range(RT):
                        if j == 0:
                            dve.wait_ge(shift_ready, e + 1)
                        dve.wait_ge(scores, START + e * RT + j + 1)
                        dve.wait_ge(p_low[j % 2], START + e * HALF + j // 2)
                        dve.wait_ge(summed[j % 2], START + e * HALF + j // 2)
                        dve.tensor_tensor(prob[j % 2][:], psS[j % 2][:], shift[s][:], ALU.subtract).then_inc(shifted[j % 2], 1)
                        if j:
                            low(e, j - 1)
                        elif s:
                            low(e - 1, RT - 1)
                        if s and j == 2:
                            normalise(e - 1)
                        if not (last and s):
                            reduce_unit(e + 1, j)
                        if s and j == 1:
                            invert_total(e - 1)
                    if not (last and s):
                        finish_max(e + 1)
                    if s:
                        low(e, RT - 1)
                        invert_total(e)
                        normalise(e)

                for u in range(UNITS):
                    reduce_unit(0, u)
                finish_max(0)
                with dve.Fori(0, PAIRS - 1) as pair:
                    head(pair, 0, False)
                    head(pair, 1, False)
                head(PAIRS - 1, 0, True)
                head(PAIRS - 1, 1, True)

            @block.tensor
            def _(pe):
                def max_unit(pair, e, s, u):
                    if u == 0:
                        pe.wait_ge(qm_loaded[s], pair * 16 + 16)
                    if u % XQT == 0 and u < WIDE * XQT:
                        pe.wait_ge(k_loaded[s][u // XQT], pair * 32 + 32)
                    pe.wait_ge(mx_reduced, e * UNITS + u)
                    for t, key, n, column in unit(u)[0]:
                        last = pe.matmul(psM[:, column:column + n], q_max[s][:, t * P:(t + 1) * P], kT_hi[s][:, key:key + n],
                                         start=True, stop=True)
                    last.then_inc(mx_scores, 1)

                def spread(src, stationary, done):
                    for c in range(XQ // BANK):
                        last = pe.matmul(psM[:, c * BANK:(c + 1) * BANK], stationary[:],
                                         src[:].rearrange("p t q -> p (t q)")[:, c * BANK:(c + 1) * BANK], start=True, stop=True)
                    last.then_inc(done, 1)

                def spread_max(e):
                    pe.wait_ge(diag_ready, e + 1)
                    spread(diag, ones_r, shift_ps)
                    pe.wait_ge(shift_ready, e + 1)

                def score(e, s, j):
                    pe.wait_ge(shifted[j % 2], START + e * HALF + j // 2)
                    key = slice(j * P, (j + 1) * P)
                    for n, (k, q) in enumerate(((kT_hi, q_hi), (kT_hi, q_lo), (kT_lo, q_hi))):
                        for c in range(XQ // BANK):
                            cols = slice(c * BANK, (c + 1) * BANK)
                            last = pe.matmul(psS[j % 2][:, cols], k[s][:, key], q[s][:, cols], start=(n == 0), stop=(n == 2))
                    last.then_inc(scores, 1)

                def value(e, j):
                    if j % HALF == 0:
                        pe.wait_ge(v_loaded[j // HALF], e * 32 + 32)
                    if j == 0:
                        pe.wait_ge(o_raw, START + e)
                    pe.wait_ge(p_low[j % 2], START + e * HALF + j // 2 + 1)
                    for n, (v, p) in enumerate(((v_hi, p_hi), (v_hi, p_lo), (v_lo, p_hi))):
                        for c in range(XQ // BANK):
                            cols = slice(c * BANK, (c + 1) * BANK)
                            last = pe.matmul(psO[:, cols], v[j // HALF][:, j % HALF, :], p[j % 2][:, cols],
                                             start=(j == 0 and n == 0), stop=(j == RT - 1 and n == 2))
                    last.then_inc(pv[j % 2], 1)

                def sum_total(e, s, units):
                    pe.wait_ge(mx_reduced, units)
                    pe.wait_ge(summed[(RT - 1) % 2], START + e * HALF + HALF)
                    for t in range(XQT):
                        last = pe.matmul(psM[:, t:t + 1], total[s][:, t * P:(t + 1) * P], ones[:, 0:1], start=True, stop=True)
                    last.then_inc(total_ps, 1)

                def spread_inverse(e):
                    pe.wait_ge(diag_inv_ready, e + 1)
                    spread(diag_inv, ones, inv_ps)
                    pe.wait_ge(o_normed, START + e + 1)

                def head(pair, s, last):
                    e = pair * 2 + s
                    pe.wait_ge(q_loaded[s], pair * 32 + 32)
                    for j in range(RT):
                        for c, (a, _) in enumerate(PIECES):
                            if a == j:
                                pe.wait_ge(k_loaded[s][c], pair * 32 + 32)
                        score(e, s, j)
                        if s and j == 2:
                            spread_inverse(e - 1)
                        if not (last and s):
                            max_unit(pair + s, e + 1, 1 - s, j)
                        if j >= 2:
                            value(e, j - 2)
                        elif s:
                            value(e - 1, RT - 2 + j)
                        if s and j == 1:
                            sum_total(e - 1, 1 - s, XKV * UNITS if last else (e + 1) * UNITS + 2)
                    if not (last and s):
                        spread_max(e + 1)
                    if s:
                        value(e, RT - 2)
                        value(e, RT - 1)
                        sum_total(e, s, XKV * UNITS if last else (e + 2) * UNITS)
                        spread_inverse(e)

                pe.wait_ge(setup, 2)
                for u in range(UNITS):
                    max_unit(0, 0, 0, u)
                spread_max(0)
                with pe.Fori(0, PAIRS - 1) as pair:
                    head(pair, 0, False)
                    head(pair, 1, False)
                head(PAIRS - 1, 0, True)
                head(PAIRS - 1, 1, True)


def cross_output(nc, sems, Wo, outT_high, outT_low, x, x1):
    with ExitStack() as stack:
        m = Scope(nc, stack, "xo")
        sem = make_sem(nc, sems, "xo")
        two = lambda name: [sem(f"{name}{s}") for s in range(2)]
        w_raw = [m.sb(f"w_raw{s}", [P, XG, D]) for s in range(2)]
        w_hi = [m.sb(f"w_hi{s}", [P, XG, D], F32R) for s in range(2)]
        w_lo = [m.sb(f"w_lo{s}", [P, XG, D], F32R) for s in range(2)]
        o_hi = [m.sb(f"o_hi{s}", [P, XQ], F32R) for s in range(2)]
        o_lo = [m.sb(f"o_lo{s}", [P, XQ], F32R) for s in range(2)]
        acc = m.sb("acc", [P, QT, D])
        psX = [m.ps(f"psX{s}", [P, QT, D]) for s in range(2)]
        x_loaded, stored = sem("x_loaded"), sem("stored")
        w_loaded, o_loaded, w_high, w_low, projected, added = map(
            two, ("w_loaded", "o_loaded", "w_high", "w_low", "projected", "added"))
        PAIRS = XKV // 2
        Wo_v = Wo.rearrange("(e g d) n -> e d g n", g=XG, d=HD)
        sems.credit(*projected, *added)
        with nc.Block() as block:
            @block.sync
            def _(sp):
                def load(e, s):
                    sp.dma_start(w_raw[s][:], Wo_v[bass.ds(e, 1), :, :, :].rearrange("e d g n -> d (e g) n")).then_inc(w_loaded[s], 16)

                def load_out(e, s):
                    for dst, src in ((o_hi, outT_high), (o_lo, outT_low)):
                        sp.dma_start(dst[s][:].bitcast(F32), src[bass.ds(e, 1), :, :].rearrange("e d q -> d (e q)")).then_inc(o_loaded[s], 16)

                for s in range(2):
                    load(s, s)
                    load_out(s, s)
                sp.dma_start(acc[:], x.rearrange("(t p) d -> p t d", p=P)).then_inc(x_loaded, 16)
                with sp.Fori(0, PAIRS - 1) as pair:
                    for s in range(2):
                        sp.wait_ge(w_low[s], pair + 1)
                        load(pair * 2 + (2 + s), s)
                        sp.wait_ge(projected[s], START + pair + 1)
                        load_out(pair * 2 + (2 + s), s)
                sp.wait_ge(added[1], START + PAIRS)
                sp.dma_start(x1.rearrange("(t p) d -> p t d", p=P), acc[:]).then_inc(stored, 16)
                sp.wait_ge(stored, 16)

            @block.scalar
            def _(act):
                with act.Fori(0, PAIRS) as pair:
                    for s in range(2):
                        act.wait_ge(w_loaded[s], pair * 16 + 16)
                        act.wait_ge(projected[s], START + pair)
                        act.copy(w_hi[s][:], w_raw[s][:]).then_inc(w_high[s], 1)

            @block.vector
            def _(dve):
                dve.wait_ge(x_loaded, 16)
                with dve.Fori(0, PAIRS) as pair:
                    for s in range(2):
                        dve.wait_ge(w_high[s], pair + 1)
                        dve.tensor_tensor(w_lo[s][:], w_raw[s][:], w_hi[s][:].bitcast(F32), ALU.subtract).then_inc(w_low[s], 1)
                    for s in range(2):
                        dve.wait_ge(projected[s], START + pair + 1)
                        dve.wait_ge(added[1 - s], START + pair + s)
                        dve.tensor_tensor(acc[:], psX[s][:], acc[:], ALU.add).then_inc(added[s], 1)

            @block.tensor
            def _(pe):
                with pe.Fori(0, PAIRS) as pair:
                    for s in range(2):
                        pe.wait_ge(o_loaded[s], pair * 32 + 32)
                        pe.wait_ge(w_low[s], pair + 1)
                        pe.wait_ge(added[s], START + pair)
                        for t in range(QT):
                            for g in range(XG):
                                rows = slice(g * NQ + t * P, g * NQ + (t + 1) * P)
                                for n, (o, w) in enumerate(((o_hi, w_hi), (o_hi, w_lo), (o_lo, w_hi))):
                                    for c in range(D // BANK):
                                        cols = slice(c * BANK, (c + 1) * BANK)
                                        last = pe.matmul(psX[s][:, t, cols], o[s][:, rows], w[s][:, g, cols],
                                                         start=(g == 0 and n == 0), stop=(g == XG - 1 and n == 2))
                        last.then_inc(projected[s], 1)


SH = 64
SG = 16
GH = SH // SG
LORA = 256
LT = LORA // P
ROPE = 64
PAIR = ROPE // 2
OGROUPS = 8
OHEADS = SH // OGROUPS
ORANK = 256
ORT = ORANK // P
OTILES = OGROUPS * ORT
MASKED = -1e30


def rotate(eng, ins, a, b, c, d, after_products, done, count):
    x1, x2, cos, sin = ins
    eng.tensor_tensor(a, x1, cos, ALU.mult)
    eng.tensor_tensor(b, x2, sin, ALU.mult)
    eng.tensor_tensor(c, x1, sin, ALU.mult)
    eng.tensor_tensor(d, x2, cos, ALU.mult).then_inc(after_products, 1)
    eng.wait_ge(after_products, count)
    eng.tensor_tensor(x1, a, b, ALU.subtract)
    eng.tensor_tensor(x2, c, d, ALU.add).then_inc(done, 1)


def latent_projections(nc, sems, wq_a, wkv, q_norm_w, kv_norm_w, cos, sin, ident, ident_bf, yT_high, yT_low,
                       qrT_high, qrT_low, kv_high, kv_low, kvT_high, kvT_low):
    with ExitStack() as stack:
        m = Scope(nc, stack, "lp")
        sem = make_sem(nc, sems, "lp")
        WT = LT + 1
        w_raw = m.sb("w_raw", [P, WT, D], BF16)
        wT = m.sb("wT", [P, KT, WT * P], F32R)
        q_w = m.sb("q_w", [P, LORA], BF16)
        kv_w = m.sb("kv_w", [P, HD], BF16)
        cos_sb = m.sb("cos_sb", [P, QT, PAIR])
        sin_sb = m.sb("sin_sb", [P, QT, PAIR])
        products = [m.sb(f"product{i}", [P, QT, PAIR]) for i in range(4)]
        unused = m.sb("unused", [P, QT, LORA + HD])
        squares = m.sb("squares", [P, 2, QT])
        var = m.sb("var", [P, 2, QT])
        rstd = m.sb("rstd", [P, 2, QT])
        power = m.sb("power", [P, 2, QT])
        qr = m.sb("qr", [P, QT, LORA])
        kv = m.sb("kv", [P, QT, HD])
        psW = m.ps("psW", [P, KT, WT * P], BF16)
        psP = m.ps("psP", [P, QT, BANK])
        psT = m.ps("psT", [P, WT, NQ])
        (w_loaded, norm_loaded, rope_loaded, w_transposed, w_ready, projected, squared, var_ready, rstd_ready, qr_ready,
         kv_normed, kv_products, kv_ready, kv_split, transposed, high, power_set) = map(sem, (
             "w_loaded", "norm_loaded", "rope_loaded", "w_transposed", "w_ready", "projected", "squared", "var_ready",
             "rstd_ready", "qr_ready", "kv_normed", "kv_products", "kv_ready", "kv_split", "transposed", "high", "power_set"))
        with nc.Block() as block:
            @block.sync
            def _(sp):
                sp.dma_start(w_raw[:, 0:LT, :], wq_a.rearrange("(t p) n -> p t n", p=P)).then_inc(w_loaded, 16)
                sp.dma_start(w_raw[:, LT, :], wkv).then_inc(w_loaded, 16)
                sp.dma_start(q_w[:], q_norm_w.rearrange("(a n) -> a n", a=1).to_broadcast([P, LORA])).then_inc(norm_loaded, 16)
                sp.dma_start(kv_w[:], kv_norm_w.rearrange("(a n) -> a n", a=1).to_broadcast([P, HD])).then_inc(norm_loaded, 16)
                sp.dma_start(cos_sb[:], cos.rearrange("(t p) n -> p t n", p=P)).then_inc(rope_loaded, 16)
                sp.dma_start(sin_sb[:], sin.rearrange("(t p) n -> p t n", p=P)).then_inc(rope_loaded, 16)

            @block.gpsimd
            def _(pool):
                pool.memset(power[:], -0.5).then_inc(power_set, 1)
                pool.wait_ge(power_set, 1)
                pool.wait_ge(var_ready, 1)
                pool.tensor_tensor(rstd[:], var[:], power[:], ALU.pow).then_inc(rstd_ready, 1)

            @block.tensor
            def _(pe):
                pe.wait_ge(w_loaded, 32)
                for k in range(KT):
                    for t in range(WT):
                        last = pe.transpose(psW[:, k, t * P:(t + 1) * P], w_raw[:, t, k * P:(k + 1) * P], ident_bf[:])
                last.then_inc(w_transposed, 1)
                pe.wait_ge(w_ready, 1)
                for t in range(QT):
                    for k in range(KT):
                        for n, y in enumerate((yT_high, yT_low)):
                            last = pe.matmul(psP[:, t, 0:WT * P], y[:, k, t * P:(t + 1) * P], wT[:, k, :],
                                             start=(k == 0 and n == 0), stop=(k == KT - 1 and n == 1))
                last.then_inc(projected, 1)
                pe.wait_ge(qr_ready, 1)
                for t in range(QT):
                    for r in range(LT):
                        pe.transpose(psT[:, r, t * P:(t + 1) * P], qr[:, t, r * P:(r + 1) * P], ident[:])
                pe.wait_ge(kv_ready, 1)
                for t in range(QT):
                    last = pe.transpose(psT[:, LT, t * P:(t + 1) * P], kv[:, t, :], ident[:])
                last.then_inc(transposed, 1)

            @block.scalar
            def _(act):
                act.wait_ge(w_transposed, 1)
                act.copy(wT[:], psW[:]).then_inc(w_ready, 1)
                act.wait_ge(projected, 1)
                for t in range(QT):
                    act.activation(unused[:, t, 0:LORA], psP[:, t, 0:LORA], ACT.Square, accum_out=squares[:, 0, t:t + 1])
                    last = act.activation(unused[:, t, LORA:LORA + HD], psP[:, t, LORA:LORA + HD], ACT.Square,
                                          accum_out=squares[:, 1, t:t + 1])
                last.then_inc(squared, 1)
                act.wait_ge(kv_ready, 1)
                act.copy(kv_high[:], kv[:]).then_inc(kv_split, 1)
                act.wait_ge(transposed, 1)
                act.copy(qrT_high[:], psT[:, 0:LT, :])
                act.copy(kvT_high[:], psT[:, LT, :]).then_inc(high, 1)

            @block.vector
            def _(dve):
                dve.wait_ge(squared, 1)
                dve.tensor_scalar(var[:, 0, :], squares[:, 0, :], 1.0 / LORA, RMS_EPS, ALU.mult, ALU.add)
                dve.tensor_scalar(var[:, 1, :], squares[:, 1, :], 1.0 / HD, RMS_EPS, ALU.mult, ALU.add).then_inc(var_ready, 1)
                dve.wait_ge(norm_loaded, 32)
                dve.wait_ge(rstd_ready, 1)
                for t in range(QT):
                    last = dve.scalar_tensor_tensor(qr[:, t, :], psP[:, t, 0:LORA], rstd[:, 0, t:t + 1], q_w[:], ALU.mult, ALU.mult)
                last.then_inc(qr_ready, 1)
                for t in range(QT):
                    last = dve.scalar_tensor_tensor(kv[:, t, :], psP[:, t, LORA:LORA + HD], rstd[:, 1, t:t + 1], kv_w[:], ALU.mult, ALU.mult)
                last.then_inc(kv_normed, 1)
                dve.wait_ge(kv_normed, 1)
                dve.wait_ge(rope_loaded, 32)
                pairs = kv[:, :, HD - ROPE:].rearrange("p t (i two) -> p t i two", two=2)
                rotate(dve, (pairs[:, :, :, 0], pairs[:, :, :, 1], cos_sb[:], sin_sb[:]), *[x[:] for x in products],
                       kv_products, kv_ready, 1)
                dve.wait_ge(kv_split, 1)
                dve.tensor_tensor(kv_low[:], kv[:], kv_high[:].bitcast(F32), ALU.subtract)
                dve.wait_ge(high, 1)
                dve.tensor_tensor(qrT_low[:], psT[:, 0:LT, :], qrT_high[:].bitcast(F32), ALU.subtract)
                dve.tensor_tensor(kvT_low[:], psT[:, LT, :], kvT_high[:].bitcast(F32), ALU.subtract)


def self_queries(nc, sems, wq_b, cos, sin, ident, ident_bf, qrT_high, qrT_low, qT_high, qT_low):
    with ExitStack() as stack:
        m = Scope(nc, stack, "sq")
        sem = make_sem(nc, sems, "sq")
        two = lambda name: [sem(f"{name}{s}") for s in range(2)]
        GC = GH * HD
        w_raw = [m.sb(f"w_raw{s}", [P, GH, LORA], BF16) for s in range(2)]
        wT = [m.sb(f"wT{s}", [P, LT, GC], F32R) for s in range(2)]
        q = [m.sb(f"q{s}", [P, QT, GH, HD]) for s in range(2)]
        cos_sb = m.sb("cos_sb", [P, QT, PAIR])
        sin_sb = m.sb("sin_sb", [P, QT, PAIR])
        products = [m.sb(f"product{i}", [P, GH, PAIR]) for i in range(4)]
        squares = [m.sb(f"squares{s}", [P, QT * GH]) for s in range(2)]
        var = [m.sb(f"var{s}", [P, QT * GH]) for s in range(2)]
        rstd = [m.sb(f"rstd{s}", [P, QT * GH]) for s in range(2)]
        power = m.sb("power", [P, QT * GH])
        unused = m.sb("unused", [P, 2, QT * GH, HD])
        psW = [m.ps(f"psW{s}", [P, LT, GC], BF16) for s in range(2)]
        psQ = [m.ps(f"psQ{s}", [P, QT, GH, HD]) for s in range(2)]
        psT = m.ps("psT", [P, QT, GH, P])
        rope_loaded, power_set, rope_products, rope_done = map(sem, ("rope_loaded", "power_set", "rope_products", "rope_done"))
        w_loaded, w_transposed, w_ready, projected, squared, var_ready, rstd_ready, normed, transposed, high, low = map(
            two, ("w_loaded", "w_transposed", "w_ready", "projected", "squared", "var_ready", "rstd_ready", "normed",
                  "transposed", "high", "low"))
        PAIRS = SG // 2
        w_v = wq_b.rearrange("(g h p) r -> g p h r", h=GH, p=P)
        sems.credit(*w_transposed, *w_ready, *projected, *normed, *low, *transposed, *var_ready, rope_done)
        with nc.Block() as block:
            @block.sync
            def _(sp):
                def load(pair, s):
                    sp.wait_ge(w_transposed[s], START + pair)
                    sp.dma_start(w_raw[s][:], w_v[bass.ds(pair * 2 + s, 1), :, :, :].rearrange("g p h r -> p (g h) r")).then_inc(w_loaded[s], 16)

                sp.dma_start(cos_sb[:], cos.rearrange("(t p) n -> p t n", p=P)).then_inc(rope_loaded, 16)
                sp.dma_start(sin_sb[:], sin.rearrange("(t p) n -> p t n", p=P)).then_inc(rope_loaded, 16)
                pipeline(sp, PAIRS, [(0, load)])

            @block.gpsimd
            def _(pool):
                def root(pair, s):
                    pool.wait_ge(var_ready[s], START + pair + 1)
                    pool.tensor_tensor(rstd[s][:], var[s][:], power[:], ALU.pow).then_inc(rstd_ready[s], 1)

                pool.memset(power[:], -0.5).then_inc(power_set, 1)
                pool.wait_ge(power_set, 1)
                pipeline(pool, PAIRS, [(0, root)])

            @block.tensor
            def _(pe):
                def transpose_weights(pair, s):
                    pe.wait_ge(w_loaded[s], pair * 16 + 16)
                    pe.wait_ge(w_ready[s], START + pair)
                    for r in range(LT):
                        for h in range(GH):
                            last = pe.transpose(psW[s][:, r, h * HD:(h + 1) * HD], w_raw[s][:, h, r * P:(r + 1) * P], ident_bf[:])
                    last.then_inc(w_transposed[s], 1)

                def multiply(pair, s):
                    pe.wait_ge(w_ready[s], START + pair + 1)
                    pe.wait_ge(normed[s], START + pair)
                    for t in range(QT):
                        for r in range(LT):
                            for n, x in enumerate((qrT_high, qrT_low)):
                                last = pe.matmul(psQ[s][:, t, :, :].rearrange("p h d -> p (h d)"), x[:, r, t * P:(t + 1) * P],
                                                 wT[s][:, r, :], start=(r == 0 and n == 0), stop=(r == LT - 1 and n == 1))
                    last.then_inc(projected[s], 1)

                def transpose(pair, s):
                    pe.wait_ge(rope_done, START + pair * 4 + 2 * (s + 1))
                    pe.wait_ge(low[1 - s], START + pair + s)
                    for t in range(QT):
                        for h in range(GH):
                            last = pe.transpose(psT[:, t, h, :], q[s][:, t, h, :], ident[:])
                    last.then_inc(transposed[s], 1)

                pipeline(pe, PAIRS, [(1, multiply), (2, transpose_weights), (0, transpose)])

            @block.scalar
            def _(act):
                def copy_weights(pair, s):
                    act.wait_ge(w_transposed[s], START + pair + 1)
                    act.wait_ge(projected[s], START + pair)
                    act.copy(wT[s][:], psW[s][:]).then_inc(w_ready[s], 1)

                def square(pair, s):
                    act.wait_ge(projected[s], START + pair + 1)
                    act.wait_ge(var_ready[s], START + pair)
                    for t in range(QT):
                        for h in range(GH):
                            i = t * GH + h
                            last = act.activation(unused[:, s, i, :], psQ[s][:, t, h, :], ACT.Square, accum_out=squares[s][:, i:i + 1])
                    last.then_inc(squared[s], 1)

                def split(pair, s):
                    act.wait_ge(transposed[s], START + pair + 1)
                    act.activation(qT_high[:, bass.ds(pair * 2 + s, 1), :, :, :].rearrange("p g t h q -> p (g t h q)"),
                                   psT[:].rearrange("p t h q -> p (t h q)"), ACT.Copy, scale=SCALE).then_inc(high[s], 1)

                pipeline(act, PAIRS, [(1, square), (2, copy_weights), (0, split)])

            @block.vector
            def _(dve):
                def normalise(pair, s):
                    dve.wait_ge(squared[s], pair + 1)
                    dve.tensor_scalar(var[s][:], squares[s][:], 1.0 / HD, RMS_EPS, ALU.mult, ALU.add).then_inc(var_ready[s], 1)
                    dve.wait_ge(rstd_ready[s], pair + 1)
                    dve.wait_ge(transposed[s], START + pair)
                    dve.tensor_tensor(q[s][:].rearrange("p t h d -> p (t h) d"), psQ[s][:].rearrange("p t h d -> p (t h) d"),
                                      broadcast_inner(rstd[s][:], HD), ALU.mult).then_inc(normed[s], 1)
                    dve.wait_ge(normed[s], START + pair + 1)
                    for t in range(QT):
                        pairs = q[s][:, t, :, HD - ROPE:].rearrange("p h (i two) -> p h i two", two=2)
                        count = pair * 4 + (2 * s + t)
                        dve.wait_ge(rope_done, START + count)
                        rotate(dve, (pairs[:, :, :, 0], pairs[:, :, :, 1], broadcast_outer(cos_sb[:, t, :], GH),
                                     broadcast_outer(sin_sb[:, t, :], GH)), *[x[:] for x in products],
                               rope_products, rope_done, count + 1)

                def split(pair, s):
                    dve.wait_ge(high[s], pair + 1)
                    group = bass.ds(pair * 2 + s, 1)
                    dve.scalar_tensor_tensor(qT_low[:, group, :, :, :].rearrange("p g t h q -> p (g t h q)"),
                                             psT[:].rearrange("p t h q -> p (t h q)"), SCALE,
                                             qT_high[:, group, :, :, :].rearrange("p g t h q -> p (g t h q)").bitcast(F32),
                                             ALU.mult, ALU.subtract).then_inc(low[s], 1)

                dve.wait_ge(rope_loaded, 32)
                pipeline(dve, PAIRS, [(1, normalise), (0, split)])


def self_maxima(nc, sems, sink, ident, kvT_high, qT_high, triangle_qk, ident_r, query_max, sink_exp):
    with ExitStack() as stack:
        m = Scope(nc, stack, "sm")
        sem = make_sem(nc, sems, "sm")
        two = lambda name: [sem(f"{name}{s}") for s in range(2)]
        sink_sb = m.sb("sink_sb", [P, SG, GH])
        stationary = [m.sb(f"stationary{s}", [P, QT, GH, P], F32R) for s in range(2)]
        raw_max = m.sb("raw_max", [P, SG, QT, GH])
        sink_shifted = m.sb("sink_shifted", [P, SG, QT, GH])
        ps0 = [m.ps(f"ps0{s}", [P, GH, P]) for s in range(2)]
        ps1 = [m.ps(f"ps1{s}", [P, GH, 2 * P]) for s in range(2)]
        sink_loaded, all_max, rounded, shifted = map(sem, ("sink_loaded", "all_max", "rounded", "shifted"))
        staged, scored, reduced = map(two, ("staged", "scored", "reduced"))
        PAIRS = SG // 2
        sems.credit(*scored, *reduced)
        with nc.Block() as block:
            @block.sync
            def _(sp):
                sp.dma_start(sink_sb[:].rearrange("p g h -> p (g h)"),
                             sink.rearrange("(a n) -> a n", a=1).to_broadcast([P, SH])).then_inc(sink_loaded, 16)

            @block.scalar
            def _(act):
                with act.Fori(0, PAIRS) as pair:
                    for s in range(2):
                        act.wait_ge(scored[s], START + pair)
                        act.copy(stationary[s][:], qT_high[:, bass.ds(pair * 2 + s, 1), :, :, :].rearrange(
                            "p g t h q -> p (g t) h q").bitcast(F32)).then_inc(staged[s], 1)
                act.wait_ge(shifted, 1)
                act.activation(sink_exp[:], sink_shifted[:], ACT.Exp)

            @block.tensor
            def _(pe):
                with pe.Fori(0, PAIRS) as pair:
                    for s in range(2):
                        pe.wait_ge(staged[s], pair + 1)
                        pe.wait_ge(reduced[s], START + pair)
                        pe.matmul(ps0[s][:], ident_r[:], broadcast_outer(triangle_qk[:, P:2 * P], GH), start=True, stop=False)
                        for h in range(GH):
                            pe.matmul(ps0[s][:, h, :], stationary[s][:, 0, h, :], kvT_high[:, 0:P], start=False, stop=(h == GH - 1))
                        for a in range(0, GH, 2):
                            pe.matmul(ps1[s][:, a:a + 2, :], ident_r[:], broadcast_outer(triangle_qk[:], 2), start=True, stop=False)
                            for h in (a, a + 1):
                                last = pe.matmul(ps1[s][:, h, :], stationary[s][:, 1, h, :], kvT_high[:], start=False, stop=(h == a + 1))
                        last.then_inc(scored[s], 1)

            @block.vector
            def _(dve):
                with dve.Fori(0, PAIRS) as pair:
                    for s in range(2):
                        dve.wait_ge(scored[s], START + pair + 1)
                        group = bass.ds(pair * 2 + s, 1)
                        dve.tensor_reduce(raw_max[:, group, 0, :].rearrange("p g h -> p (g h)"), ps0[s][:], AX.X, ALU.max)
                        dve.tensor_reduce(raw_max[:, group, 1, :].rearrange("p g h -> p (g h)"), ps1[s][:], AX.X, ALU.max).then_inc(reduced[s], 1)
                for s in range(2):
                    dve.wait_ge(reduced[s], START + PAIRS)
                dve.wait_ge(sink_loaded, 16)
                for t in range(QT):
                    last = dve.tensor_tensor(query_max[:, :, t, :], raw_max[:, :, t, :], sink_sb[:], ALU.max)
                last.then_inc(rounded, 1)
                dve.wait_ge(rounded, 1)
                for t in range(QT):
                    last = dve.tensor_tensor(sink_shifted[:, :, t, :], sink_sb[:], query_max[:, :, t, :].bitcast(F32), ALU.subtract)
                last.then_inc(shifted, 1)


def self_attention(nc, sems, ident, ones, ident_r, ones_r, triangle_kq, kv_high, kv_low, kvT_high, kvT_low,
                   query_max, sink_exp, qT_high, qT_low, inverse):
    with ExitStack() as stack:
        m = Scope(nc, stack, "sa")
        sem = make_sem(nc, sems, "sa")
        two = lambda name: [sem(f"{name}{s}") for s in range(2)]
        CHUNKS = [(0, 0), (1, 0), (1, 1)]
        NC = len(CHUNKS)
        GQ = GH * P
        diag = m.sb("diag", [P, QT * GH, P], F32R)
        shift = [m.sb(f"shift{s}", [P, QT, GQ]) for s in range(2)]
        prob = [m.sb(f"prob{s}", [P, NC, GQ]) for s in range(2)]
        p_hi = [m.sb(f"p_hi{s}", [P, NC, GQ], F32R) for s in range(2)]
        p_lo = [m.sb(f"p_lo{s}", [P, NC, GQ], F32R) for s in range(2)]
        sums = [m.sb(f"sums{s}", [P, QT * GH]) for s in range(2)]
        psM = m.ps("psM", [P, QT, GQ])
        psS = m.ps("psS", [P, NC, GQ])
        psO = m.ps("psO", [P, QT, GQ])
        psD = m.ps("psD", [P, QT * GH])
        (diag_ready, spread, shift_ready, scored, shifted, exps, p_high, p_low, added_chunks, valued, o_high, o_low, summed,
         added, inverted) = map(two, ("diag_ready", "spread", "shift_ready", "scored", "shifted", "exps", "p_high", "p_low",
                                      "added_chunks", "valued", "o_high", "o_low", "summed", "added", "inverted"))
        PAIRS = SG // 2

        def group(ap, pair, s):
            return ap[:, bass.ds(pair * 2 + s, 1), :, :, :].rearrange("p g t h q -> p (g t) (h q)")

        def small(ap, pair, s):
            return ap[:, bass.ds(pair * 2 + s, 1), :, :].rearrange("p g t h -> p (g t h)")

        sems.credit(*o_low, *added, *valued, *summed, *inverted, *shift_ready, *shifted, *spread)
        with nc.Block() as block:
            @block.tensor
            def _(pe):
                def spread_maxima(pair, s):
                    pe.wait_ge(diag_ready[s], pair + 1)
                    pe.wait_ge(shift_ready[1 - s], START + pair + s)
                    for t in range(QT):
                        last = pe.matmul(psM[:, t, :], ones_r[:], diag[:, t * GH:(t + 1) * GH, :].rearrange("p h q -> p (h q)"),
                                         start=True, stop=True)
                    last.then_inc(spread[s], 1)

                def scores(pair, s):
                    pe.wait_ge(shifted[1 - s], START + pair + s)
                    for i, (t, k) in enumerate(CHUNKS):
                        if t == k:
                            pe.matmul(psS[:, i, :], ident_r[:], broadcast_outer(triangle_kq[:], GH), start=True, stop=False)
                        for n, (key, q) in enumerate(((kvT_high, qT_high), (kvT_high, qT_low), (kvT_low, qT_high))):
                            last = pe.matmul(psS[:, i, :], key[:, k * P:(k + 1) * P], group(q, pair, s)[:, t, :],
                                             start=(n == 0 and t != k), stop=(n == 2))
                    last.then_inc(scored[s], 1)

                def values(pair, s):
                    pe.wait_ge(p_low[s], pair + 1)
                    pe.wait_ge(o_low[1 - s], START + pair + s)
                    for i, (t, k) in enumerate(CHUNKS):
                        for n, (v, p) in enumerate(((kv_high, p_hi), (kv_high, p_lo), (kv_low, p_hi))):
                            last = pe.matmul(psO[:, t, :], v[:, k, :], p[s][:, i, :], start=(n == 0 and k == 0),
                                             stop=(n == 2 and t == k))
                    last.then_inc(valued[s], 1)
                    pe.wait_ge(added[1 - s], START + pair + s)
                    pe.wait_ge(added_chunks[s], pair + 1)
                    for t in range(QT):
                        for h in range(GH):
                            last = pe.matmul(psD[:, t * GH + h:t * GH + h + 1], prob[s][:, 2 * t, h * P:(h + 1) * P],
                                             ones[:, 0:1], start=True, stop=True)
                    last.then_inc(summed[s], 1)

                pipeline(pe, PAIRS, [(1, scores), (2, spread_maxima), (0, values)])

            @block.scalar
            def _(act):
                def take_maxima(pair, s):
                    act.wait_ge(spread[s], START + pair + 1)
                    act.wait_ge(shifted[s], START + pair)
                    act.copy(shift[s][:], psM[:]).then_inc(shift_ready[s], 1)

                def exponentials(pair, s):
                    act.wait_ge(shifted[s], START + pair + 1)
                    act.activation(prob[s][:], prob[s][:], ACT.Exp).then_inc(exps[s], 1)
                    act.wait_ge(exps[s], pair + 1)
                    act.wait_ge(valued[s], START + pair)
                    act.copy(p_hi[s][:], prob[s][:]).then_inc(p_high[s], 1)

                def take_out(pair, s):
                    act.wait_ge(valued[s], START + pair + 1)
                    act.copy(group(qT_high, pair, s), psO[:]).then_inc(o_high[s], 1)

                pipeline(act, PAIRS, [(1, exponentials), (2, take_maxima), (0, take_out)])

            @block.gpsimd
            def _(pool):
                def add_chunks(pair, s):
                    pool.wait_ge(p_low[s], pair + 1)
                    pool.tensor_tensor(prob[s][:, 2, :], prob[s][:, 1, :], prob[s][:, 2, :], ALU.add).then_inc(added_chunks[s], 1)

                pipeline(pool, PAIRS, [(0, add_chunks)])

            @block.vector
            def _(dve):
                def place_maxima(pair, s):
                    dve.wait_ge(spread[1 - s], START + pair + s)
                    dve.tensor_tensor(diag[:], broadcast_outer(ident[:], QT * GH),
                                      broadcast_inner(small(query_max, pair, s).bitcast(F32), P), ALU.mult).then_inc(diag_ready[s], 1)

                def shift_scores(pair, s):
                    dve.wait_ge(shift_ready[s], START + pair + 1)
                    dve.wait_ge(scored[s], pair + 1)
                    dve.wait_ge(summed[s], START + pair)
                    dve.tensor_tensor(prob[s][:, 0, :], psS[:, 0, :], shift[s][:, 0, :], ALU.subtract)
                    dve.tensor_tensor(prob[s][:, 1:3, :], psS[:, 1:3, :], broadcast_outer(shift[s][:, 1, :], 2), ALU.subtract).then_inc(shifted[s], 1)

                def split_probabilities(pair, s):
                    dve.wait_ge(p_high[s], pair + 1)
                    dve.tensor_tensor(p_lo[s][:], prob[s][:], p_hi[s][:].bitcast(F32), ALU.subtract).then_inc(p_low[s], 1)

                def take_out(pair, s):
                    dve.wait_ge(o_high[s], pair + 1)
                    dve.tensor_tensor(group(qT_low, pair, s), psO[:], group(qT_high, pair, s).bitcast(F32), ALU.subtract).then_inc(o_low[s], 1)
                    dve.wait_ge(summed[s], START + pair + 1)
                    dve.wait_ge(inverted[s], START + pair)
                    dve.tensor_tensor(sums[s][:], psD[:], small(sink_exp, pair, s), ALU.add).then_inc(added[s], 1)
                    dve.wait_ge(added[s], START + pair + 1)
                    dve.reciprocal(small(inverse, pair, s), sums[s][:]).then_inc(inverted[s], 1)

                pipeline(dve, PAIRS, [(0, split_probabilities), (1, shift_scores), (3, place_maxima), (0, take_out)])


def rotate_outputs(nc, sems, cos, sin, ident, ones, ident_r, swap_r, oT_high, oT_low, inverse):
    with ExitStack() as stack:
        m = Scope(nc, stack, "ro")
        sem = make_sem(nc, sems, "ro")
        two = lambda name: [sem(f"{name}{s}") for s in range(2)]
        GQ = GH * P
        angle = m.sb("angle", [P, 2, QT, PAIR])
        wide = m.sb("wide", [P, 2, QT, HD])
        wideT = m.sb("wideT", [P, 2, QT, P])
        by_cos = [m.sb(f"by_cos{s}", [P, QT, GH, P]) for s in range(2)]
        by_sin = [m.sb(f"by_sin{s}", [P, QT, GH, P]) for s in range(2)]
        turned = [m.sb(f"turned{s}", [P, QT * GQ]) for s in range(2)]
        out = [m.sb(f"out{s}", [P, QT * GQ]) for s in range(2)]
        diag = m.sb("diag", [P, QT * GH, P])
        psU = m.ps("psU", [P, QT, GQ])
        psR = m.ps("psR", [P, QT, GQ])
        psI = m.ps("psI", [P, QT * GQ])
        psT = m.ps("psT", [P, 2, QT, P])
        angles_loaded, filled, widened, wide_transposed, wide_ready = map(sem, (
            "angles_loaded", "filled", "widened", "wide_transposed", "wide_ready"))
        moved, multiplied, turned_ready, diag_ready, spread, scaled, high, low = map(
            two, ("moved", "multiplied", "turned_ready", "diag_ready", "spread", "scaled", "high", "low"))
        PAIRS = SG // 2

        def group(ap, pair, s):
            return ap[:, bass.ds(pair * 2 + s, 1), :, :, :].rearrange("p g t h q -> p (g t) (h q)")

        sems.credit(*scaled, *multiplied, *spread, *turned_ready, *low)
        with nc.Block() as block:
            @block.sync
            def _(sp):
                for i, src in enumerate((cos, sin)):
                    sp.dma_start(angle[:, i, :, :], src.rearrange("(t p) n -> p t n", p=P)).then_inc(angles_loaded, 16)

            @block.gpsimd
            def _(pool):
                pool.memset(wide[:, 0, :, 0:HD - ROPE], 1.0)
                pool.memset(wide[:, 1, :, 0:HD - ROPE], 0.0).then_inc(filled, 1)
                with pool.Fori(0, PAIRS) as pair:
                    for s in range(2):
                        pool.wait_ge(multiplied[s], START + pair + 1)
                        pool.wait_ge(scaled[s], START + pair)
                        pool.tensor_tensor(turned[s][:], by_cos[s][:].rearrange("p t h q -> p (t h q)"),
                                           by_sin[s][:].rearrange("p t h q -> p (t h q)"), ALU.add).then_inc(turned_ready[s], 1)

            @block.tensor
            def _(pe):
                pe.wait_ge(widened, 1)
                pe.wait_ge(filled, 1)
                for i in range(2):
                    for t in range(QT):
                        last = pe.transpose(psT[:, i, t, :], wide[:, i, t, :], ident[:])
                last.then_inc(wide_transposed, 1)

                def move(pair, s):
                    pe.wait_ge(multiplied[1 - s], START + pair + s)
                    for ps, matrix in ((psU, ident_r), (psR, swap_r)):
                        for n, o in enumerate((oT_high, oT_low)):
                            for t in range(QT):
                                last = pe.matmul(ps[:, t, :], matrix[:], group(o, pair, s)[:, t, :], start=(n == 0), stop=(n == 1))
                    last.then_inc(moved[s], 1)

                def spread_inverses(pair, s):
                    pe.wait_ge(diag_ready[s], pair + 1)
                    pe.wait_ge(scaled[1 - s], START + pair + s)
                    for t in range(QT):
                        last = pe.matmul(psI[:, t * GQ:(t + 1) * GQ], ones[:],
                                         diag[:, t * GH:(t + 1) * GH, :].rearrange("p h q -> p (h q)"), start=True, stop=True)
                    last.then_inc(spread[s], 1)

                pipeline(pe, PAIRS, [(1, move), (0, spread_inverses)])

            @block.scalar
            def _(act):
                act.wait_ge(wide_transposed, 1)
                act.copy(wideT[:], psT[:]).then_inc(wide_ready, 1)
                with act.Fori(0, PAIRS) as pair:
                    for s in range(2):
                        act.wait_ge(scaled[s], START + pair + 1)
                        act.copy(group(oT_high, pair, s).rearrange("p t n -> p (t n)"), out[s][:]).then_inc(high[s], 1)

            @block.vector
            def _(dve):
                dve.wait_ge(angles_loaded, 32)
                for i in range(2):
                    rotated = wide[:, i, :, HD - ROPE:].rearrange("p t (n two) -> p t n two", two=2)
                    for half in range(2):
                        last = dve.tensor_copy(rotated[:, :, :, half], angle[:, i, :, :])
                last.then_inc(widened, 1)
                dve.wait_ge(wide_ready, 1)

                def place_inverses(pair, s):
                    dve.wait_ge(spread[1 - s], START + pair + s)
                    dve.tensor_tensor(diag[:], broadcast_outer(ident[:], QT * GH), broadcast_inner(
                        inverse[:, bass.ds(pair * 2 + s, 1), :, :].rearrange("p g t h -> p (g t h)"), P), ALU.mult).then_inc(diag_ready[s], 1)

                def multiply(pair, s):
                    dve.wait_ge(moved[s], pair + 1)
                    dve.wait_ge(turned_ready[s], START + pair)
                    for t in range(QT):
                        for i, (ps, dst) in enumerate(((psU, by_cos), (psR, by_sin))):
                            last = dve.tensor_tensor(dst[s][:, t, :, :], ps[:, t, :].rearrange("p (h q) -> p h q", h=GH),
                                                     broadcast_outer(wideT[:, i, t, :], GH), ALU.mult)
                    last.then_inc(multiplied[s], 1)

                def scale(pair, s):
                    dve.wait_ge(turned_ready[s], START + pair + 1)
                    dve.wait_ge(spread[s], START + pair + 1)
                    dve.wait_ge(low[s], START + pair)
                    dve.tensor_tensor(out[s][:], psI[:], turned[s][:], ALU.mult).then_inc(scaled[s], 1)

                def split(pair, s):
                    dve.wait_ge(high[s], pair + 1)
                    dve.tensor_tensor(group(oT_low, pair, s).rearrange("p t n -> p (t n)"), out[s][:],
                                      group(oT_high, pair, s).rearrange("p t n -> p (t n)").bitcast(F32), ALU.subtract).then_inc(low[s], 1)

                pipeline(dve, PAIRS, [(1, multiply), (0, scale), (1, place_inverses), (0, split)])


def grouped_projection(nc, sems, wo_a, ident_bf, oT_high, oT_low, ogT):
    with ExitStack() as stack:
        m = Scope(nc, stack, "gp")
        sem = make_sem(nc, sems, "gp")
        two = lambda name: [sem(f"{name}{s}") for s in range(2)]
        w_raw = [m.sb(f"w_raw{s}", [P, ORT, OHEADS * HD], BF16) for s in range(2)]
        wT = [m.sb(f"wT{s}", [P, OHEADS, ORANK], F32R) for s in range(2)]
        psW = [m.ps(f"psW{s}", [P, OHEADS, ORANK], BF16) for s in range(2)]
        psG = [m.ps(f"psG{s}", [P, ORT, NQ]) for s in range(2)]
        w_loaded, w_transposed, w_ready, projected, copied = map(
            two, ("w_loaded", "w_transposed", "w_ready", "projected", "copied"))
        PAIRS = OGROUPS // 2
        w_v = wo_a.rearrange("(g t p) n -> g p t n", t=ORT, p=P)
        sems.credit(*w_ready, *copied)
        with nc.Block() as block:
            @block.sync
            def _(sp):
                def load(g, s):
                    sp.dma_start(w_raw[s][:], w_v[bass.ds(g, 1), :, :, :].rearrange("g p t n -> p (g t) n")).then_inc(w_loaded[s], 16)

                load(0, 0)
                load(1, 1)
                with sp.Fori(0, PAIRS - 1) as pair:
                    for s in range(2):
                        sp.wait_ge(w_transposed[s], pair + 1)
                        load(pair * 2 + (2 + s), s)

            @block.tensor
            def _(pe):
                with pe.Fori(0, PAIRS) as pair:
                    for s in range(2):
                        pe.wait_ge(w_loaded[s], pair * 16 + 16)
                        pe.wait_ge(w_ready[s], START + pair)
                        for h in range(OHEADS):
                            for r in range(ORT):
                                last = pe.transpose(psW[s][:, h, r * P:(r + 1) * P], w_raw[s][:, r, h * HD:(h + 1) * HD], ident_bf[:])
                        last.then_inc(w_transposed[s], 1)
                    for s in range(2):
                        pe.wait_ge(w_ready[s], START + pair + 1)
                        pe.wait_ge(copied[s], START + pair)
                        for r in range(ORT):
                            for h in range(OHEADS):
                                group = bass.ds(pair * 4 + (s * 2 + h // GH), 1)
                                for n, o in enumerate((oT_high, oT_low)):
                                    last = pe.matmul(psG[s][:, r, :].rearrange("p (t q) -> p t q", t=QT), wT[s][:, h, r * P:(r + 1) * P],
                                                     o[:, group, :, h % GH, :].rearrange("p g t q -> p (g t) q"),
                                                     start=(h == 0 and n == 0), stop=(h == OHEADS - 1 and n == 1))
                        last.then_inc(projected[s], 1)

            @block.scalar
            def _(act):
                with act.Fori(0, PAIRS) as pair:
                    for s in range(2):
                        act.wait_ge(w_transposed[s], pair + 1)
                        act.copy(wT[s][:], psW[s][:]).then_inc(w_ready[s], 1)

            @block.vector
            def _(dve):
                with dve.Fori(0, PAIRS) as pair:
                    for s in range(2):
                        dve.wait_ge(projected[s], pair + 1)
                        dve.tensor_copy(ogT[:, bass.ds(pair * 4 + s * 2, ORT), :], psG[s][:]).then_inc(copied[s], 1)


def output_projection(nc, sems, wo_b, ident_bf, ogT, x1, x2):
    with ExitStack() as stack:
        m = Scope(nc, stack, "op")
        sem = make_sem(nc, sems, "op")
        STEP = 4
        STEPS = OTILES // STEP
        NT = D // P
        w_raw = [m.sb(f"w_raw{s}", [P, NT, STEP * P], BF16) for s in range(2)]
        wT = [m.sb(f"wT{s}", [P, STEP, D], F32R) for s in range(2)]
        ogT_high, ogT_low = (m.sb(f"ogT_{p}", [P, OTILES, NQ], F32R) for p in ("high", "low"))
        x = m.sb("x", [P, QT, D])
        y = m.sb("y", [P, QT, D])
        psW = m.ps("psW", [P, STEP, D], BF16)
        psX = m.ps("psX", [P, QT, D])
        w_loaded = [sem(f"w_loaded{s}") for s in range(2)]
        x_loaded, w_transposed, w_ready, og_high, og_low, projected, added, stored = map(sem, (
            "x_loaded", "w_transposed", "w_ready", "og_high", "og_low", "projected", "added", "stored"))
        w_v = wo_b.rearrange("(t p) r -> p t r", p=P)
        with nc.Block() as block:
            @block.sync
            def _(sp):
                for i in range(STEPS):
                    if i >= 2:
                        sp.wait_ge(w_transposed, i - 1)
                    sp.dma_start(w_raw[i % 2][:], w_v[:, :, i * STEP * P:(i + 1) * STEP * P]).then_inc(w_loaded[i % 2], 16)
                    if i == 1:
                        sp.dma_start(x[:], x1.rearrange("(t p) d -> p t d", p=P)).then_inc(x_loaded, 16)
                sp.wait_ge(added, 1)
                sp.dma_start(x2.rearrange("(t p) d -> p t d", p=P), y[:]).then_inc(stored, 16)
                sp.wait_ge(stored, 16)

            @block.tensor
            def _(pe):
                def transpose(i):
                    pe.wait_ge(w_loaded[i % 2], 16 * (i // 2 + 1))
                    if i:
                        pe.wait_ge(w_ready, i)
                    for r in range(STEP):
                        for n in range(NT):
                            last = pe.transpose(psW[:, r, n * P:(n + 1) * P], w_raw[i % 2][:, n, r * P:(r + 1) * P], ident_bf[:])
                    last.then_inc(w_transposed, 1)

                transpose(0)
                pe.wait_ge(og_low, 1)
                for i in range(STEPS):
                    if i + 1 < STEPS:
                        transpose(i + 1)
                    pe.wait_ge(w_ready, i + 1)
                    for t in range(QT):
                        for r in range(STEP):
                            for n, og in enumerate((ogT_high, ogT_low)):
                                for c in range(D // BANK):
                                    cols = slice(c * BANK, (c + 1) * BANK)
                                    last = pe.matmul(psX[:, t, cols], og[:, i * STEP + r, t * P:(t + 1) * P], wT[i % 2][:, r, cols],
                                                     start=(i == 0 and r == 0 and n == 0), stop=(i == STEPS - 1 and r == STEP - 1 and n == 1))
                    last.then_inc(projected, 1)

            @block.scalar
            def _(act):
                act.copy(ogT_high[:], ogT[:]).then_inc(og_high, 1)
                for i in range(STEPS):
                    act.wait_ge(w_transposed, i + 1)
                    if i >= 2:
                        act.wait_ge(projected, i - 1)
                    act.copy(wT[i % 2][:], psW[:]).then_inc(w_ready, 1)

            @block.vector
            def _(dve):
                dve.wait_ge(og_high, 1)
                dve.tensor_tensor(ogT_low[:], ogT[:], ogT_high[:].bitcast(F32), ALU.subtract).then_inc(og_low, 1)
                dve.wait_ge(x_loaded, 16)
                dve.wait_ge(projected, STEPS)
                dve.tensor_tensor(y[:], psX[:], x[:], ALU.add).then_inc(added, 1)


def gated_linear(nc, sems, x2, weight, bias, centroids, assignments, ident, ones, yT_high, yT_low, out):
    with ExitStack() as stack:
        m = Scope(nc, stack, "gl")
        sem = make_sem(nc, sems, "gl")
        CLUSTERS = 64
        THRESHOLD = 0.01
        INV_TEMPERATURE = 10.0
        NT = D // P
        w_raw = m.sb("w_raw", [P, NT, D])
        w_hi = m.sb("w_hi", [P, KT, D], F32R)
        w_lo = m.sb("w_lo", [P, KT, D], F32R)
        c_raw = m.sb("c_raw", [CLUSTERS, D])
        c_hi = m.sb("c_hi", [P, KT, CLUSTERS], F32R)
        c_lo = m.sb("c_lo", [P, KT, CLUSTERS], F32R)
        x = m.sb("x", [P, QT, D])
        bias_sb = m.sb("bias_sb", [P, D])
        assign = m.sb("assign", [CLUSTERS, D], I32)
        assign_f = m.sb("assign_f", [CLUSTERS, D])
        index = m.sb("index", [CLUSTERS, 1], I32)
        index_f = m.sb("index_f", [CLUSTERS, 1])
        onehot = m.sb("onehot", [CLUSTERS, D])
        peak = m.sb("peak", [P, QT])
        minus_peak = m.sb("minus_peak", [P, QT])
        exps = m.sb("exps", [P, QT, CLUSTERS])
        sums = m.sb("sums", [P, QT])
        inverse = m.sb("inverse", [P, QT])
        hits = m.sb("hits", [P, QT, CLUSTERS])
        row_hit = m.sb("row_hit", [P, QT])
        cluster_hit = m.sb("cluster_hit", [CLUSTERS, P])
        dense = m.sb("dense", [P, QT, D])
        gated = m.sb("gated", [P, QT, D])
        y = m.sb("y", [P, QT, D])
        psW = m.ps("psW", [P, D])
        psY = m.ps("psY", [P, QT, D])
        psL = m.ps("psL", [P, BANK])
        (w_loaded, c_loaded, x_loaded, bias_loaded, assign_loaded, index_made, indices, onehot_made, c_transposed, c_high,
         c_low, logits, peaked, negated, exped, inverted, hit, row_ready, counted, cluster_ready, w_transposed, w_high,
         w_low, projected, selected, biased, gated_ready, done, stored) = map(sem, (
             "w_loaded", "c_loaded", "x_loaded", "bias_loaded", "assign_loaded", "index_made", "indices", "onehot_made",
             "c_transposed", "c_high", "c_low", "logits", "peaked", "negated", "exped", "inverted", "hit", "row_ready",
             "counted", "cluster_ready", "w_transposed", "w_high", "w_low", "projected", "selected", "biased",
             "gated_ready", "done", "stored"))
        cT = psL[:, 0:KT * CLUSTERS].rearrange("p (k c) -> p k c", k=KT)
        logit = psL[:, 0:QT * CLUSTERS].rearrange("p (t c) -> p t c", t=QT)
        with nc.Block() as block:
            @block.sync
            def _(sp):
                sp.dma_start(c_raw[:], centroids).then_inc(c_loaded, 16)
                sp.dma_start(w_raw[:], weight.rearrange("(t p) n -> p t n", p=P)).then_inc(w_loaded, 16)
                sp.dma_start(assign[:], assignments.rearrange("(a n) -> a n", a=1).to_broadcast([CLUSTERS, D])).then_inc(assign_loaded, 16)
                sp.dma_start(bias_sb[:], bias.rearrange("(a n) -> a n", a=1).to_broadcast([P, D])).then_inc(bias_loaded, 16)
                sp.dma_start(x[:], x2.rearrange("(t p) d -> p t d", p=P)).then_inc(x_loaded, 16)
                sp.wait_ge(done, 1)
                sp.dma_start(out.rearrange("(t p) d -> p t d", p=P), y[:]).then_inc(stored, 16)
                sp.wait_ge(stored, 16)

            @block.gpsimd
            def _(pool):
                pool.iota(index[:], pattern=[[0, 1]], base=0, channel_multiplier=1).then_inc(index_made, 1)

            @block.tensor
            def _(pe):
                def transpose_weights(k):
                    if k:
                        pe.wait_ge(w_low, k)
                    for n in range(NT):
                        last = pe.transpose(psW[:, n * P:(n + 1) * P], w_raw[:, n, k * P:(k + 1) * P], ident[:])
                    last.then_inc(w_transposed, 1)

                pe.wait_ge(c_loaded, 16)
                for k in range(KT):
                    last = pe.transpose(cT[:, k, :], c_raw[:, k * P:(k + 1) * P], ident[0:CLUSTERS, 0:CLUSTERS])
                last.then_inc(c_transposed, 1)
                pe.wait_ge(w_loaded, 16)
                transpose_weights(0)
                pe.wait_ge(c_low, 1)
                for t in range(QT):
                    for k in range(KT):
                        rows = slice(t * P, (t + 1) * P)
                        for n, (a, b) in enumerate(((yT_high, c_hi), (yT_high, c_lo), (yT_low, c_hi))):
                            last = pe.matmul(logit[:, t, :], a[:, k, rows], b[:, k, :], start=(k == 0 and n == 0),
                                             stop=(k == KT - 1 and n == 2))
                last.then_inc(logits, 1)
                for k in range(KT):
                    if k + 1 < KT:
                        transpose_weights(k + 1)
                    pe.wait_ge(w_low, k + 1)
                    for t in range(QT):
                        for n, (a, w) in enumerate(((yT_high, w_hi), (yT_high, w_lo), (yT_low, w_hi))):
                            for c in range(D // BANK):
                                cols = slice(c * BANK, (c + 1) * BANK)
                                last = pe.matmul(psY[:, t, cols], a[:, k, t * P:(t + 1) * P], w[:, k, cols],
                                                 start=(k == 0 and n == 0), stop=(k == KT - 1 and n == 2))
                last.then_inc(projected, 1)
                pe.wait_ge(hit, 1)
                for t in range(QT):
                    last = pe.matmul(psL[0:CLUSTERS, 0:P], hits[:, t, :], ones[:], start=(t == 0), stop=(t == QT - 1))
                last.then_inc(counted, 1)
                pe.wait_ge(cluster_ready, 1)
                pe.wait_ge(onehot_made, 1)
                for c in range(D // BANK):
                    cols = slice(c * BANK, (c + 1) * BANK)
                    last = pe.matmul(psW[:, cols], cluster_hit[:], onehot[:, cols], start=True, stop=True)
                last.then_inc(selected, 1)

            @block.scalar
            def _(act):
                act.wait_ge(c_transposed, 1)
                act.copy(c_hi[:], cT).then_inc(c_high, 1)

                def weights(k):
                    act.wait_ge(w_transposed, k + 1)
                    act.copy(w_hi[:, k, :], psW[:]).then_inc(w_high, 1)

                weights(0)
                act.wait_ge(negated, 1)
                for t in range(QT):
                    last = act.activation(exps[:, t, :], logit[:, t, :], ACT.Exp, bias=minus_peak[:, t:t + 1],
                                          scale=INV_TEMPERATURE, accum_out=sums[:, t:t + 1])
                last.then_inc(exped, 1)
                for k in range(1, KT):
                    weights(k)

            @block.vector
            def _(dve):
                dve.wait_ge(c_high, 1)
                dve.tensor_tensor(c_lo[:], cT, c_hi[:].bitcast(F32), ALU.subtract).then_inc(c_low, 1)

                def weights(k):
                    dve.wait_ge(w_high, k + 1)
                    dve.tensor_tensor(w_lo[:, k, :], psW[:], w_hi[:, k, :].bitcast(F32), ALU.subtract).then_inc(w_low, 1)

                weights(0)
                dve.wait_ge(logits, 1)
                dve.tensor_reduce(peak[:], logit, AX.X, ALU.max).then_inc(peaked, 1)
                dve.wait_ge(peaked, 1)
                dve.tensor_scalar(minus_peak[:], peak[:], -INV_TEMPERATURE, None, ALU.mult).then_inc(negated, 1)
                weights(1)
                dve.wait_ge(exped, 1)
                dve.reciprocal(inverse[:], sums[:]).then_inc(inverted, 1)
                dve.wait_ge(inverted, 1)
                for t in range(QT):
                    last = dve.tensor_scalar(hits[:, t, :], exps[:, t, :], inverse[:, t:t + 1], THRESHOLD, ALU.mult, ALU.is_gt)
                last.then_inc(hit, 1)
                dve.wait_ge(hit, 1)
                dve.tensor_reduce(row_hit[:], hits[:], AX.X, ALU.max).then_inc(row_ready, 1)
                for k in range(2, KT):
                    weights(k)
                dve.wait_ge(assign_loaded, 16)
                dve.wait_ge(index_made, 1)
                dve.tensor_copy(index_f[:], index[:])
                dve.tensor_copy(assign_f[:], assign[:]).then_inc(indices, 1)
                dve.wait_ge(indices, 1)
                dve.tensor_scalar(onehot[:], assign_f[:], index_f[:, 0:1], None, ALU.is_equal).then_inc(onehot_made, 1)
                dve.wait_ge(counted, 1)
                dve.tensor_scalar(cluster_hit[:], psL[0:CLUSTERS, 0:P], 0.5, None, ALU.is_gt).then_inc(cluster_ready, 1)
                dve.wait_ge(bias_loaded, 16)
                dve.wait_ge(projected, 1)
                dve.tensor_tensor(dense[:], psY[:], broadcast_outer(bias_sb[:], QT), ALU.add).then_inc(biased, 1)
                dve.wait_ge(biased, 1)
                dve.wait_ge(row_ready, 1)
                dve.wait_ge(selected, 1)
                for t in range(QT):
                    last = dve.scalar_tensor_tensor(gated[:, t, :], dense[:, t, :], row_hit[:, t:t + 1], psW[:], ALU.mult, ALU.mult)
                last.then_inc(gated_ready, 1)
                dve.wait_ge(gated_ready, 1)
                dve.wait_ge(x_loaded, 16)
                dve.tensor_tensor(y[:], gated[:], x[:], ALU.add).then_inc(done, 1)


def self_constants(nc, sems, ident, ones, ident_r, ones_r, swap_r, triangle_qk, triangle_kq):
    with ExitStack() as stack:
        m = Scope(nc, stack, "sc")
        sem = make_sem(nc, sems, "sc")
        swap = m.sb("swap", [P, P])
        qk = m.sb("qk", [P, 2 * P])
        kq = m.sb("kq", [P, P])
        cleared, made = sem("cleared"), sem("made")
        with nc.Block() as block:
            @block.gpsimd
            def _(pool):
                pool.memset(swap[:], 0.0)
                pool.memset(qk[:], 0.0)
                pool.memset(kq[:], 0.0).then_inc(cleared, 1)
                pool.wait_ge(cleared, 1)
                pairs = swap[:].rearrange("p (i two) -> p i two", two=2)
                pool.affine_select(out=pairs[:, :, 0], in_=pairs[:, :, 0], compare_op=ALU.not_equal, fill=1.0, base=-1,
                                   pattern=[[-2, P // 2]], channel_multiplier=1)
                pool.affine_select(out=pairs[:, :, 1], in_=pairs[:, :, 1], compare_op=ALU.not_equal, fill=-1.0, base=0,
                                   pattern=[[-2, P // 2]], channel_multiplier=1)
                pool.affine_select(out=qk[:, P:2 * P], in_=qk[:, P:2 * P], compare_op=ALU.is_ge, fill=MASKED, base=0,
                                   pattern=[[-1, P]], channel_multiplier=1)
                pool.affine_select(out=kq[:], in_=kq[:], compare_op=ALU.is_ge, fill=MASKED, base=0,
                                   pattern=[[1, P]], channel_multiplier=-1).then_inc(made, 1)

            @block.vector
            def _(dve):
                dve.tensor_copy(ident_r[:], ident[:])
                dve.tensor_copy(ones_r[:], ones[:])
                dve.wait_ge(made, 1)
                dve.tensor_copy(swap_r[:], swap[:])
                dve.tensor_copy(triangle_qk[:], qk[:])
                dve.tensor_copy(triangle_kq[:], kq[:])


def perceiver_kernel(nc, x, context, Wq, Wk, Wv, Wo, xq_norm_w, xk_norm_w, wq_a, q_norm_w, wq_b, wkv, kv_norm_w, wo_a,
                     wo_b, sink, cos, sin, weight, bias, centroids, assignments, out):
    def scratch(name, shape):
        return nc.dram_tensor(name, shape, F32, kind="Internal").ap()

    keyT_high, keyT_low = (scratch(f"keyT_{p}", [XKV, HD, NK]) for p in ("high", "low"))
    val_high, val_low = (scratch(f"val_{p}", [XKV, P, RT, HD]) for p in ("high", "low"))
    xqT_high, xqT_low = (scratch(f"xqT_{p}", [XKV, HD, XQ]) for p in ("high", "low"))
    xoT_high, xoT_low = (scratch(f"xoT_{p}", [XKV, HD, XQ]) for p in ("high", "low"))
    x1, x2 = scratch("x1", [NQ, D]), scratch("x2", [NQ, D])
    x, context, out = x[0], context[0], out[0]

    sems = Semaphores(nc)
    with ExitStack() as whole:
        top = Scope(nc, whole, "top")
        ident = top.sb("ident", [P, P])
        ident_bf = top.sb("ident_bf", [P, P], BF16)
        ones = top.sb("ones", [P, P])
        constants(nc, sems, ident, ident_bf, ones)

        with ExitStack() as stack:
            m = Scope(nc, stack, "cross")
            yT_high, yT_low = (m.sb(f"yT_{p}", [P, KT, NQ], F32R) for p in ("high", "low"))
            layernorm_transposed(nc, sems, "ln0", x, ident, yT_high, yT_low)
            project_keys_values(nc, sems, context, Wk, Wv, ident, yT_high, yT_low, keyT_high, keyT_low, val_high, val_low)
            project_queries(nc, sems, Wq, xq_norm_w, xk_norm_w, ident, yT_high, yT_low, xqT_high, xqT_low)
        cross_attention(nc, sems, ident, ones, keyT_high, keyT_low, val_high, val_low, xqT_high, xqT_low, xoT_high, xoT_low)
        cross_output(nc, sems, Wo, xoT_high, xoT_low, x, x1)
        sems.release()

        with ExitStack() as stack:
            m = Scope(nc, stack, "self")
            ident_r, ones_r, swap_r, triangle_kq = (m.sb(n, [P, P], F32R) for n in ("ident_r", "ones_r", "swap_r", "triangle_kq"))
            triangle_qk = m.sb("triangle_qk", [P, 2 * P], F32R)
            self_constants(nc, sems, ident, ones, ident_r, ones_r, swap_r, triangle_qk, triangle_kq)
            qrT_high, qrT_low = (m.sb(f"qrT_{p}", [P, LT, NQ], F32R) for p in ("high", "low"))
            kv_high, kv_low = (m.sb(f"kv_{p}", [P, QT, HD], F32R) for p in ("high", "low"))
            kvT_high, kvT_low = (m.sb(f"kvT_{p}", [P, NQ], F32R) for p in ("high", "low"))
            query_max = m.sb("query_max", [P, SG, QT, GH], F32R)
            sink_exp = m.sb("sink_exp", [P, SG, QT, GH])
            inverse = m.sb("inverse", [P, SG, QT, GH])
            with ExitStack() as inner:
                i = Scope(nc, inner, "latent")
                yT_high, yT_low = (i.sb(f"yT_{p}", [P, KT, NQ], F32R) for p in ("high", "low"))
                layernorm_transposed(nc, sems, "ln1", x1, ident, yT_high, yT_low)
                latent_projections(nc, sems, wq_a, wkv, q_norm_w, kv_norm_w, cos, sin, ident, ident_bf, yT_high, yT_low,
                                   qrT_high, qrT_low, kv_high, kv_low, kvT_high, kvT_low)
            ogT = m.sb("ogT", [P, OTILES, NQ])
            with ExitStack() as inner:
                i = Scope(nc, inner, "heads")
                qT_high, qT_low = (i.sb(f"qT_{p}", [P, SG, QT, GH, P], F32R) for p in ("high", "low"))
                self_queries(nc, sems, wq_b, cos, sin, ident, ident_bf, qrT_high, qrT_low, qT_high, qT_low)
                self_maxima(nc, sems, sink, ident, kvT_high, qT_high, triangle_qk, ident_r, query_max, sink_exp)
                self_attention(nc, sems, ident, ones, ident_r, ones_r, triangle_kq, kv_high, kv_low, kvT_high, kvT_low,
                               query_max, sink_exp, qT_high, qT_low, inverse)
                rotate_outputs(nc, sems, cos, sin, ident, ones, ident_r, swap_r, qT_high, qT_low, inverse)
                grouped_projection(nc, sems, wo_a, ident_bf, qT_high, qT_low, ogT)
            output_projection(nc, sems, wo_b, ident_bf, ogT, x1, x2)
        sems.release()

        with ExitStack() as stack:
            m = Scope(nc, stack, "linear")
            yT_high, yT_low = (m.sb(f"yT_{p}", [P, KT, NQ], F32R) for p in ("high", "low"))
            layernorm_transposed(nc, sems, "ln2", x2, ident, yT_high, yT_low)
            gated_linear(nc, sems, x2, weight, bias, centroids, assignments, ident, ones, yT_high, yT_low, out)


_INS = ['x', 'ctx_4096', 'L0_xattn_Wq', 'L0_xattn_Wk', 'L0_xattn_Wv', 'L0_xattn_Wo', 'L0_xattn_q_norm_w', 'L0_xattn_k_norm_w',
        'L0_attn_wq_a', 'L0_attn_q_norm_w', 'L0_attn_wq_b', 'L0_attn_wkv', 'L0_attn_kv_norm_w', 'L0_attn_wo_a', 'L0_attn_wo_b',
        'L0_attn_attn_sink', 'L0_attn_cos', 'L0_attn_sin', 'L0_ffn_weight', 'L0_ffn_bias', 'L0_ffn_centroids', 'L0_ffn_assignments']


def kernel(**inputs):
    import numpy as _np
    import concourse.bacc as _bacc
    from concourse import mybir as _mybir
    from concourse.bass_utils import run_bass_kernel_spmd as _run

    nc = _bacc.Bacc("TRN2", target_bir_lowering=False, num_devices=1)
    arrays, args = {}, []
    for name in _INS:
        a = _np.ascontiguousarray(inputs[name])
        arrays[f"in_{name}_dram"] = a
        args.append(nc.dram_tensor(f"in_{name}_dram", a.shape, _mybir.dt.from_np(a.dtype), kind="ExternalInput").ap())
    args.append(nc.dram_tensor("out_dram", (1, NQ, D), F32, kind="ExternalOutput").ap())
    perceiver_kernel(nc, *args)
    return _run(nc, [arrays], core_ids=[0]).results[0]["out_dram"]
```

```python
from contextlib import ExitStack

import concourse.bass as bass
from concourse import mybir

F32 = mybir.dt.float32
F32R = mybir.dt.float32r
BF16 = mybir.dt.bfloat16
I32 = mybir.dt.int32
ALU = mybir.AluOpType
ACT = mybir.ActivationFunctionType
AX = mybir.AxisListType

P = 128
BANK = 512

D = 1024
KT = D // P
NQ = 256
QT = NQ // P
NCTX = 4096
NK = NCTX + NQ
HD = 128

XH = 32
XKV = 8
XG = XH // XKV
XQ = XG * NQ
XQT = XQ // P
RT = NK // P
CT = NCTX // P
HALF = RT // 2

LN_EPS = 1e-5
RMS_EPS = 1e-6
SCALE = float(HD) ** -0.5


START = 1


class Scope:

    def __init__(self, nc, stack, tag):
        self.nc, self.stack, self.tag = nc, stack, tag

    def sb(self, name, shape, dt=F32):
        return self.stack.enter_context(self.nc.sbuf_tensor(f"{self.tag}_{name}", shape, dt))

    def ps(self, name, shape, dt=F32):
        return self.stack.enter_context(self.nc.psum_tensor(f"{self.tag}_{name}", shape, dt))


class Semaphores:

    def __init__(self, nc):
        self.nc, self.handles = nc, []

    def new(self, name):
        self.handles.append(self.nc.alloc_semaphore(name=name))
        return self.handles[-1]

    def credit(self, *handles):
        for handle in handles:
            self.nc.gpsimd.sem_inc(handle, START)

    def release(self):
        self.nc.clear_and_free_semaphores(self.handles)
        self.handles = []
        self.nc.all_engine_barrier()


def make_sem(nc, sems, tag):
    return lambda name: sems.new(f"{tag}_{name}")


def pipeline(eng, pairs, stages):
    groups, far = 2 * pairs, max(lead for lead, _ in stages)
    full = (groups - far) // 2

    def written_out(steps):
        for g in steps:
            for lead, stage in stages:
                if 0 <= g + lead < groups:
                    stage((g + lead) // 2, (g + lead) % 2)

    written_out(range(-far, 0))
    with eng.Fori(0, full) as pair:
        for s in range(2):
            for lead, stage in stages:
                stage(pair + (s + lead) // 2, (s + lead) % 2)
    written_out(range(2 * full, groups))


def broadcast_inner(ap, n):
    return ap.unsqueeze(2).to_broadcast([ap.shape[0], ap.shape[1], n])


def broadcast_outer(ap, n):
    return ap.unsqueeze(1).to_broadcast([ap.shape[0], n, ap.shape[1]])


def constants(nc, sems, ident, ident_bf, ones):
    sem = make_sem(nc, sems, "const")
    cleared, made = sem("cleared"), sem("made")
    with nc.Block() as block:
        @block.gpsimd
        def _(pool):
            pool.memset(ones[:], 1.0)
            pool.memset(ident[:], 0.0).then_inc(cleared, 1)
            pool.wait_ge(cleared, 1)
            pool.affine_select(out=ident[:], in_=ident[:], compare_op=ALU.not_equal, fill=1.0, base=0,
                               pattern=[[-1, P]], channel_multiplier=1).then_inc(made, 1)

        @block.vector
        def _(dve):
            dve.wait_ge(made, 1)
            dve.tensor_copy(ident_bf[:], ident[:])


def layernorm_transposed(nc, sems, tag, x, ident, yT_high, yT_low, rows=None, meanwhile=lambda sp: None):
    with ExitStack() as stack:
        m = Scope(nc, stack, tag)
        sem = make_sem(nc, sems, tag)
        y = m.sb("y", [P, QT, D])
        stats = m.sb("stats", [P, QT, 2, 6])
        mean_var = m.sb("mean_var", [P, QT, 2])
        var_eps = m.sb("var_eps", [P, QT])
        rstd = m.sb("rstd", [P, QT])
        power = m.sb("power", [P, QT])
        psT = m.ps("psT", [P, KT, NQ])
        loaded, half_stats, aggregated, eps_added, rstd_ready, normed, transposed, high, power_set = map(sem, (
            "loaded", "half_stats", "aggregated", "eps_added", "rstd_ready", "normed", "transposed", "high", "power_set"))
        with nc.Block() as block:
            @block.sync
            def _(sp):
                if rows is not None:
                    sp.dma_start(x[:], rows.rearrange("(t p) d -> p t d", p=P)).then_inc(loaded, 16)
                meanwhile(sp)

            @block.vector
            def _(dve):
                if rows is not None:
                    dve.wait_ge(loaded, 16)
                for t in range(QT):
                    for c in range(2):
                        last = dve.bn_stats(stats[:, t, c, :], x[:, t, c * 512:(c + 1) * 512])
                last.then_inc(half_stats, 1)
                dve.wait_ge(half_stats, 1)
                for t in range(QT):
                    last = dve.bn_aggr(mean_var[:, t, :], stats[:, t, :, :].rearrange("p a b -> p (a b)"))
                last.then_inc(aggregated, 1)
                dve.wait_ge(rstd_ready, 1)
                for t in range(QT):
                    last = dve.tensor_scalar(y[:, t, :], x[:, t, :], mean_var[:, t, 0:1], rstd[:, t:t + 1],
                                             ALU.subtract, ALU.mult)
                last.then_inc(normed, 1)
                dve.wait_ge(high, 1)
                dve.tensor_tensor(yT_low[:], psT[:], yT_high[:].bitcast(F32), ALU.subtract)

            @block.gpsimd
            def _(pool):
                pool.memset(power[:], -0.5).then_inc(power_set, 1)
                pool.wait_ge(aggregated, 1)
                pool.tensor_scalar(var_eps[:], mean_var[:, :, 1], 1.0, LN_EPS, ALU.mult, ALU.add).then_inc(eps_added, 1)
                pool.wait_ge(power_set, 1)
                pool.wait_ge(eps_added, 1)
                pool.tensor_tensor(rstd[:], var_eps[:], power[:], ALU.pow).then_inc(rstd_ready, 1)

            @block.tensor
            def _(pe):
                pe.wait_ge(normed, 1)
                for t in range(QT):
                    for k in range(KT):
                        last = pe.transpose(psT[:, k, t * P:(t + 1) * P], y[:, t, k * P:(k + 1) * P], ident[:])
                last.then_inc(transposed, 1)

            @block.scalar
            def _(act):
                act.wait_ge(transposed, 1)
                act.copy(yT_high[:], psT[:]).then_inc(high, 1)


class QueryWeights:
    GC = XG * HD

    def __init__(self, nc, sems, m, Wq):
        sem = make_sem(nc, sems, "qw")
        self.Wq = Wq.rearrange("(k p) n -> p k n", p=P)
        self.raw = [m.sb(f"w_raw{s}", [P, KT, self.GC]) for s in range(2)]
        self.loaded = [sem(f"loaded{s}") for s in range(2)]

    def load(self, sp, group, s):
        sp.dma_start(self.raw[s][:], self.Wq[:, :, bass.ds(group * self.GC, self.GC)]).then_inc(self.loaded[s], 16)


def project_queries(nc, sems, weights, q_norm_w, k_norm_w, ident, yT_high, yT_low, qT_high, qT_low, prefetch):
    with ExitStack() as stack:
        m = Scope(nc, stack, "q")
        sem = make_sem(nc, sems, "q")
        GC, w_raw, w_loaded = weights.GC, weights.raw, weights.loaded
        w_hi = [m.sb(f"w_hi{s}", [P, KT, GC], F32R) for s in range(2)]
        w_lo = [m.sb(f"w_lo{s}", [P, KT, GC], F32R) for s in range(2)]
        q = [m.sb(f"q{s}", [P, QT * XG, HD]) for s in range(2)]
        q_hi = [m.sb(f"q_hi{s}", [P, XQ], F32R) for s in range(2)]
        q_lo = [m.sb(f"q_lo{s}", [P, XQ], F32R) for s in range(2)]
        squares = [m.sb(f"squares{s}", [P, QT * XG]) for s in range(2)]
        var = [m.sb(f"var{s}", [P, QT * XG]) for s in range(2)]
        rstd = [m.sb(f"rstd{s}", [P, QT * XG]) for s in range(2)]
        power = m.sb("power", [P, QT * XG])
        norm_w = m.sb("norm_w", [P, 2])
        weight = m.sb("weight", [P, 1])
        psQ = [m.ps(f"psQ{s}", [P, QT * XG, HD]) for s in range(2)]
        psT = [m.ps(f"psT{s}", [P, XG, QT, P]) for s in range(2)]
        (norm_loaded, weight_ready, power_set) = map(sem, ("norm_loaded", "weight_ready", "power_set"))
        two = lambda name: [sem(f"{name}{s}") for s in range(2)]
        w_high, w_low, projected, squared, var_ready, rstd_ready, scaled, transposed, high, low, stored = map(
            two, ("w_high", "w_low", "projected", "squared", "var_ready", "rstd_ready", "scaled",
                  "transposed", "high", "low", "stored"))
        PAIRS = XKV // 2

        sems.credit(*w_low, *projected, *var_ready, *low, *stored, *scaled)
        with nc.Block() as block:
            @block.sync
            def _(sp):
                def load(pair, s):
                    if isinstance(pair, int) and pair == 0:
                        return
                    sp.wait_ge(w_low[s], START + pair)
                    weights.load(sp, pair * 2 + s, s)

                def store(pair, s):
                    sp.wait_ge(low[s], START + pair + 1)
                    for src, dst in ((q_hi, qT_high), (q_lo, qT_low)):
                        sp.dma_start(dst[bass.ds(pair * 2 + s, 1), :, :].rearrange("e d q -> d (e q)"),
                                     src[s][:].bitcast(F32)).then_inc(stored[s], 16)

                sp.dma_start(norm_w[:, 0:1], q_norm_w.rearrange("(d a) -> d a", a=1)).then_inc(norm_loaded, 16)
                sp.dma_start(norm_w[:, 1:2], k_norm_w.rearrange("(d a) -> d a", a=1)).then_inc(norm_loaded, 16)
                prefetch(sp)
                pipeline(sp, PAIRS, [(3, load), (0, store)])
                for s in range(2):
                    sp.wait_ge(stored[s], START + 32 * PAIRS)

            @block.scalar
            def _(act):
                def split_weights(pair, s):
                    act.wait_ge(w_loaded[s], pair * 16 + 16)
                    act.wait_ge(projected[s], START + pair)
                    act.copy(w_hi[s][:], w_raw[s][:]).then_inc(w_high[s], 1)

                def square(pair, s):
                    act.wait_ge(projected[s], START + pair + 1)
                    act.wait_ge(var_ready[s], START + pair)
                    act.wait_ge(low[s], START + pair)
                    for g in range(QT * XG):
                        last = act.activation(psT[s][:, g % XG, g // XG, :], psQ[s][:, g, :], ACT.Square,
                                              accum_out=squares[s][:, g:g + 1])
                    last.then_inc(squared[s], 1)

                def split(pair, s):
                    act.wait_ge(transposed[s], pair + 1)
                    act.wait_ge(stored[s], START + pair * 32)
                    act.activation(q_hi[s][:], psT[s][:].rearrange("p g t q -> p (g t q)"), ACT.Copy,
                                   scale=weight[:, 0:1]).then_inc(high[s], 1)

                act.wait_ge(weight_ready, 1)
                pipeline(act, PAIRS, [(0, square), (2, split_weights), (0, split)])

            @block.vector
            def _(dve):
                def split_weights(pair, s):
                    dve.wait_ge(w_high[s], pair + 1)
                    dve.tensor_tensor(w_lo[s][:], w_raw[s][:], w_hi[s][:].bitcast(F32), ALU.subtract).then_inc(w_low[s], 1)

                def normalise(pair, s):
                    dve.wait_ge(squared[s], pair + 1)
                    dve.tensor_scalar(var[s][:], squares[s][:], 1.0 / HD, RMS_EPS, ALU.mult, ALU.add).then_inc(var_ready[s], 1)
                    dve.wait_ge(rstd_ready[s], pair + 1)
                    dve.tensor_tensor(q[s][:], psQ[s][:], broadcast_inner(rstd[s][:], HD), ALU.mult).then_inc(scaled[s], 1)

                def split(pair, s):
                    dve.wait_ge(high[s], pair + 1)
                    dve.scalar_tensor_tensor(q_lo[s][:], psT[s][:].rearrange("p g t q -> p (g t q)"), weight[:, 0:1],
                                             q_hi[s][:].bitcast(F32), ALU.mult, ALU.subtract).then_inc(low[s], 1)

                dve.wait_ge(norm_loaded, 32)
                dve.scalar_tensor_tensor(weight[:], norm_w[:, 0:1], SCALE, norm_w[:, 1:2], ALU.mult, ALU.mult).then_inc(weight_ready, 1)
                dve.wait_ge(weight_ready, 1)
                pipeline(dve, PAIRS, [(0, normalise), (2, split_weights), (0, split)])

            @block.gpsimd
            def _(pool):
                def root(pair, s):
                    pool.wait_ge(var_ready[s], START + pair + 1)
                    pool.tensor_tensor(rstd[s][:], var[s][:], power[:], ALU.pow).then_inc(rstd_ready[s], 1)

                pool.memset(power[:], -0.5).then_inc(power_set, 1)
                pool.wait_ge(power_set, 1)
                pipeline(pool, PAIRS, [(0, root)])

            @block.tensor
            def _(pe):
                def project(pair, s):
                    pe.wait_ge(w_low[s], START + pair + 1)
                    pe.wait_ge(scaled[s], START + pair)
                    for t in range(QT):
                        rows = slice(t * P, (t + 1) * P)
                        for k in range(KT):
                            for n, (y, w) in enumerate(((yT_high, w_hi), (yT_high, w_lo), (yT_low, w_hi))):
                                last = pe.matmul(psQ[s][:, t * XG:(t + 1) * XG, :].rearrange("p g d -> p (g d)"),
                                                 y[:, k, rows], w[s][:, k, :],
                                                 start=(k == 0 and n == 0), stop=(k == KT - 1 and n == 2))
                    last.then_inc(projected[s], 1)

                def transpose(pair, s):
                    pe.wait_ge(scaled[s], START + pair + 1)
                    for t in range(QT):
                        for g in range(XG):
                            last = pe.transpose(psT[s][:, g, t, :], q[s][:, t * XG + g, :], ident[:])
                    last.then_inc(transposed[s], 1)

                pipeline(pe, PAIRS, [(1, project), (0, transpose)])


class KeyValueWeights:

    def __init__(self, nc, sems, m, Wk, Wv):
        sem = make_sem(nc, sems, "kvw")
        self.W = Wk, Wv
        self.chunks = [(c, k) for c in range(2) for k in range(KT)]
        self.buffers = [m.sb(f"part{i}", [P, D], F32R) for i in range(8)]
        self.loaded = [sem(f"loaded{i}") for i in range(len(self.buffers))]

    def load(self, sp, i):
        c, k = self.chunks[i]
        b = i % len(self.buffers)
        sp.dma_start(self.buffers[b][:].bitcast(F32), self.W[c][k * P:(k + 1) * P, :]).then_inc(self.loaded[b], 16)

    def load_first(self, sp):
        for i in range(len(self.buffers)):
            self.load(sp, i)

    def raw(self, eng, i):
        b = i % len(self.buffers)
        eng.wait_ge(self.loaded[b], 16 * (i // len(self.buffers) + 1))
        return self.buffers[b][:].bitcast(F32)


def project_keys_values(nc, sems, context, weights, ident, yT_high, yT_low, keyT_high, keyT_low, val_high, val_low):
    with ExitStack() as stack:
        m = Scope(nc, stack, "kv")
        sem = make_sem(nc, sems, "kv")
        row = [m.sb(f"row{s}", [P, D]) for s in range(2)]
        xT_high = [m.sb(f"xT_high{s}", [P, KT, P], F32R) for s in range(2)]
        xT_low = [m.sb(f"xT_low{s}", [P, KT, P], F32R) for s in range(2)]
        W_high = m.sb("W_high", [P, KT, 2 * D], F32R)
        W_low = m.sb("W_low", [P, KT, 2 * D], F32R)
        key = m.sb("key", [P, D])
        v_hi, v_lo = weights.buffers[0:2], weights.buffers[2:4]
        kT_hi, kT_lo = ([b[:].rearrange("p (e n) -> p e n", e=XKV) for b in weights.buffers[i:i + 2]] for i in (4, 6))
        squares = m.sb("squares", [P, XKV])
        var = m.sb("var", [P, XKV])
        rstd = m.sb("rstd", [P, XKV])
        power = m.sb("power", [P, XKV])
        psX = m.ps("psX", [P, KT, P])
        psK = m.ps("psK", [P, D])
        psV = m.ps("psV", [P, D])
        psT = m.ps("psT", [P, XKV, P])

        row_loaded = [sem(f"row_loaded{s}") for s in range(2)]
        (w_high, w_low, x_transposed, x_high, x_low, k_projected, k_squared, k_var, k_rstd, k_scaled, v_projected,
         v_high, v_lowed, k_transposed, k_high, k_lowed, power_set) = map(sem, (
            "w_high", "w_low", "x_transposed", "x_high", "x_low", "k_projected", "k_squared", "k_var", "k_rstd",
            "k_scaled", "v_projected", "v_high", "v_lowed", "k_transposed", "k_high", "k_lowed", "power_set"))
        v_stored = [sem(f"v_stored{s}") for s in range(2)]
        k_stored = [sem(f"k_stored{s}") for s in range(2)]

        CHUNKS = weights.chunks

        def columns(W, i):
            c, k = CHUNKS[i]
            return W[:, k, c * D:(c + 1) * D]

        PAIRS = CT // 2

        def tiles(eng, step, peeled=0):
            for r in range(2 * peeled):
                step(r, r // 2, r % 2, True)
            with eng.Fori(peeled, PAIRS - 1) as pair:
                step(pair * 2, pair, 0, True)
                step(pair * 2 + 1, pair, 1, True)
            for r in range(CT - 2, RT):
                step(r, r // 2, r % 2, r + 1 < CT)

        sems.credit(k_lowed, k_var, *v_stored, *k_stored, k_transposed, k_scaled, v_lowed, x_low)
        with nc.Block() as block:
            @block.sync
            def _(sp):
                for r in range(2):
                    sp.dma_start(row[r][:], context[r * P:(r + 1) * P, :]).then_inc(row_loaded[r], 16)
                first = len(weights.buffers)
                for i in range(first, len(CHUNKS)):
                    sp.wait_ge(w_low, i - first + 1)
                    weights.load(sp, i)

                def step(r, pair, s, load):
                    if load:
                        sp.wait_ge(x_transposed, r + 1)
                        sp.dma_start(row[s][:], context[bass.ds((r + 2) * P, P), :]).then_inc(row_loaded[s], 16)
                    sp.wait_ge(v_lowed, START + r + 1)
                    for src, dst in ((v_hi, val_high), (v_lo, val_low)):
                        sp.dma_start(dst[:, :, bass.ds(r, 1), :].rearrange("e p t d -> p (e t) d"),
                                     src[s][:].bitcast(F32).rearrange("p (e d) -> p e d", e=XKV)).then_inc(v_stored[s], 16)
                    sp.wait_ge(k_lowed, START + r + 1)
                    for src, dst in ((kT_hi, keyT_high), (kT_lo, keyT_low)):
                        sp.dma_start(dst[:, :, bass.ds(r * P, P)].rearrange("e d k -> d e k"),
                                     src[s][:].bitcast(F32)).then_inc(k_stored[s], 16)

                with sp.Fori(0, PAIRS - 1) as pair:
                    step(pair * 2, pair, 0, True)
                    step(pair * 2 + 1, pair, 1, True)
                for r in range(CT - 2, RT):
                    step(r, r // 2, r % 2, False)
                for s in range(2):
                    sp.wait_ge(v_stored[s], START + 32 * (RT // 2))
                    sp.wait_ge(k_stored[s], START + 32 * (RT // 2))

            @block.scalar
            def _(act):
                def rows_high(r, s):
                    act.wait_ge(x_transposed, r + 1)
                    act.copy(xT_high[s][:], psX[:]).then_inc(x_high, 1)

                def step(r, pair, s, has_next):
                    act.wait_ge(k_projected, r + 1)
                    act.wait_ge(k_lowed, START + r)
                    act.wait_ge(k_var, START + r)
                    for e in range(XKV):
                        last = act.activation(psT[:, e, :], psK[:, e * HD:(e + 1) * HD], ACT.Square,
                                              accum_out=squares[:, e:e + 1])
                    last.then_inc(k_squared, 1)
                    if has_next:
                        rows_high(r + 1, 1 - s)
                    act.wait_ge(v_projected, r + 1)
                    act.wait_ge(v_stored[s], START + 32 * pair)
                    act.copy(v_hi[s][:], psV[:]).then_inc(v_high, 1)
                    act.wait_ge(k_transposed, START + r + 1)
                    act.wait_ge(k_stored[s], START + 32 * pair)
                    act.copy(kT_hi[s][:], psT[:]).then_inc(k_high, 1)

                rows_high(0, 0)
                for i in range(len(CHUNKS)):
                    act.copy(columns(W_high, i), weights.raw(act, i)).then_inc(w_high, 1)
                tiles(act, step)

            @block.vector
            def _(dve):
                def rows_low(r, s):
                    dve.wait_ge(x_high, r + 1)
                    dve.tensor_tensor(xT_low[s][:], psX[:], xT_high[s][:].bitcast(F32), ALU.subtract).then_inc(x_low, 1)

                def step(r, pair, s, has_next):
                    dve.wait_ge(k_squared, r + 1)
                    dve.tensor_scalar(var[:], squares[:], 1.0 / HD, RMS_EPS, ALU.mult, ALU.add).then_inc(k_var, 1)
                    dve.wait_ge(k_rstd, r + 1)
                    dve.wait_ge(k_transposed, START + r)
                    dve.tensor_tensor(key[:].rearrange("p (e d) -> p e d", e=XKV),
                                      psK[:].rearrange("p (e d) -> p e d", e=XKV),
                                      broadcast_inner(rstd[:], HD), ALU.mult).then_inc(k_scaled, 1)
                    if has_next:
                        rows_low(r + 1, 1 - s)
                    dve.wait_ge(v_high, r + 1)
                    dve.tensor_tensor(v_lo[s][:], psV[:], v_hi[s][:].bitcast(F32), ALU.subtract).then_inc(v_lowed, 1)
                    dve.wait_ge(k_high, r + 1)
                    dve.tensor_tensor(kT_lo[s][:], psT[:], kT_hi[s][:].bitcast(F32), ALU.subtract).then_inc(k_lowed, 1)

                rows_low(0, 0)
                for i in range(len(CHUNKS)):
                    dve.wait_ge(w_high, i + 1)
                    dve.tensor_tensor(columns(W_low, i), weights.raw(dve, i), columns(W_high, i).bitcast(F32),
                                      ALU.subtract).then_inc(w_low, 1)
                tiles(dve, step)

            @block.gpsimd
            def _(pool):
                pool.memset(power[:], -0.5).then_inc(power_set, 1)
                pool.wait_ge(power_set, 1)

                def step(r, pair, s, has_next):
                    pool.wait_ge(k_var, START + r + 1)
                    pool.tensor_tensor(rstd[:], var[:], power[:], ALU.pow).then_inc(k_rstd, 1)

                tiles(pool, step)

            @block.tensor
            def _(pe):
                def transpose_rows(r, pair, s):
                    pe.wait_ge(row_loaded[s], pair * 16 + 16)
                    pe.wait_ge(x_low, START + r)
                    for k in range(KT):
                        last = pe.transpose(psX[:, k, :], row[s][:, k * P:(k + 1) * P], ident[:])
                    last.then_inc(x_transposed, 1)

                def project(ps, x_hi, x_lo, first, wait):
                    for k in range(KT):
                        if wait:
                            pe.wait_ge(w_low, CHUNKS.index((first // D, k)) + 1)
                        for n, (x, W) in enumerate(((x_hi, W_high), (x_hi, W_low), (x_lo, W_high))):
                            for c in range(D // BANK):
                                last = pe.matmul(ps[:, c * BANK:(c + 1) * BANK], x(k),
                                                 W[:, k, first + c * BANK:first + (c + 1) * BANK],
                                                 start=(k == 0 and n == 0), stop=(k == KT - 1 and n == 2))
                    return last

                def step(r, pair, s, has_next):
                    if isinstance(r, int) and r >= CT:
                        t = slice((r - CT) * P, (r - CT + 1) * P)
                        x_hi, x_lo = (lambda k: yT_high[:, k, t]), (lambda k: yT_low[:, k, t])
                    else:
                        x_hi, x_lo = (lambda k: xT_high[s][:, k, :]), (lambda k: xT_low[s][:, k, :])
                        pe.wait_ge(x_low, START + r + 1)
                    pe.wait_ge(k_scaled, START + r)
                    project(psK, x_hi, x_lo, 0, isinstance(r, int) and r == 0).then_inc(k_projected, 1)
                    if has_next:
                        transpose_rows(r + 1, pair + s, 1 - s)
                    pe.wait_ge(v_lowed, START + r)
                    project(psV, x_hi, x_lo, D, isinstance(r, int) and r == 0).then_inc(v_projected, 1)
                    pe.wait_ge(k_scaled, START + r + 1)
                    for e in range(XKV):
                        last = pe.transpose(psT[:, e, :], key[:, e * HD:(e + 1) * HD], ident[:])
                    last.then_inc(k_transposed, 1)

                transpose_rows(0, 0, 0)
                tiles(pe, step, peeled=1)
def cross_attention(nc, sems, ident, ones, keyT_high, keyT_low, val_high, val_low, qT_high, qT_low, outT_high, outT_low):
    with ExitStack() as stack:
        m = Scope(nc, stack, "xa")
        sem = make_sem(nc, sems, "xa")
        two = lambda name: [sem(f"{name}{s}") for s in range(2)]
        PIECE = BANK * 2 // P
        PIECES = [(c * PIECE, (c + 1) * PIECE) for c in range(3)] + [(3 * PIECE, RT)]
        WIDE = RT // PIECE
        REST = RT * P - WIDE * PIECE * P
        PER = BANK * 2 // REST
        UNITS = WIDE * XQT + XQT // PER
        assert UNITS == RT
        PE_SHIFTED = [j for j in range(RT) if j < 2 or j % 3 == 1]
        DVE_TILES = RT - len(PE_SHIFTED)

        def dve_tiles(j):
            return sum(i not in PE_SHIFTED for i in range(j))


        kT_hi = [m.sb(f"kT_hi{s}", [P, NK], F32R) for s in range(2)]
        kT_lo = [m.sb(f"kT_lo{s}", [P, NK], F32R) for s in range(2)]
        v_hi = [m.sb(f"v_hi{s}", [P, HALF, HD], F32R) for s in range(2)]
        v_lo = [m.sb(f"v_lo{s}", [P, HALF, HD], F32R) for s in range(2)]
        q_hi = [m.sb(f"q_hi{s}", [P, XQ], F32R) for s in range(2)]
        q_lo = [m.sb(f"q_lo{s}", [P, XQ], F32R) for s in range(2)]
        q_max = [m.sb(f"q_max{s}", [P, XQ], F32R) for s in range(2)]
        prob = [m.sb(f"prob{s}", [P, XQ]) for s in range(2)]
        p_hi = [m.sb(f"p_hi{s}", [P, XQ], F32R) for s in range(2)]
        p_lo = [m.sb(f"p_lo{s}", [P, XQ], F32R) for s in range(2)]
        shift = m.sb("shift", [P, XQ])
        total = [m.sb(f"total{s}", [P, XQ]) for s in range(2)]
        zeros = m.sb("zeros", [P, 1])
        part_max = m.sb("part_max", [P, XQT, WIDE + 1])
        query_max = m.sb("query_max", [P, XQT])
        diag = [m.sb(f"diag{s}", [P, XQT, P], F32R) for s in range(2)]
        ones_r = m.sb("ones_r", [P, P], F32R)
        minus_r = m.sb("minus_r", [P, P], F32R)
        inverse = m.sb("inverse", [P, XQT])
        diag_inv = m.sb("diag_inv", [P, XQT, P])
        raw = m.sb("raw", [P, XQ])
        out = m.sb("out", [P, XQ])
        o_hi = m.sb("o_hi", [P, XQ], F32R)
        o_lo = m.sb("o_lo", [P, XQ], F32R)
        psS = [m.ps(f"psS{s}", [P, XQ]) for s in range(2)]
        psO = m.ps("psO", [P, XQ])
        psM = m.ps("psM", [P, XQ])

        setup, scores, shifted, exps, p_high, o_normed, o_high, o_lowed = map(sem, (
            "setup", "scores", "shifted", "exps", "p_high", "o_normed", "o_high", "o_lowed"))
        summed, p_low, pv = map(two, ("summed", "p_low", "pv"))
        qm_loaded, v_loaded = map(two, ("qm_loaded", "v_loaded"))
        q_loaded = two("q_loaded")
        k_loaded = [[sem(f"k_loaded{s}_{c}") for c in range(len(PIECES))] for s in range(2)]
        (mx_scores, mx_reduced, query_max_ready, diag_ready, shift_ps, shift_ready, o_raw, total_ps, inverse_ready,
         diag_inv_ready, inv_ps, o_stored) = map(sem, (
             "mx_scores", "mx_reduced", "query_max_ready", "diag_ready", "shift_ps", "shift_ready", "o_raw", "total_ps",
             "inverse_ready", "diag_inv_ready", "inv_ps", "o_stored"))
        PAIRS = XKV // 2

        def unit(u, ps):
            if u < WIDE * XQT:
                c, t = u // XQT, u % XQT
                return ([(t, c * PIECE * P + i * BANK, BANK, i * BANK) for i in range(2)],
                        part_max[:, t:t + 1, c], ps[:].rearrange("p (a n) -> p a n", a=1))
            t = (u - WIDE * XQT) * PER
            return ([(t + i, WIDE * PIECE * P, REST, i * REST) for i in range(PER)],
                    part_max[:, t:t + PER, WIDE], ps[:].rearrange("p (a n) -> p a n", a=PER))

        MAX_PS = [psM] + psS
        SUM_STEP, NORM_STEP, SPLIT_STEP = 3, 5, 6

        def units_at(j):
            return {0: [], 1: [0, 1]}.get(j, [j])

        def heads(eng, head):
            head(0, 0, 0, True, False)
            with eng.Fori(0, PAIRS - 1) as pair:
                head(pair * 2 + 1, pair, 1, False, False)
                head(pair * 2 + 2, pair + 1, 0, False, False)
            head(XKV - 1, PAIRS - 1, 1, False, True)

        sems.credit(scores, total_ps, *pv, o_normed, o_stored, *p_low, *summed, inv_ps, o_lowed, shifted, o_raw)
        with nc.Block() as block:
            @block.sync
            def _(sp):
                def load_qmax(e, s):
                    sp.dma_start(q_max[s][:].bitcast(F32), qT_high[bass.ds(e, 1), :, :].rearrange("e d q -> d (e q)")).then_inc(qm_loaded[s], 16)

                def load_q(e, s):
                    for dst, src in ((q_hi, qT_high), (q_lo, qT_low)):
                        sp.dma_start(dst[s][:].bitcast(F32), src[bass.ds(e, 1), :, :].rearrange("e d q -> d (e q)")).then_inc(q_loaded[s], 16)

                def load_keys(e, s, c):
                    a, b = (x * P for x in PIECES[c])
                    for dst, src in ((kT_hi, keyT_high), (kT_lo, keyT_low)):
                        sp.dma_start(dst[s][:, a:b].bitcast(F32),
                                     src[bass.ds(e, 1), :, a:b].rearrange("e d k -> d (e k)")).then_inc(k_loaded[s][c], 16)

                def load_values(e, half):
                    for dst, src in ((v_hi, val_high), (v_lo, val_low)):
                        sp.dma_start(dst[half][:].bitcast(F32),
                                     src[bass.ds(e, 1), :, half * HALF:(half + 1) * HALF, :].rearrange("e p t d -> p (e t) d")).then_inc(v_loaded[half], 16)

                def store(e):
                    sp.wait_ge(o_lowed, START + e + 1)
                    for src, dst in ((o_hi, outT_high), (o_lo, outT_low)):
                        sp.dma_start(dst[bass.ds(e, 1), :, :].rearrange("e d q -> d (e q)"), src[:].bitcast(F32)).then_inc(o_stored, 16)

                def head(e, s, ahead2, ahead1):
                    if ahead2:
                        sp.wait_ge(shift_ready, e + 1)
                        load_qmax(e + 2, s)
                    if ahead1:
                        sp.wait_ge(scores, START + e * RT)
                        load_q(e + 1, 1 - s)
                    for c, (_, b) in enumerate(PIECES):
                        if c == 1 and not (isinstance(e, int) and e == 0):
                            store(e - 1)
                        if ahead2:
                            sp.wait_ge(scores, START + e * RT + b)
                            load_keys(e + 2, s, c)
                        if c == 2 and ahead1:
                            sp.wait_ge(pv[(HALF - 1) % 2], START + e * HALF + (HALF - 1) // 2 + 1)
                            load_values(e + 1, 0)
                    if ahead1:
                        sp.wait_ge(pv[(RT - 1) % 2], START + e * HALF + HALF)
                        load_values(e + 1, 1)

                load_qmax(0, 0)
                for c in range(len(PIECES)):
                    load_keys(0, 0, c)
                load_q(0, 0)
                load_values(0, 0)
                load_qmax(1, 1)
                load_keys(1, 1, 0)
                load_values(0, 1)
                for c in range(1, len(PIECES)):
                    load_keys(1, 1, c)
                head(0, 0, True, True)
                with sp.Fori(0, PAIRS - 2) as pair:
                    head(pair * 2 + 1, 1, True, True)
                    head(pair * 2 + 2, 0, True, True)
                head(XKV - 3, 1, True, True)
                head(XKV - 2, 0, False, True)
                head(XKV - 1, 1, False, False)
                store(XKV - 1)
                sp.wait_ge(o_stored, START + 32 * XKV)

            @block.gpsimd
            def _(pool):
                pool.memset(zeros[:], 0.0).then_inc(setup, 1)
                pool.wait_ge(setup, 2)

                def split_out(e):
                    pool.wait_ge(o_high, e + 1)
                    pool.tensor_tensor(o_lo[:], out[:], o_hi[:].bitcast(F32), ALU.subtract).then_inc(o_lowed, 1)

                def head(e, pair, s, first, last):
                    for j in range(RT):
                        pool.wait_ge(exps, e * RT + j + 1)
                        if j:
                            pool.wait_ge(summed[(j - 1) % 2], START + e * HALF + (j - 1) // 2 + 1)
                        elif not first:
                            pool.wait_ge(total_ps, START + e - 1)
                        pool.tensor_tensor(total[s][:], total[s][:] if j else zeros[:].to_broadcast([P, XQ]), prob[j % 2][:],
                                           ALU.add).then_inc(summed[j % 2], 1)
                        if j == SPLIT_STEP and not first:
                            split_out(e - 1)

                heads(pool, head)
                split_out(XKV - 1)

            @block.scalar
            def _(act):
                def head(e, pair, s, first, last):
                    for j in range(RT):
                        if j in PE_SHIFTED:
                            act.wait_ge(scores, START + e * RT + j + 1)
                            act.wait_ge(p_low[j % 2], START + e * HALF + j // 2)
                            act.wait_ge(summed[j % 2], START + e * HALF + j // 2)
                            act.activation(prob[j % 2][:], psS[j % 2][:], ACT.Exp).then_inc(exps, 1)
                        else:
                            act.wait_ge(shifted, START + e * DVE_TILES + dve_tiles(j + 1))
                            act.activation(prob[j % 2][:], prob[j % 2][:], ACT.Exp).then_inc(exps, 1)
                        act.wait_ge(exps, e * RT + j + 1)
                        act.wait_ge(pv[j % 2], START + e * HALF + j // 2)
                        act.copy(p_hi[j % 2][:], prob[j % 2][:]).then_inc(p_high, 1)
                        if j == 0:
                            act.wait_ge(shift_ps, e + 1)
                            act.copy(shift[:], psM[:]).then_inc(shift_ready, 1)
                        if j == 1 and not first:
                            take_out(e - 1)
                        if j == SPLIT_STEP and not first:
                            split_out(e - 1)

                def take_out(e):
                    act.wait_ge(pv[(RT - 1) % 2], START + e * HALF + HALF)
                    act.wait_ge(o_normed, START + e)
                    act.copy(raw[:], psO[:]).then_inc(o_raw, 1)

                def split_out(e):
                    act.wait_ge(o_normed, START + e + 1)
                    act.wait_ge(o_stored, START + e * 32)
                    act.copy(o_hi[:], out[:]).then_inc(o_high, 1)

                heads(act, head)
                take_out(XKV - 1)
                split_out(XKV - 1)

            @block.vector
            def _(dve):
                dve.tensor_copy(ones_r[:], ones[:])
                dve.tensor_scalar(minus_r[:], ones[:], -1.0, 0.0, ALU.mult, ALU.add).then_inc(setup, 1)

                def reduce_unit(e, u, ps):
                    dve.wait_ge(mx_scores, e * UNITS + u + 1)
                    _, dst, src = unit(u, ps)
                    dve.tensor_reduce(dst, src, AX.X, ALU.max).then_inc(mx_reduced, 1)

                def finish_max(e, s):
                    dve.wait_ge(mx_reduced, (e + 1) * UNITS)
                    dve.tensor_reduce(query_max[:], part_max[:], AX.X, ALU.max).then_inc(query_max_ready, 1)
                    dve.wait_ge(query_max_ready, e + 1)
                    dve.tensor_tensor(diag[s][:], broadcast_outer(ident[:], XQT), broadcast_inner(query_max[:], P),
                                      ALU.mult).then_inc(diag_ready, 1)

                def low(e, j):
                    dve.wait_ge(p_high, e * RT + j + 1)
                    dve.tensor_tensor(p_lo[j % 2][:], prob[j % 2][:], p_hi[j % 2][:].bitcast(F32), ALU.subtract).then_inc(p_low[j % 2], 1)

                def invert_total(e):
                    dve.wait_ge(total_ps, START + e + 1)
                    dve.reciprocal(inverse[:], psM[:, 0:XQT]).then_inc(inverse_ready, 1)
                    dve.wait_ge(inverse_ready, e + 1)
                    dve.wait_ge(inv_ps, START + e)
                    dve.tensor_tensor(diag_inv[:], broadcast_outer(ident[:], XQT), broadcast_inner(inverse[:], P),
                                      ALU.mult).then_inc(diag_inv_ready, 1)

                def normalise(e):
                    dve.wait_ge(inv_ps, START + e + 1)
                    dve.wait_ge(o_raw, START + e + 1)
                    dve.wait_ge(o_lowed, START + e)
                    dve.tensor_tensor(out[:], psM[:], raw[:], ALU.mult).then_inc(o_normed, 1)

                def head(e, pair, s, first, last):
                    for j in range(RT):
                        if j not in PE_SHIFTED:
                            if dve_tiles(j) == 0:
                                dve.wait_ge(shift_ready, e + 1)
                            dve.wait_ge(scores, START + e * RT + j + 1)
                            dve.wait_ge(p_low[j % 2], START + e * HALF + j // 2)
                            dve.wait_ge(summed[j % 2], START + e * HALF + j // 2)
                            dve.tensor_tensor(prob[j % 2][:], psS[j % 2][:], shift[:], ALU.subtract).then_inc(shifted, 1)
                        if j:
                            low(e, j - 1)
                        elif not first:
                            low(e - 1, RT - 1)
                        if j == SUM_STEP and not first:
                            invert_total(e - 1)
                        if j == NORM_STEP and not first:
                            normalise(e - 1)
                        if not last:
                            for u in units_at(j):
                                reduce_unit(e + 1, u, psM)
                    if not last:
                        finish_max(e + 1, 1 - s)

                for u in range(UNITS):
                    reduce_unit(0, u, MAX_PS[u % len(MAX_PS)])
                finish_max(0, 0)
                heads(dve, head)
                low(XKV - 1, RT - 1)
                invert_total(XKV - 1)
                normalise(XKV - 1)

            @block.tensor
            def _(pe):
                def max_unit(pair, e, s, u, ps):
                    if u == 0:
                        pe.wait_ge(qm_loaded[s], pair * 16 + 16)
                    if u % XQT == 0 and u < WIDE * XQT:
                        pe.wait_ge(k_loaded[s][u // XQT], pair * 32 + 32)
                    for t, key, n, column in unit(u, ps)[0]:
                        last = pe.matmul(ps[:, column:column + n], q_max[s][:, t * P:(t + 1) * P], kT_hi[s][:, key:key + n],
                                         start=True, stop=True)
                    last.then_inc(mx_scores, 1)

                def spread(src, stationary, done):
                    for c in range(XQ // BANK):
                        last = pe.matmul(psM[:, c * BANK:(c + 1) * BANK], stationary[:],
                                         src[:].rearrange("p t q -> p (t q)")[:, c * BANK:(c + 1) * BANK], start=True, stop=True)
                    last.then_inc(done, 1)

                def score(e, s, j, first):
                    if j >= 2 or not first:
                        before, i = (e, j - 2) if j >= 2 else (e - 1, RT - 2 + j)
                        if i in PE_SHIFTED:
                            pe.wait_ge(exps, before * RT + i + 1)
                        else:
                            pe.wait_ge(shifted, START + before * DVE_TILES + dve_tiles(i + 1))
                    key = slice(j * P, (j + 1) * P)
                    shift_here = j in PE_SHIFTED
                    for n, (k, q) in enumerate(((kT_hi, q_hi), (kT_hi, q_lo), (kT_lo, q_hi))):
                        for c in range(XQ // BANK):
                            cols = slice(c * BANK, (c + 1) * BANK)
                            last = pe.matmul(psS[j % 2][:, cols], k[s][:, key], q[s][:, cols], start=(n == 0),
                                             stop=(n == 2 and not shift_here))
                    if shift_here:
                        if j == PE_SHIFTED[0]:
                            pe.wait_ge(diag_ready, e + 1)
                        for c in range(XQ // BANK):
                            cols = slice(c * BANK, (c + 1) * BANK)
                            last = pe.matmul(psS[j % 2][:, cols], minus_r[:], diag[s][:].rearrange("p t q -> p (t q)")[:, cols],
                                             start=False, stop=True)
                    last.then_inc(scores, 1)

                def value(e, j):
                    if j % HALF == 0:
                        pe.wait_ge(v_loaded[j // HALF], e * 32 + 32)
                    if j == 0:
                        pe.wait_ge(o_raw, START + e)
                    pe.wait_ge(p_low[j % 2], START + e * HALF + j // 2 + 1)
                    for n, (v, p) in enumerate(((v_hi, p_hi), (v_hi, p_lo), (v_lo, p_hi))):
                        for c in range(XQ // BANK):
                            cols = slice(c * BANK, (c + 1) * BANK)
                            last = pe.matmul(psO[:, cols], v[j // HALF][:, j % HALF, :], p[j % 2][:, cols],
                                             start=(j == 0 and n == 0), stop=(j == RT - 1 and n == 2))
                    last.then_inc(pv[j % 2], 1)

                def sum_total(e, s):
                    pe.wait_ge(summed[(RT - 1) % 2], START + e * HALF + HALF)
                    for t in range(XQT):
                        last = pe.matmul(psM[:, t:t + 1], total[s][:, t * P:(t + 1) * P], ones[:, 0:1], start=True, stop=True)
                    last.then_inc(total_ps, 1)

                def spread_inverse(e):
                    pe.wait_ge(diag_inv_ready, e + 1)
                    spread(diag_inv, ones, inv_ps)

                def head(e, pair, s, first, last):
                    pe.wait_ge(q_loaded[s], pair * 32 + 32)
                    for j in range(RT):
                        for c, (a, _) in enumerate(PIECES):
                            if a == j:
                                pe.wait_ge(k_loaded[s][c], pair * 32 + 32)
                        score(e, s, j, first)
                        if j == 1 and not last:
                            pe.wait_ge(shift_ready, e + 1)
                            max_unit(pair + s, e + 1, 1 - s, 0, psM)
                        if j in (SUM_STEP, NORM_STEP) and not first:
                            if last:
                                pe.wait_ge(shift_ready, e + 1)
                            else:
                                pe.wait_ge(mx_reduced, (e + 1) * UNITS + j)
                            if j == SUM_STEP:
                                sum_total(e - 1, 1 - s)
                            else:
                                spread_inverse(e - 1)
                        if j >= 2:
                            value(e, j - 2)
                        elif not first:
                            value(e - 1, RT - 2 + j)
                        if j == 0:
                            spread(diag[s], ones_r, shift_ps)
                        elif not last:
                            if j == SUM_STEP and not first:
                                pe.wait_ge(inverse_ready, e)
                            elif j == NORM_STEP and not first:
                                pe.wait_ge(o_normed, START + e)
                            else:
                                pe.wait_ge(mx_reduced, (e + 1) * UNITS + j)
                            max_unit(pair + s, e + 1, 1 - s, j, psM)

                pe.wait_ge(setup, 2)
                for u in range(UNITS):
                    if u >= len(MAX_PS):
                        pe.wait_ge(mx_reduced, u - len(MAX_PS) + 1)
                    max_unit(0, 0, 0, u, MAX_PS[u % len(MAX_PS)])
                pe.wait_ge(mx_reduced, UNITS)
                heads(pe, head)
                value(XKV - 1, RT - 2)
                value(XKV - 1, RT - 1)
                pe.wait_ge(o_normed, START + XKV - 1)
                sum_total(XKV - 1, 1)
                spread_inverse(XKV - 1)


def cross_output(nc, sems, Wo, outT_high, outT_low, x, acc):
    with ExitStack() as stack:
        m = Scope(nc, stack, "xo")
        sem = make_sem(nc, sems, "xo")
        SLOTS = 4
        ROUNDS = XKV // SLOTS
        w_raw = [m.sb(f"w_raw{s}", [P, XG, D]) for s in range(SLOTS)]
        w_hi = [m.sb(f"w_hi{s}", [P, XG, D], F32R) for s in range(2)]
        w_lo = [m.sb(f"w_lo{s}", [P, XG, D], F32R) for s in range(2)]
        o_hi = [m.sb(f"o_hi{s}", [P, XQ], F32R) for s in range(SLOTS)]
        o_lo = [m.sb(f"o_lo{s}", [P, XQ], F32R) for s in range(SLOTS)]
        psX = [m.ps(f"psX{s}", [P, QT, D]) for s in range(2)]
        x_loaded, w_high, w_low = map(sem, ("x_loaded", "w_high", "w_low"))
        projected, added = ([sem(f"{name}{s}") for s in range(2)] for name in ("projected", "added"))
        w_loaded, o_loaded = ([sem(f"{name}{s}") for s in range(SLOTS)] for name in ("w_loaded", "o_loaded"))
        Wo_v = Wo.rearrange("(e g d) n -> e d g n", g=XG, d=HD)
        sems.credit(*projected, *added)
        with nc.Block() as block:
            @block.sync
            def _(sp):
                for e in range(XKV):
                    s = e % SLOTS
                    if e >= SLOTS:
                        sp.wait_ge(w_low, (e - SLOTS + 1) * XG)
                        sp.wait_ge(projected[s % 2], START + (e - SLOTS) // 2 + 1)
                    sp.dma_start(w_raw[s][:], Wo_v[e]).then_inc(w_loaded[s], 16)
                    for dst, src in ((o_hi, outT_high), (o_lo, outT_low)):
                        sp.dma_start(dst[s][:].bitcast(F32), src[e]).then_inc(o_loaded[s], 16)
                    if e == 0:
                        sp.dma_start(acc[:], x.rearrange("(t p) d -> p t d", p=P)).then_inc(x_loaded, 16)

            @block.scalar
            def _(act):
                with act.Fori(0, ROUNDS) as turn:
                    for s in range(SLOTS):
                        act.wait_ge(w_loaded[s], turn * 16 + 16)
                        act.wait_ge(projected[s % 2], START + turn * 2 + s // 2)
                        for g in range(XG):
                            act.copy(w_hi[s % 2][:, g, :], w_raw[s][:, g, :]).then_inc(w_high, 1)

            @block.vector
            def _(dve):
                def split(turn, s):
                    for g in range(XG):
                        dve.wait_ge(w_high, turn * (SLOTS * XG) + (s * XG + g + 1))
                        dve.tensor_tensor(w_lo[s % 2][:, g, :], w_raw[s][:, g, :], w_hi[s % 2][:, g, :].bitcast(F32),
                                          ALU.subtract).then_inc(w_low, 1)

                def add(turn, s):
                    dve.wait_ge(projected[s % 2], START + turn * 2 + (s // 2 + 1))
                    dve.wait_ge(added[1 - s % 2], START + turn * 2 + (s + 1) // 2)
                    dve.tensor_tensor(acc[:], psX[s % 2][:], acc[:], ALU.add).then_inc(added[s % 2], 1)

                dve.wait_ge(x_loaded, 16)
                with dve.Fori(0, ROUNDS) as turn:
                    for s in range(SLOTS):
                        split(turn, s)
                        if s >= 2:
                            add(turn, s - 2)
                    for s in range(SLOTS - 2, SLOTS):
                        add(turn, s)

            @block.tensor
            def _(pe):
                with pe.Fori(0, ROUNDS) as turn:
                    for s in range(SLOTS):
                        pe.wait_ge(o_loaded[s], turn * 32 + 32)
                        pe.wait_ge(added[s % 2], START + turn * 2 + s // 2)
                        for g in range(XG):
                            pe.wait_ge(w_low, turn * (SLOTS * XG) + (s * XG + g + 1))
                            for t in range(QT):
                                rows = slice(g * NQ + t * P, g * NQ + (t + 1) * P)
                                for n, (o, w) in enumerate(((o_hi, w_hi[s % 2]), (o_hi, w_lo[s % 2]), (o_lo, w_hi[s % 2]))):
                                    for c in range(D // BANK):
                                        cols = slice(c * BANK, (c + 1) * BANK)
                                        last = pe.matmul(psX[s % 2][:, t, cols], o[s][:, rows], w[:, g, cols],
                                                         start=(g == 0 and n == 0), stop=(g == XG - 1 and n == 2))
                        last.then_inc(projected[s % 2], 1)


SH = 64
SG = 16
GH = SH // SG
LORA = 256
LT = LORA // P
ROPE = 64
PAIR = ROPE // 2
OGROUPS = 8
OHEADS = SH // OGROUPS
ORANK = 256
ORT = ORANK // P
OTILES = OGROUPS * ORT
MASKED = -1e30


def rotate(eng, ins, a, b, c, d, after_products, done, count):
    x1, x2, cos, sin = ins
    eng.tensor_tensor(a, x1, cos, ALU.mult)
    eng.tensor_tensor(b, x2, sin, ALU.mult)
    eng.tensor_tensor(c, x1, sin, ALU.mult)
    eng.tensor_tensor(d, x2, cos, ALU.mult).then_inc(after_products, 1)
    eng.wait_ge(after_products, count)
    eng.tensor_tensor(x1, a, b, ALU.subtract)
    eng.tensor_tensor(x2, c, d, ALU.add).then_inc(done, 1)


class LatentInputs:
    WT = LT + 1

    def __init__(self, nc, sems, m):
        sem = make_sem(nc, sems, "lpw")
        self.w_raw = m.sb("w_raw", [P, self.WT, D], BF16)
        self.q_w = m.sb("q_w", [P, LORA], BF16)
        self.kv_w = m.sb("kv_w", [P, HD], BF16)
        self.w_loaded, self.norm_loaded, self.rope_loaded = map(sem, ("w_loaded", "norm_loaded", "rope_loaded"))

    def load(self, sp, wq_a, wkv, q_norm_w, kv_norm_w, cos, sin, cos_sb, sin_sb):
        sp.dma_start(self.w_raw[:, 0:LT, :], wq_a.rearrange("(t p) n -> p t n", p=P)).then_inc(self.w_loaded, 16)
        sp.dma_start(self.w_raw[:, LT, :], wkv).then_inc(self.w_loaded, 16)
        sp.dma_start(self.q_w[:], q_norm_w.rearrange("(a n) -> a n", a=1).to_broadcast([P, LORA])).then_inc(self.norm_loaded, 16)
        sp.dma_start(self.kv_w[:], kv_norm_w.rearrange("(a n) -> a n", a=1).to_broadcast([P, HD])).then_inc(self.norm_loaded, 16)
        sp.dma_start(cos_sb[:], cos.rearrange("(t p) n -> p t n", p=P)).then_inc(self.rope_loaded, 16)
        sp.dma_start(sin_sb[:], sin.rearrange("(t p) n -> p t n", p=P)).then_inc(self.rope_loaded, 16)


def latent_projections(nc, sems, inputs, cos_sb, sin_sb, ident, ident_bf, yT_high, yT_low,
                       qrT_high, qrT_low, kv_high, kv_low, kvT_high, kvT_low):
    with ExitStack() as stack:
        m = Scope(nc, stack, "lp")
        sem = make_sem(nc, sems, "lp")
        WT, w_raw, q_w, kv_w = inputs.WT, inputs.w_raw, inputs.q_w, inputs.kv_w
        wT = m.sb("wT", [P, KT, WT * P], F32R)
        products = [m.sb(f"product{i}", [P, QT, PAIR]) for i in range(4)]
        unused = m.sb("unused", [P, QT, LORA + HD])
        squares = m.sb("squares", [P, 2, QT])
        var = m.sb("var", [P, 2, QT])
        rstd = m.sb("rstd", [P, 2, QT])
        power = m.sb("power", [P, 2, QT])
        qr = m.sb("qr", [P, QT, LORA])
        kv = m.sb("kv", [P, QT, HD])
        psW = m.ps("psW", [P, KT, WT * P], BF16)
        psP = m.ps("psP", [P, QT, BANK])
        psT = m.ps("psT", [P, WT, NQ])
        (w_transposed, w_ready, projected, squared, var_ready, rstd_ready, qr_ready,
         kv_normed, kv_products, kv_ready, kv_split, transposed, high, power_set) = map(sem, (
             "w_transposed", "w_ready", "projected", "squared", "var_ready",
             "rstd_ready", "qr_ready", "kv_normed", "kv_products", "kv_ready", "kv_split", "transposed", "high", "power_set"))
        with nc.Block() as block:
            @block.gpsimd
            def _(pool):
                pool.memset(power[:], -0.5).then_inc(power_set, 1)
                pool.wait_ge(power_set, 1)
                pool.wait_ge(var_ready, 1)
                pool.tensor_tensor(rstd[:], var[:], power[:], ALU.pow).then_inc(rstd_ready, 1)

            @block.tensor
            def _(pe):
                pe.wait_ge(inputs.w_loaded, 32)
                for k in range(KT):
                    for t in range(WT):
                        last = pe.transpose(psW[:, k, t * P:(t + 1) * P], w_raw[:, t, k * P:(k + 1) * P], ident_bf[:])
                last.then_inc(w_transposed, 1)
                pe.wait_ge(w_ready, 1)
                for t in range(QT):
                    for k in range(KT):
                        for n, y in enumerate((yT_high, yT_low)):
                            last = pe.matmul(psP[:, t, 0:WT * P], y[:, k, t * P:(t + 1) * P], wT[:, k, :],
                                             start=(k == 0 and n == 0), stop=(k == KT - 1 and n == 1))
                last.then_inc(projected, 1)
                pe.wait_ge(qr_ready, 1)
                for t in range(QT):
                    for r in range(LT):
                        pe.transpose(psT[:, r, t * P:(t + 1) * P], qr[:, t, r * P:(r + 1) * P], ident[:])
                pe.wait_ge(kv_ready, 1)
                for t in range(QT):
                    last = pe.transpose(psT[:, LT, t * P:(t + 1) * P], kv[:, t, :], ident[:])
                last.then_inc(transposed, 1)

            @block.scalar
            def _(act):
                act.wait_ge(w_transposed, 1)
                act.copy(wT[:], psW[:]).then_inc(w_ready, 1)
                act.wait_ge(projected, 1)
                for t in range(QT):
                    act.activation(unused[:, t, 0:LORA], psP[:, t, 0:LORA], ACT.Square, accum_out=squares[:, 0, t:t + 1])
                    last = act.activation(unused[:, t, LORA:LORA + HD], psP[:, t, LORA:LORA + HD], ACT.Square,
                                          accum_out=squares[:, 1, t:t + 1])
                last.then_inc(squared, 1)
                act.wait_ge(kv_ready, 1)
                act.copy(kv_high[:], kv[:]).then_inc(kv_split, 1)
                act.wait_ge(transposed, 1)
                act.copy(qrT_high[:], psT[:, 0:LT, :])
                act.copy(kvT_high[:], psT[:, LT, :]).then_inc(high, 1)

            @block.vector
            def _(dve):
                dve.wait_ge(squared, 1)
                dve.tensor_scalar(var[:, 0, :], squares[:, 0, :], 1.0 / LORA, RMS_EPS, ALU.mult, ALU.add)
                dve.tensor_scalar(var[:, 1, :], squares[:, 1, :], 1.0 / HD, RMS_EPS, ALU.mult, ALU.add).then_inc(var_ready, 1)
                dve.wait_ge(inputs.norm_loaded, 32)
                dve.wait_ge(rstd_ready, 1)
                for t in range(QT):
                    last = dve.scalar_tensor_tensor(qr[:, t, :], psP[:, t, 0:LORA], rstd[:, 0, t:t + 1], q_w[:], ALU.mult, ALU.mult)
                last.then_inc(qr_ready, 1)
                for t in range(QT):
                    last = dve.scalar_tensor_tensor(kv[:, t, :], psP[:, t, LORA:LORA + HD], rstd[:, 1, t:t + 1], kv_w[:], ALU.mult, ALU.mult)
                last.then_inc(kv_normed, 1)
                dve.wait_ge(kv_normed, 1)
                dve.wait_ge(inputs.rope_loaded, 32)
                pairs = kv[:, :, HD - ROPE:].rearrange("p t (i two) -> p t i two", two=2)
                rotate(dve, (pairs[:, :, :, 0], pairs[:, :, :, 1], cos_sb[:], sin_sb[:]), *[x[:] for x in products],
                       kv_products, kv_ready, 1)
                dve.wait_ge(kv_split, 1)
                dve.tensor_tensor(kv_low[:], kv[:], kv_high[:].bitcast(F32), ALU.subtract)
                dve.wait_ge(high, 1)
                dve.tensor_tensor(qrT_low[:], psT[:, 0:LT, :], qrT_high[:].bitcast(F32), ALU.subtract)
                dve.tensor_tensor(kvT_low[:], psT[:, LT, :], kvT_high[:].bitcast(F32), ALU.subtract)


def self_queries(nc, sems, wq_b, cos_sb, sin_sb, ident, ident_bf, qrT_high, qrT_low, qT_high, qT_low):
    with ExitStack() as stack:
        m = Scope(nc, stack, "sq")
        sem = make_sem(nc, sems, "sq")
        two = lambda name: [sem(f"{name}{s}") for s in range(2)]
        GC = GH * HD
        w_raw = [m.sb(f"w_raw{s}", [P, GH, LORA], BF16) for s in range(2)]
        wT = [m.sb(f"wT{s}", [P, LT, GC], F32R) for s in range(2)]
        q = [m.sb(f"q{s}", [P, QT, GH, HD]) for s in range(2)]
        products = [m.sb(f"product{i}", [P, QT, GH, PAIR]) for i in range(4)]
        squares = [m.sb(f"squares{s}", [P, QT * GH]) for s in range(2)]
        var = [m.sb(f"var{s}", [P, QT * GH]) for s in range(2)]
        rstd = [m.sb(f"rstd{s}", [P, QT * GH]) for s in range(2)]
        power = m.sb("power", [P, QT * GH])
        unused = m.sb("unused", [P, 2, QT * GH, HD])
        psW = [m.ps(f"psW{s}", [P, LT, GC], BF16) for s in range(2)]
        psQ = [m.ps(f"psQ{s}", [P, QT, GH, HD]) for s in range(2)]
        psT = m.ps("psT", [P, QT, GH, P])
        power_set, rope_products, rope_done = map(sem, ("power_set", "rope_products", "rope_done"))
        w_loaded, w_transposed, w_ready, projected, squared, var_ready, rstd_ready, normed, transposed, high, low = map(
            two, ("w_loaded", "w_transposed", "w_ready", "projected", "squared", "var_ready", "rstd_ready", "normed",
                  "transposed", "high", "low"))
        PAIRS = SG // 2
        w_v = wq_b.rearrange("(g h p) r -> g p h r", h=GH, p=P)
        sems.credit(*w_transposed, *w_ready, *projected, *normed, *low, *transposed, *var_ready, rope_done)
        with nc.Block() as block:
            @block.sync
            def _(sp):
                def load(pair, s):
                    sp.wait_ge(w_transposed[s], START + pair)
                    sp.dma_start(w_raw[s][:], w_v[bass.ds(pair * 2 + s, 1), :, :, :].rearrange("g p h r -> p (g h) r")).then_inc(w_loaded[s], 16)

                pipeline(sp, PAIRS, [(0, load)])

            @block.gpsimd
            def _(pool):
                def root(pair, s):
                    pool.wait_ge(var_ready[s], START + pair + 1)
                    pool.tensor_tensor(rstd[s][:], var[s][:], power[:], ALU.pow).then_inc(rstd_ready[s], 1)

                pool.memset(power[:], -0.5).then_inc(power_set, 1)
                pool.wait_ge(power_set, 1)
                pipeline(pool, PAIRS, [(0, root)])

            @block.tensor
            def _(pe):
                def transpose_weights(pair, s):
                    pe.wait_ge(w_loaded[s], pair * 16 + 16)
                    pe.wait_ge(w_ready[s], START + pair)
                    for r in range(LT):
                        for h in range(GH):
                            last = pe.transpose(psW[s][:, r, h * HD:(h + 1) * HD], w_raw[s][:, h, r * P:(r + 1) * P], ident_bf[:])
                    last.then_inc(w_transposed[s], 1)

                def multiply(pair, s):
                    pe.wait_ge(w_ready[s], START + pair + 1)
                    pe.wait_ge(normed[s], START + pair)
                    for t in range(QT):
                        for r in range(LT):
                            for n, x in enumerate((qrT_high, qrT_low)):
                                last = pe.matmul(psQ[s][:, t, :, :].rearrange("p h d -> p (h d)"), x[:, r, t * P:(t + 1) * P],
                                                 wT[s][:, r, :], start=(r == 0 and n == 0), stop=(r == LT - 1 and n == 1))
                    last.then_inc(projected[s], 1)

                def transpose(pair, s):
                    pe.wait_ge(rope_done, START + pair * 2 + (s + 1))
                    pe.wait_ge(low[1 - s], START + pair + s)
                    for t in range(QT):
                        for h in range(GH):
                            last = pe.transpose(psT[:, t, h, :], q[s][:, t, h, :], ident[:])
                    last.then_inc(transposed[s], 1)

                pipeline(pe, PAIRS, [(0, transpose), (3, multiply), (4, transpose_weights)])

            @block.scalar
            def _(act):
                def copy_weights(pair, s):
                    act.wait_ge(w_transposed[s], START + pair + 1)
                    act.wait_ge(projected[s], START + pair)
                    act.copy(wT[s][:], psW[s][:]).then_inc(w_ready[s], 1)

                def square(pair, s):
                    act.wait_ge(projected[s], START + pair + 1)
                    act.wait_ge(var_ready[s], START + pair)
                    for t in range(QT):
                        for h in range(GH):
                            i = t * GH + h
                            last = act.activation(unused[:, s, i, :], psQ[s][:, t, h, :], ACT.Square, accum_out=squares[s][:, i:i + 1])
                    last.then_inc(squared[s], 1)

                def split(pair, s):
                    act.wait_ge(transposed[s], START + pair + 1)
                    act.activation(qT_high[:, bass.ds(pair * 2 + s, 1), :, :, :].rearrange("p g t h q -> p (g t h q)"),
                                   psT[:].rearrange("p t h q -> p (t h q)"), ACT.Copy, scale=SCALE).then_inc(high[s], 1)

                pipeline(act, PAIRS, [(0, split), (3, square), (4, copy_weights)])

            @block.vector
            def _(dve):
                def mean(pair, s):
                    dve.wait_ge(squared[s], pair + 1)
                    dve.tensor_scalar(var[s][:], squares[s][:], 1.0 / HD, RMS_EPS, ALU.mult, ALU.add).then_inc(var_ready[s], 1)

                def normalise(pair, s):
                    dve.wait_ge(rstd_ready[s], pair + 1)
                    dve.wait_ge(transposed[s], START + pair)
                    dve.tensor_tensor(q[s][:].rearrange("p t h d -> p (t h) d"), psQ[s][:].rearrange("p t h d -> p (t h) d"),
                                      broadcast_inner(rstd[s][:], HD), ALU.mult).then_inc(normed[s], 1)

                def turn(pair, s):
                    dve.wait_ge(normed[s], START + pair + 1)
                    pairs = q[s][:, :, :, HD - ROPE:].rearrange("p t h (i two) -> p t h i two", two=2)
                    count = pair * 2 + s
                    dve.wait_ge(rope_done, START + count)
                    cos_h, sin_h = (x[:].unsqueeze(2).to_broadcast([P, QT, GH, PAIR]) for x in (cos_sb, sin_sb))
                    rotate(dve, (pairs[:, :, :, :, 0], pairs[:, :, :, :, 1], cos_h, sin_h), *[x[:] for x in products],
                           rope_products, rope_done, count + 1)

                def split(pair, s):
                    dve.wait_ge(high[s], pair + 1)
                    group = bass.ds(pair * 2 + s, 1)
                    dve.scalar_tensor_tensor(qT_low[:, group, :, :, :].rearrange("p g t h q -> p (g t h q)"),
                                             psT[:].rearrange("p t h q -> p (t h q)"), SCALE,
                                             qT_high[:, group, :, :, :].rearrange("p g t h q -> p (g t h q)").bitcast(F32),
                                             ALU.mult, ALU.subtract).then_inc(low[s], 1)

                pipeline(dve, PAIRS, [(1, normalise), (2, mean), (1, turn), (0, split)])


def self_maxima(nc, sems, sink, ident, kvT_high, qT_high, triangle_qk, ident_r, query_max, sink_exp):
    with ExitStack() as stack:
        m = Scope(nc, stack, "sm")
        sem = make_sem(nc, sems, "sm")
        two = lambda name: [sem(f"{name}{s}") for s in range(2)]
        sink_sb = m.sb("sink_sb", [P, SG, GH])
        stationary = [m.sb(f"stationary{s}", [P, QT, GH, P], F32R) for s in range(2)]
        raw_max = m.sb("raw_max", [P, SG, QT, GH])
        sink_shifted = m.sb("sink_shifted", [P, SG, QT, GH])
        ps0 = [m.ps(f"ps0{s}", [P, GH, P]) for s in range(2)]
        ps1 = [m.ps(f"ps1{s}", [P, GH, 2 * P]) for s in range(2)]
        sink_loaded, all_max, rounded, shifted = map(sem, ("sink_loaded", "all_max", "rounded", "shifted"))
        staged, scored, reduced = map(two, ("staged", "scored", "reduced"))
        PAIRS = SG // 2
        sems.credit(*scored, *reduced)
        with nc.Block() as block:
            @block.sync
            def _(sp):
                sp.dma_start(sink_sb[:].rearrange("p g h -> p (g h)"),
                             sink.rearrange("(a n) -> a n", a=1).to_broadcast([P, SH])).then_inc(sink_loaded, 16)

            @block.scalar
            def _(act):
                with act.Fori(0, PAIRS) as pair:
                    for s in range(2):
                        act.wait_ge(scored[s], START + pair)
                        act.copy(stationary[s][:], qT_high[:, bass.ds(pair * 2 + s, 1), :, :, :].rearrange(
                            "p g t h q -> p (g t) h q").bitcast(F32)).then_inc(staged[s], 1)
                act.wait_ge(shifted, 1)
                act.activation(sink_exp[:], sink_shifted[:], ACT.Exp)

            @block.tensor
            def _(pe):
                with pe.Fori(0, PAIRS) as pair:
                    for s in range(2):
                        pe.wait_ge(staged[s], pair + 1)
                        pe.wait_ge(reduced[s], START + pair)
                        pe.matmul(ps0[s][:], ident_r[:], broadcast_outer(triangle_qk[:, P:2 * P], GH), start=True, stop=False)
                        for h in range(GH):
                            pe.matmul(ps0[s][:, h, :], stationary[s][:, 0, h, :], kvT_high[:, 0:P], start=False, stop=(h == GH - 1))
                        for a in range(0, GH, 2):
                            pe.matmul(ps1[s][:, a:a + 2, :], ident_r[:], broadcast_outer(triangle_qk[:], 2), start=True, stop=False)
                            for h in (a, a + 1):
                                last = pe.matmul(ps1[s][:, h, :], stationary[s][:, 1, h, :], kvT_high[:], start=False, stop=(h == a + 1))
                        last.then_inc(scored[s], 1)

            @block.vector
            def _(dve):
                with dve.Fori(0, PAIRS) as pair:
                    for s in range(2):
                        dve.wait_ge(scored[s], START + pair + 1)
                        group = bass.ds(pair * 2 + s, 1)
                        dve.tensor_reduce(raw_max[:, group, 0, :].rearrange("p g h -> p (g h)"), ps0[s][:], AX.X, ALU.max)
                        dve.tensor_reduce(raw_max[:, group, 1, :].rearrange("p g h -> p (g h)"), ps1[s][:], AX.X, ALU.max).then_inc(reduced[s], 1)
                for s in range(2):
                    dve.wait_ge(reduced[s], START + PAIRS)
                dve.wait_ge(sink_loaded, 16)
                for t in range(QT):
                    last = dve.tensor_tensor(query_max[:, :, t, :], raw_max[:, :, t, :], sink_sb[:], ALU.max)
                last.then_inc(rounded, 1)
                dve.wait_ge(rounded, 1)
                for t in range(QT):
                    last = dve.tensor_tensor(sink_shifted[:, :, t, :], sink_sb[:], query_max[:, :, t, :].bitcast(F32), ALU.subtract)
                last.then_inc(shifted, 1)


def self_attention(nc, sems, ident, ident_r, ones_r, minus_r, triangle_kq, kv_high, kv_low, kvT_high, kvT_low,
                   query_max, sink_exp, qT_high, qT_low, sums, inverse):
    with ExitStack() as stack:
        m = Scope(nc, stack, "sa")
        sem = make_sem(nc, sems, "sa")
        two = lambda name: [sem(f"{name}{s}") for s in range(2)]
        CHUNKS = [(0, 0), (1, 0), (1, 1)]
        NC = len(CHUNKS)
        GQ = GH * P
        ROWS = SG * QT * GH
        diag = m.sb("diag", [P, QT * GH, P], F32R)
        prob = [m.sb(f"prob{s}", [P, NC, GQ]) for s in range(2)]
        p_hi = [m.sb(f"p_hi{s}", [P, NC, GQ], F32R) for s in range(2)]
        p_lo = [m.sb(f"p_lo{s}", [P, NC, GQ], F32R) for s in range(2)]
        sum_row = m.sb("sum_row", [1, QT * GQ])
        all_sums = m.sb("all_sums", [ROWS, P])
        with_sink = m.sb("with_sink", [ROWS, P])
        inverted = m.sb("inverted", [ROWS, P])
        psS = m.ps("psS", [P, NC, GQ])
        psO = m.ps("psO", [P, QT, GQ])
        psD = m.ps("psD", [P, QT, GQ])
        psE = m.ps("psE", [ROWS, P])
        diag_ready, p_high, p_low, valued, o_high, o_low = map(two, (
            "diag_ready", "p_high", "p_low", "valued", "o_high", "o_low"))
        scored = [[sem(f"scored{s}_{i}") for i in range(NC)] for s in range(2)]
        exps = [sem(f"exps{i}") for i in range(NC)]
        sums_taken, stored, sink_transposed, sums_loaded, sink_added, inverse_ready, inverse_stored = map(sem, (
            "sums_taken", "stored", "sink_transposed", "sums_loaded", "sink_added", "inverse_ready", "inverse_stored"))
        PAIRS = SG // 2

        def group(ap, pair, s):
            return ap[:, bass.ds(pair * 2 + s, 1), :, :, :].rearrange("p g t h q -> p (g t) (h q)")

        sems.credit(*o_low, *valued, *p_low, sums_taken, stored, *scored[0], *scored[1], *exps)
        with nc.Block() as block:
            @block.sync
            def _(sp):
                def store(pair, s):
                    sp.wait_ge(sums_taken, START + pair * 2 + (s + 1))
                    sp.dma_start(sums[bass.ds(pair * 2 + s, 1), :], sum_row[:]).then_inc(stored, 16)

                pipeline(sp, PAIRS, [(0, store)])
                sp.wait_ge(stored, START + 16 * SG)
                sp.dma_start(all_sums[:], sums.rearrange("g (n q) -> (g n) q", q=P)).then_inc(sums_loaded, 16)
                sp.wait_ge(inverse_ready, 1)
                sp.dma_start(inverse.rearrange("g (n q) -> (g n) q", q=P), inverted[:]).then_inc(inverse_stored, 16)
                sp.wait_ge(inverse_stored, 16)

            @block.tensor
            def _(pe):
                def scores(pair, s):
                    pe.wait_ge(diag_ready[s], pair + 1)
                    for i, (t, k) in enumerate(CHUNKS):
                        pe.wait_ge(exps[i], START + pair * 2 + s)
                        if t == k:
                            pe.matmul(psS[:, i, :], ident_r[:], broadcast_outer(triangle_kq[:], GH), start=True, stop=False)
                        for n, (key, q) in enumerate(((kvT_high, qT_high), (kvT_high, qT_low), (kvT_low, qT_high))):
                            pe.matmul(psS[:, i, :], key[:, k * P:(k + 1) * P], group(q, pair, s)[:, t, :],
                                      start=(n == 0 and t != k), stop=False)
                        pe.matmul(psS[:, i, :], minus_r[:], diag[:, t * GH:(t + 1) * GH, :].rearrange("p h q -> p (h q)"),
                                  start=False, stop=True).then_inc(scored[s][i], 1)

                def values(pair, s):
                    pe.wait_ge(p_low[s], START + pair + 1)
                    pe.wait_ge(sums_taken, START + pair * 2 + s)
                    for i, (t, k) in enumerate(CHUNKS):
                        for n, p in enumerate((p_hi, p_lo)):
                            pe.matmul(psD[:, t, :], ones_r[:], p[s][:, i, :], start=(n == 0 and k == 0),
                                      stop=(n == 1 and t == k))
                    pe.wait_ge(o_low[1 - s], START + pair + s)
                    for i, (t, k) in enumerate(CHUNKS):
                        for n, (v, p) in enumerate(((kv_high, p_hi), (kv_high, p_lo), (kv_low, p_hi))):
                            last = pe.matmul(psO[:, t, :], v[:, k, :], p[s][:, i, :], start=(n == 0 and k == 0),
                                             stop=(n == 2 and t == k))
                    last.then_inc(valued[s], 1)

                pe.transpose(psE[:], sink_exp[:].rearrange("p g t h -> p (g t h)"), ident[:]).then_inc(sink_transposed, 1)
                pipeline(pe, PAIRS, [(1, scores), (0, values)])

            @block.scalar
            def _(act):
                def exponentials(pair, s):
                    act.wait_ge(p_low[s], START + pair)
                    for i in range(NC):
                        act.wait_ge(scored[s][i], START + pair + 1)
                        last = act.activation(prob[s][:, i, :], psS[:, i, :], ACT.Exp).then_inc(exps[i], 1)
                    for i in range(NC):
                        act.wait_ge(exps[i], START + pair * 2 + s + 1)
                    act.wait_ge(valued[s], START + pair)
                    act.copy(p_hi[s][:], prob[s][:]).then_inc(p_high[s], 1)

                def take_out(pair, s):
                    act.wait_ge(valued[s], START + pair + 1)
                    act.copy(group(qT_high, pair, s), psO[:]).then_inc(o_high[s], 1)

                pipeline(act, PAIRS, [(1, exponentials), (0, take_out)])

            @block.gpsimd
            def _(pool):
                def place_maxima(pair, s):
                    pool.wait_ge(scored[1 - s][NC - 1], START + pair + s)
                    pool.tensor_tensor(diag[:], broadcast_outer(ident[:], QT * GH), broadcast_inner(
                        query_max[:, bass.ds(pair * 2 + s, 1), :, :].rearrange("p g t h -> p (g t h)").bitcast(F32), P),
                        ALU.mult).then_inc(diag_ready[s], 1)

                pipeline(pool, PAIRS, [(0, place_maxima)])

            @block.vector
            def _(dve):
                def split_probabilities(pair, s):
                    dve.wait_ge(p_high[s], pair + 1)
                    dve.tensor_tensor(p_lo[s][:], prob[s][:], p_hi[s][:].bitcast(F32), ALU.subtract).then_inc(p_low[s], 1)

                def take_out(pair, s):
                    dve.wait_ge(o_high[s], pair + 1)
                    dve.tensor_tensor(group(qT_low, pair, s), psO[:], group(qT_high, pair, s).bitcast(F32), ALU.subtract).then_inc(o_low[s], 1)
                    dve.wait_ge(stored, START + pair * 32 + 16 * s)
                    dve.tensor_copy(sum_row[:], psD[0:1, :, :].rearrange("p t n -> p (t n)")).then_inc(sums_taken, 1)

                pipeline(dve, PAIRS, [(1, split_probabilities), (0, take_out)])
                dve.wait_ge(sink_transposed, 1)
                dve.wait_ge(sums_loaded, 16)
                dve.tensor_tensor(with_sink[:], psE[:], all_sums[:], ALU.add).then_inc(sink_added, 1)
                dve.wait_ge(sink_added, 1)
                dve.reciprocal(inverted[:], with_sink[:]).then_inc(inverse_ready, 1)


def rotate_outputs(nc, sems, cos_sb, sin_sb, ident, ident_r, swap_r, oT_high, oT_low, inverse):
    with ExitStack() as stack:
        m = Scope(nc, stack, "ro")
        sem = make_sem(nc, sems, "ro")
        two = lambda name: [sem(f"{name}{s}") for s in range(2)]
        GQ = GH * P
        wide = m.sb("wide", [P, 2, QT, HD])
        wideT = m.sb("wideT", [P, 2, QT, P])
        by_cos = [m.sb(f"by_cos{s}", [P, QT, GH, P]) for s in range(2)]
        by_sin = [m.sb(f"by_sin{s}", [P, QT, GH, P]) for s in range(2)]
        turned = [m.sb(f"turned{s}", [P, QT * GQ]) for s in range(2)]
        out = [m.sb(f"out{s}", [P, QT * GQ]) for s in range(2)]
        inv = [m.sb(f"inv{s}", [P, QT * GQ]) for s in range(2)]
        psU = [m.ps(f"psU{s}", [P, QT, GQ]) for s in range(2)]
        psR = [m.ps(f"psR{s}", [P, QT, GQ]) for s in range(2)]
        psT = psR[1][:, 0, :].rearrange("p (i t q) -> p i t q", i=2, t=QT)
        filled, widened, wide_transposed, wide_ready = map(sem, ("filled", "widened", "wide_transposed", "wide_ready"))
        moved, multiplied, turned_ready, inv_loaded, scaled, high, low = map(
            two, ("moved", "multiplied", "turned_ready", "inv_loaded", "scaled", "high", "low"))
        PAIRS = SG // 2

        def group(ap, pair, s):
            return ap[:, bass.ds(pair * 2 + s, 1), :, :, :].rearrange("p g t h q -> p (g t) (h q)")

        sems.credit(*scaled, *multiplied, *turned_ready, *low)
        with nc.Block() as block:
            @block.sync
            def _(sp):
                def load(pair, s):
                    sp.wait_ge(scaled[s], START + pair)
                    sp.dma_start(inv[s][:], inverse[bass.ds(pair * 2 + s, 1), :].to_broadcast([P, QT * GQ])).then_inc(inv_loaded[s], 16)

                pipeline(sp, PAIRS, [(0, load)])

            @block.gpsimd
            def _(pool):
                pool.memset(wide[:, 0, :, 0:HD - ROPE], 1.0)
                pool.memset(wide[:, 1, :, 0:HD - ROPE], 0.0).then_inc(filled, 1)
                with pool.Fori(0, PAIRS) as pair:
                    for s in range(2):
                        pool.wait_ge(multiplied[s], START + pair + 1)
                        pool.wait_ge(scaled[s], START + pair)
                        pool.tensor_tensor(turned[s][:], by_cos[s][:].rearrange("p t h q -> p (t h q)"),
                                           by_sin[s][:].rearrange("p t h q -> p (t h q)"), ALU.add).then_inc(turned_ready[s], 1)

            @block.tensor
            def _(pe):
                pe.wait_ge(widened, 1)
                pe.wait_ge(filled, 1)
                for i in range(2):
                    for t in range(QT):
                        last = pe.transpose(psT[:, i, t, :], wide[:, i, t, :], ident[:])
                last.then_inc(wide_transposed, 1)

                def move(pair, s):
                    pe.wait_ge(multiplied[s], START + pair)
                    for ps, matrix in ((psU[s], ident_r), (psR[s], swap_r)):
                        for n, o in enumerate((oT_high, oT_low)):
                            for t in range(QT):
                                last = pe.matmul(ps[:, t, :], matrix[:], group(o, pair, s)[:, t, :], start=(n == 0), stop=(n == 1))
                    last.then_inc(moved[s], 1)

                pe.wait_ge(wide_ready, 1)
                pipeline(pe, PAIRS, [(0, move)])

            @block.scalar
            def _(act):
                act.wait_ge(wide_transposed, 1)
                act.copy(wideT[:], psT).then_inc(wide_ready, 1)
                with act.Fori(0, PAIRS) as pair:
                    for s in range(2):
                        act.wait_ge(scaled[s], START + pair + 1)
                        act.copy(group(oT_high, pair, s).rearrange("p t n -> p (t n)"), out[s][:]).then_inc(high[s], 1)

            @block.vector
            def _(dve):
                for i, angle in enumerate((cos_sb, sin_sb)):
                    rotated = wide[:, i, :, HD - ROPE:].rearrange("p t (n two) -> p t n two", two=2)
                    for half in range(2):
                        last = dve.tensor_copy(rotated[:, :, :, half], angle[:])
                last.then_inc(widened, 1)
                dve.wait_ge(wide_ready, 1)

                def multiply(pair, s):
                    dve.wait_ge(moved[s], pair + 1)
                    dve.wait_ge(turned_ready[s], START + pair)
                    for t in range(QT):
                        for i, (ps, dst) in enumerate(((psU[s], by_cos), (psR[s], by_sin))):
                            last = dve.tensor_tensor(dst[s][:, t, :, :], ps[:, t, :].rearrange("p (h q) -> p h q", h=GH),
                                                     broadcast_outer(wideT[:, i, t, :], GH), ALU.mult)
                    last.then_inc(multiplied[s], 1)

                def scale(pair, s):
                    dve.wait_ge(turned_ready[s], START + pair + 1)
                    dve.wait_ge(inv_loaded[s], pair * 16 + 16)
                    dve.wait_ge(low[s], START + pair)
                    dve.tensor_tensor(out[s][:], inv[s][:], turned[s][:], ALU.mult).then_inc(scaled[s], 1)

                def split(pair, s):
                    dve.wait_ge(high[s], pair + 1)
                    dve.tensor_tensor(group(oT_low, pair, s).rearrange("p t n -> p (t n)"), out[s][:],
                                      group(oT_high, pair, s).rearrange("p t n -> p (t n)").bitcast(F32), ALU.subtract).then_inc(low[s], 1)

                pipeline(dve, PAIRS, [(2, multiply), (1, scale), (0, split)])


def grouped_projection(nc, sems, wo_a, ident_bf, oT_high, oT_low, ogT):
    with ExitStack() as stack:
        m = Scope(nc, stack, "gp")
        sem = make_sem(nc, sems, "gp")
        two = lambda name: [sem(f"{name}{s}") for s in range(2)]
        w_raw = [m.sb(f"w_raw{s}", [P, ORT, OHEADS * HD], BF16) for s in range(2)]
        wT = [m.sb(f"wT{s}", [P, OHEADS, ORANK], F32R) for s in range(2)]
        psW = [m.ps(f"psW{s}", [P, OHEADS, ORANK], BF16) for s in range(2)]
        psG = [m.ps(f"psG{s}", [P, ORT, NQ]) for s in range(2)]
        w_loaded, w_transposed, w_ready, projected, copied = map(
            two, ("w_loaded", "w_transposed", "w_ready", "projected", "copied"))
        PAIRS = OGROUPS // 2
        w_v = wo_a.rearrange("(g t p) n -> g p t n", t=ORT, p=P)
        sems.credit(*w_ready, *copied)
        with nc.Block() as block:
            @block.sync
            def _(sp):
                def load(g, s):
                    sp.dma_start(w_raw[s][:], w_v[bass.ds(g, 1), :, :, :].rearrange("g p t n -> p (g t) n")).then_inc(w_loaded[s], 16)

                load(0, 0)
                load(1, 1)
                with sp.Fori(0, PAIRS - 1) as pair:
                    for s in range(2):
                        sp.wait_ge(w_transposed[s], pair + 1)
                        load(pair * 2 + (2 + s), s)

            @block.tensor
            def _(pe):
                with pe.Fori(0, PAIRS) as pair:
                    for s in range(2):
                        pe.wait_ge(w_loaded[s], pair * 16 + 16)
                        pe.wait_ge(w_ready[s], START + pair)
                        for h in range(OHEADS):
                            for r in range(ORT):
                                last = pe.transpose(psW[s][:, h, r * P:(r + 1) * P], w_raw[s][:, r, h * HD:(h + 1) * HD], ident_bf[:])
                        last.then_inc(w_transposed[s], 1)
                    for s in range(2):
                        pe.wait_ge(w_ready[s], START + pair + 1)
                        pe.wait_ge(copied[s], START + pair)
                        for r in range(ORT):
                            for h in range(OHEADS):
                                group = bass.ds(pair * 4 + (s * 2 + h // GH), 1)
                                for n, o in enumerate((oT_high, oT_low)):
                                    last = pe.matmul(psG[s][:, r, :].rearrange("p (t q) -> p t q", t=QT), wT[s][:, h, r * P:(r + 1) * P],
                                                     o[:, group, :, h % GH, :].rearrange("p g t q -> p (g t) q"),
                                                     start=(h == 0 and n == 0), stop=(h == OHEADS - 1 and n == 1))
                        last.then_inc(projected[s], 1)

            @block.scalar
            def _(act):
                with act.Fori(0, PAIRS) as pair:
                    for s in range(2):
                        act.wait_ge(w_transposed[s], pair + 1)
                        act.copy(wT[s][:], psW[s][:]).then_inc(w_ready[s], 1)

            @block.vector
            def _(dve):
                with dve.Fori(0, PAIRS) as pair:
                    for s in range(2):
                        dve.wait_ge(projected[s], pair + 1)
                        dve.tensor_copy(ogT[:, bass.ds(pair * 4 + s * 2, ORT), :], psG[s][:]).then_inc(copied[s], 1)


def output_projection(nc, sems, wo_b, ident_bf, ogT, x1, y, meanwhile):
    with ExitStack() as stack:
        m = Scope(nc, stack, "op")
        sem = make_sem(nc, sems, "op")
        STEP = 4
        STEPS = OTILES // STEP
        NT = D // P
        w_raw = [m.sb(f"w_raw{s}", [P, NT, STEP * P], BF16) for s in range(2)]
        wT = [m.sb(f"wT{s}", [P, STEP, D], F32R) for s in range(2)]
        ogT_high, ogT_low = (m.sb(f"ogT_{p}", [P, OTILES, NQ], F32R) for p in ("high", "low"))
        x = m.sb("x", [P, QT, D])
        psW = m.ps("psW", [P, STEP, D], BF16)
        psX = m.ps("psX", [P, QT, D])
        w_loaded = [sem(f"w_loaded{s}") for s in range(2)]
        x_loaded, w_transposed, w_ready, og_high, og_low, projected = map(sem, (
            "x_loaded", "w_transposed", "w_ready", "og_high", "og_low", "projected"))
        w_v = wo_b.rearrange("(t p) r -> p t r", p=P)
        with nc.Block() as block:
            @block.sync
            def _(sp):
                for i in range(STEPS):
                    if i >= 2:
                        sp.wait_ge(w_transposed, i - 1)
                    sp.dma_start(w_raw[i % 2][:], w_v[:, :, i * STEP * P:(i + 1) * STEP * P]).then_inc(w_loaded[i % 2], 16)
                    if i == 1:
                        sp.dma_start(x[:], x1.rearrange("(t p) d -> p t d", p=P)).then_inc(x_loaded, 16)
                meanwhile(sp)

            @block.tensor
            def _(pe):
                def transpose(i):
                    pe.wait_ge(w_loaded[i % 2], 16 * (i // 2 + 1))
                    if i:
                        pe.wait_ge(w_ready, i)
                    for r in range(STEP):
                        for n in range(NT):
                            last = pe.transpose(psW[:, r, n * P:(n + 1) * P], w_raw[i % 2][:, n, r * P:(r + 1) * P], ident_bf[:])
                    last.then_inc(w_transposed, 1)

                transpose(0)
                pe.wait_ge(og_low, 1)
                for i in range(STEPS):
                    if i + 1 < STEPS:
                        transpose(i + 1)
                    pe.wait_ge(w_ready, i + 1)
                    for t in range(QT):
                        for r in range(STEP):
                            for n, og in enumerate((ogT_high, ogT_low)):
                                for c in range(D // BANK):
                                    cols = slice(c * BANK, (c + 1) * BANK)
                                    last = pe.matmul(psX[:, t, cols], og[:, i * STEP + r, t * P:(t + 1) * P], wT[i % 2][:, r, cols],
                                                     start=(i == 0 and r == 0 and n == 0), stop=(i == STEPS - 1 and r == STEP - 1 and n == 1))
                    last.then_inc(projected, 1)

            @block.scalar
            def _(act):
                act.copy(ogT_high[:], ogT[:]).then_inc(og_high, 1)
                for i in range(STEPS):
                    act.wait_ge(w_transposed, i + 1)
                    if i >= 2:
                        act.wait_ge(projected, i - 1)
                    act.copy(wT[i % 2][:], psW[:]).then_inc(w_ready, 1)

            @block.vector
            def _(dve):
                dve.wait_ge(og_high, 1)
                dve.tensor_tensor(ogT_low[:], ogT[:], ogT_high[:].bitcast(F32), ALU.subtract).then_inc(og_low, 1)
                dve.wait_ge(x_loaded, 16)
                dve.wait_ge(projected, STEPS)
                dve.tensor_tensor(y[:], psX[:], x[:], ALU.add)


CLUSTERS = 64
THRESHOLD = 0.01
INV_TEMPERATURE = 10.0


class LinearInputs:

    def __init__(self, nc, sems, m):
        sem = make_sem(nc, sems, "glw")
        self.w_raw = m.sb("w_raw", [P, D // P, D])
        self.c_raw = m.sb("c_raw", [CLUSTERS, D])
        self.bias = m.sb("bias", [P, D])
        self.assign = m.sb("assign", [CLUSTERS, D], I32)
        self.w_loaded, self.c_loaded, self.bias_loaded, self.assign_loaded = map(sem, (
            "w_loaded", "c_loaded", "bias_loaded", "assign_loaded"))

    def load(self, sp, weight, bias, centroids, assignments):
        sp.dma_start(self.c_raw[:], centroids).then_inc(self.c_loaded, 16)
        sp.dma_start(self.w_raw[:], weight.rearrange("(t p) n -> p t n", p=P)).then_inc(self.w_loaded, 16)
        sp.dma_start(self.assign[:], assignments.rearrange("(a n) -> a n", a=1).to_broadcast([CLUSTERS, D])).then_inc(self.assign_loaded, 16)
        sp.dma_start(self.bias[:], bias.rearrange("(a n) -> a n", a=1).to_broadcast([P, D])).then_inc(self.bias_loaded, 16)


def gated_linear(nc, sems, x, inputs, ident, ones, yT_high, yT_low, out):
    with ExitStack() as stack:
        m = Scope(nc, stack, "gl")
        sem = make_sem(nc, sems, "gl")
        NT = D // P
        w_raw, c_raw, bias_sb, assign = inputs.w_raw, inputs.c_raw, inputs.bias, inputs.assign
        w_hi = m.sb("w_hi", [P, KT, D], F32R)
        w_lo = m.sb("w_lo", [P, KT, D], F32R)
        c_hi = m.sb("c_hi", [P, KT, CLUSTERS], F32R)
        c_lo = m.sb("c_lo", [P, KT, CLUSTERS], F32R)
        logitT = m.sb("logitT", [CLUSTERS, NQ])
        assign_f = m.sb("assign_f", [CLUSTERS, D])
        index = m.sb("index", [CLUSTERS, 1], I32)
        index_f = m.sb("index_f", [CLUSTERS, 1])
        onehot = m.sb("onehot", [CLUSTERS, D])
        peak = m.sb("peak", [P, QT])
        minus_peak = m.sb("minus_peak", [P, QT])
        exps = m.sb("exps", [P, QT, CLUSTERS])
        sums = m.sb("sums", [P, QT])
        inverse = m.sb("inverse", [P, QT])
        hits = m.sb("hits", [P, QT, CLUSTERS])
        row_hit = m.sb("row_hit", [P, QT])
        cluster_hit = m.sb("cluster_hit", [CLUSTERS, P])
        gate = m.sb("gate", [P, QT, D])
        base = m.sb("base", [P, QT, D])
        y = m.sb("y", [P, QT, D])
        psW = m.ps("psW", [P, D])
        psY = m.ps("psY", [P, QT, D])
        psL = m.ps("psL", [P, BANK])
        psG = m.ps("psG", [P, BANK])
        (index_made, indices, converted, onehot_made, c_transposed, c_high, c_low, logits_T, logits_copied, logits, peaked,
         negated, exped, inverted, hit, row_ready, counted, cluster_ready, w_transposed, w_high, w_low, selected, gate_ready,
         bias_gated, base_ready, projected, multiplied, done, stored) = map(sem, (
             "index_made", "indices", "converted", "onehot_made", "c_transposed", "c_high", "c_low", "logits_T", "logits_copied",
             "logits", "peaked", "negated", "exped", "inverted", "hit", "row_ready", "counted", "cluster_ready", "w_transposed",
             "w_high", "w_low", "selected", "gate_ready", "bias_gated", "base_ready", "projected", "multiplied", "done", "stored"))
        cT = psL[:, 0:KT * CLUSTERS].rearrange("p (k c) -> p k c", k=KT)
        logit = psL[:, 0:QT * CLUSTERS].rearrange("p (t c) -> p t c", t=QT)
        columns = (psL, psG)
        halves = [slice(c * BANK, (c + 1) * BANK) for c in range(D // BANK)]
        LOGIT_TILE, COUNT_TILE, SELECT_TILE = 0, 2, 3
        with nc.Block() as block:
            @block.sync
            def _(sp):
                for t in range(QT):
                    sp.wait_ge(done, t + 1)
                    sp.dma_start(out[t * P:(t + 1) * P, :], y[:, t, :]).then_inc(stored, 16)
                sp.wait_ge(stored, 16 * QT)

            @block.gpsimd
            def _(pool):
                pool.iota(index[:], pattern=[[0, 1]], base=0, channel_multiplier=1).then_inc(index_made, 1)

            @block.tensor
            def _(pe):
                def transpose_weights(k):
                    if k:
                        pe.wait_ge(w_low, k)
                    for n in range(NT):
                        last = pe.transpose(psW[:, n * P:(n + 1) * P], w_raw[:, n, k * P:(k + 1) * P], ident[:])
                    last.then_inc(w_transposed, 1)

                pe.wait_ge(inputs.c_loaded, 16)
                for k in range(KT):
                    last = pe.transpose(cT[:, k, :], c_raw[:, k * P:(k + 1) * P], ident[0:CLUSTERS, 0:CLUSTERS])
                last.then_inc(c_transposed, 1)
                pe.wait_ge(inputs.w_loaded, 16)
                transpose_weights(0)
                pe.wait_ge(c_low, 1)
                for k in range(KT):
                    for n, (c, a) in enumerate(((c_hi, yT_high), (c_hi, yT_low), (c_lo, yT_high))):
                        last = pe.matmul(psG[0:CLUSTERS, 0:NQ], c[:, k, :], a[:, k, :], start=(k == 0 and n == 0),
                                         stop=(k == KT - 1 and n == 2))
                last.then_inc(logits_T, 1)
                for k in range(KT):
                    if k + 1 < KT:
                        transpose_weights(k + 1)
                    pe.wait_ge(w_low, k + 1)
                    for t in range(QT):
                        for n, (a, w) in enumerate(((yT_high, w_hi), (yT_high, w_lo), (yT_low, w_hi))):
                            for cols in halves:
                                last = pe.matmul(psY[:, t, cols], a[:, k, t * P:(t + 1) * P], w[:, k, cols],
                                                 start=(k == 0 and n == 0), stop=(k == KT - 1 and n == 2))
                        if k == KT - 1:
                            last.then_inc(projected, 1)
                    if k == LOGIT_TILE:
                        pe.wait_ge(logits_copied, 1)
                        for t in range(QT):
                            last = pe.transpose(logit[:, t, :], logitT[:, t * P:(t + 1) * P], ident[0:CLUSTERS, 0:CLUSTERS])
                        last.then_inc(logits, 1)
                    if k == COUNT_TILE:
                        pe.wait_ge(hit, 1)
                        for t in range(QT):
                            last = pe.matmul(psL[0:CLUSTERS, 0:P], hits[:, t, :], ones[:], start=(t == 0), stop=(t == QT - 1))
                        last.then_inc(counted, 1)
                    if k == SELECT_TILE:
                        pe.wait_ge(cluster_ready, 1)
                        pe.wait_ge(onehot_made, 1)
                        for ps, cols in zip(columns, halves):
                            last = pe.matmul(ps[:], cluster_hit[:], onehot[:, cols], start=True, stop=True)
                        last.then_inc(selected, 1)

            @block.scalar
            def _(act):
                act.wait_ge(c_transposed, 1)
                act.copy(c_hi[:], cT).then_inc(c_high, 1)

                def weights(k):
                    act.wait_ge(w_transposed, k + 1)
                    act.copy(w_hi[:, k, :], psW[:]).then_inc(w_high, 1)

                weights(0)
                act.wait_ge(logits_T, 1)
                act.copy(logitT[:], psG[0:CLUSTERS, 0:NQ]).then_inc(logits_copied, 1)
                weights(1)
                act.wait_ge(negated, 1)
                for t in range(QT):
                    last = act.activation(exps[:, t, :], logit[:, t, :], ACT.Exp, bias=minus_peak[:, t:t + 1],
                                          scale=INV_TEMPERATURE, accum_out=sums[:, t:t + 1])
                last.then_inc(exped, 1)
                for k in range(2, KT):
                    weights(k)

            @block.vector
            def _(dve):
                dve.wait_ge(c_high, 1)
                dve.tensor_tensor(c_lo[:], cT, c_hi[:].bitcast(F32), ALU.subtract).then_inc(c_low, 1)

                def weights(k):
                    dve.wait_ge(w_high, k + 1)
                    dve.tensor_tensor(w_lo[:, k, :], psW[:], w_hi[:, k, :].bitcast(F32), ALU.subtract).then_inc(w_low, 1)

                weights(0)
                dve.wait_ge(inputs.assign_loaded, 16)
                dve.wait_ge(index_made, 1)
                dve.tensor_copy(index_f[:], index[:])
                dve.tensor_copy(assign_f[:], assign[:]).then_inc(indices, 1)
                weights(1)
                dve.wait_ge(logits, 1)
                dve.tensor_reduce(peak[:], logit, AX.X, ALU.max).then_inc(peaked, 1)
                dve.wait_ge(peaked, 1)
                dve.tensor_scalar(minus_peak[:], peak[:], -INV_TEMPERATURE, None, ALU.mult).then_inc(negated, 1)
                dve.wait_ge(indices, 1)
                dve.tensor_scalar(onehot[:], assign_f[:], index_f[:, 0:1], None, ALU.is_equal).then_inc(onehot_made, 1)
                weights(2)
                dve.wait_ge(exped, 1)
                dve.reciprocal(inverse[:], sums[:]).then_inc(inverted, 1)
                dve.wait_ge(inverted, 1)
                for t in range(QT):
                    last = dve.tensor_scalar(hits[:, t, :], exps[:, t, :], inverse[:, t:t + 1], THRESHOLD, ALU.mult, ALU.is_gt)
                last.then_inc(hit, 1)
                dve.wait_ge(hit, 1)
                dve.tensor_reduce(row_hit[:], hits[:], AX.X, ALU.max).then_inc(row_ready, 1)
                weights(3)
                dve.wait_ge(counted, 1)
                dve.tensor_scalar(cluster_hit[:], psL[0:CLUSTERS, 0:P], 0.5, None, ALU.is_gt).then_inc(cluster_ready, 1)
                weights(4)
                weights(5)
                dve.wait_ge(selected, 1)
                dve.wait_ge(row_ready, 1)
                for t in range(QT):
                    for ps, cols in zip(columns, halves):
                        last = dve.tensor_scalar(gate[:, t, cols], ps[:], row_hit[:, t:t + 1], None, ALU.mult)
                last.then_inc(gate_ready, 1)
                weights(6)
                dve.wait_ge(gate_ready, 1)
                dve.wait_ge(inputs.bias_loaded, 16)
                dve.tensor_tensor(base[:], gate[:], broadcast_outer(bias_sb[:], QT), ALU.mult).then_inc(bias_gated, 1)
                weights(7)
                dve.wait_ge(bias_gated, 1)
                dve.tensor_tensor(base[:], base[:], x[:], ALU.add).then_inc(base_ready, 1)
                dve.wait_ge(base_ready, 1)
                for t in range(QT):
                    dve.wait_ge(projected, t + 1)
                    dve.tensor_tensor(y[:, t, :], psY[:, t, :], gate[:, t, :], ALU.mult).then_inc(multiplied, 1)
                    dve.wait_ge(multiplied, t + 1)
                    dve.tensor_tensor(y[:, t, :], y[:, t, :], base[:, t, :], ALU.add).then_inc(done, 1)


def self_constants(nc, sems, ident, ones, ident_r, ones_r, minus_r, swap_r, triangle_qk, triangle_kq):
    with ExitStack() as stack:
        m = Scope(nc, stack, "sc")
        sem = make_sem(nc, sems, "sc")
        swap = m.sb("swap", [P, P])
        qk = m.sb("qk", [P, 2 * P])
        kq = m.sb("kq", [P, P])
        cleared, made = sem("cleared"), sem("made")
        with nc.Block() as block:
            @block.gpsimd
            def _(pool):
                pool.memset(swap[:], 0.0)
                pool.memset(qk[:], 0.0)
                pool.memset(kq[:], 0.0).then_inc(cleared, 1)
                pool.wait_ge(cleared, 1)
                pairs = swap[:].rearrange("p (i two) -> p i two", two=2)
                pool.affine_select(out=pairs[:, :, 0], in_=pairs[:, :, 0], compare_op=ALU.not_equal, fill=1.0, base=-1,
                                   pattern=[[-2, P // 2]], channel_multiplier=1)
                pool.affine_select(out=pairs[:, :, 1], in_=pairs[:, :, 1], compare_op=ALU.not_equal, fill=-1.0, base=0,
                                   pattern=[[-2, P // 2]], channel_multiplier=1)
                pool.affine_select(out=qk[:, P:2 * P], in_=qk[:, P:2 * P], compare_op=ALU.is_ge, fill=MASKED, base=0,
                                   pattern=[[-1, P]], channel_multiplier=1)
                pool.affine_select(out=kq[:], in_=kq[:], compare_op=ALU.is_ge, fill=MASKED, base=0,
                                   pattern=[[1, P]], channel_multiplier=-1).then_inc(made, 1)

            @block.vector
            def _(dve):
                dve.tensor_copy(ident_r[:], ident[:])
                dve.tensor_copy(ones_r[:], ones[:])
                dve.tensor_scalar(minus_r[:], ones[:], -1.0, 0.0, ALU.mult, ALU.add)
                dve.wait_ge(made, 1)
                dve.tensor_copy(swap_r[:], swap[:])
                dve.tensor_copy(triangle_qk[:], qk[:])
                dve.tensor_copy(triangle_kq[:], kq[:])


def perceiver_kernel(nc, x, context, Wq, Wk, Wv, Wo, xq_norm_w, xk_norm_w, wq_a, q_norm_w, wq_b, wkv, kv_norm_w, wo_a,
                     wo_b, sink, cos, sin, weight, bias, centroids, assignments, out):
    def scratch(name, shape):
        return nc.dram_tensor(name, shape, F32, kind="Internal").ap()

    keyT_high, keyT_low = (scratch(f"keyT_{p}", [XKV, HD, NK]) for p in ("high", "low"))
    val_high, val_low = (scratch(f"val_{p}", [XKV, P, RT, HD]) for p in ("high", "low"))
    xqT_high, xqT_low = (scratch(f"xqT_{p}", [XKV, HD, XQ]) for p in ("high", "low"))
    xoT_high, xoT_low = (scratch(f"xoT_{p}", [XKV, HD, XQ]) for p in ("high", "low"))
    x1 = scratch("x1", [NQ, D])
    sums, inverse = (scratch(name, [SG, QT * GH * P]) for name in ("sums", "inverse"))
    x, context, out = x[0], context[0], out[0]

    sems = Semaphores(nc)
    with ExitStack() as whole:
        top = Scope(nc, whole, "top")
        ident = top.sb("ident", [P, P])
        ident_bf = top.sb("ident_bf", [P, P], BF16)
        ones = top.sb("ones", [P, P])
        constants(nc, sems, ident, ident_bf, ones)

        with ExitStack() as stack:
            m = Scope(nc, stack, "cross")
            yT_high, yT_low = (m.sb(f"yT_{p}", [P, KT, NQ], F32R) for p in ("high", "low"))
            kv_weights = KeyValueWeights(nc, sems, m, Wk, Wv)
            with ExitStack() as inner:
                i = Scope(nc, inner, "queries")
                q_weights = QueryWeights(nc, sems, i, Wq)
                x_sb = i.sb("x", [P, QT, D])

                def load_query_weights(sp):
                    for s in range(2):
                        q_weights.load(sp, s, s)

                layernorm_transposed(nc, sems, "ln0", x_sb, ident, yT_high, yT_low, rows=x, meanwhile=load_query_weights)
                project_queries(nc, sems, q_weights, xq_norm_w, xk_norm_w, ident, yT_high, yT_low, xqT_high, xqT_low,
                                prefetch=kv_weights.load_first)
            project_keys_values(nc, sems, context, kv_weights, ident, yT_high, yT_low, keyT_high, keyT_low, val_high, val_low)
        cross_attention(nc, sems, ident, ones, keyT_high, keyT_low, val_high, val_low, xqT_high, xqT_low, xoT_high, xoT_low)

        with ExitStack() as stack:
            m = Scope(nc, stack, "self")
            ident_r, ones_r, minus_r, swap_r, triangle_kq = (
                m.sb(n, [P, P], F32R) for n in ("ident_r", "ones_r", "minus_r", "swap_r", "triangle_kq"))
            triangle_qk = m.sb("triangle_qk", [P, 2 * P], F32R)
            qrT_high, qrT_low = (m.sb(f"qrT_{p}", [P, LT, NQ], F32R) for p in ("high", "low"))
            kv_high, kv_low = (m.sb(f"kv_{p}", [P, QT, HD], F32R) for p in ("high", "low"))
            kvT_high, kvT_low = (m.sb(f"kvT_{p}", [P, NQ], F32R) for p in ("high", "low"))
            query_max = m.sb("query_max", [P, SG, QT, GH], F32R)
            sink_exp = m.sb("sink_exp", [P, SG, QT, GH])
            cos_sb, sin_sb = (m.sb(f"{n}_sb", [P, QT, PAIR]) for n in ("cos", "sin"))
            with ExitStack() as inner:
                i = Scope(nc, inner, "latent")
                x1_sb = i.sb("x1", [P, QT, D])
                cross_output(nc, sems, Wo, xoT_high, xoT_low, x, x1_sb)
                sems.release()
                x1_stored = sems.new("x1_stored")
                inputs = LatentInputs(nc, sems, i)
                yT_high, yT_low = (i.sb(f"yT_{p}", [P, KT, NQ], F32R) for p in ("high", "low"))
                self_constants(nc, sems, ident, ones, ident_r, ones_r, minus_r, swap_r, triangle_qk, triangle_kq)

                def load_inputs_and_store_x1(sp):
                    inputs.load(sp, wq_a, wkv, q_norm_w, kv_norm_w, cos, sin, cos_sb, sin_sb)
                    sp.dma_start(x1.rearrange("(t p) d -> p t d", p=P), x1_sb[:]).then_inc(x1_stored, 16)
                    sp.wait_ge(x1_stored, 16)

                layernorm_transposed(nc, sems, "ln1", x1_sb, ident, yT_high, yT_low, meanwhile=load_inputs_and_store_x1)
                latent_projections(nc, sems, inputs, cos_sb, sin_sb, ident, ident_bf, yT_high, yT_low,
                                   qrT_high, qrT_low, kv_high, kv_low, kvT_high, kvT_low)
            ogT = m.sb("ogT", [P, OTILES, NQ])
            with ExitStack() as inner:
                i = Scope(nc, inner, "heads")
                qT_high, qT_low = (i.sb(f"qT_{p}", [P, SG, QT, GH, P], F32R) for p in ("high", "low"))
                self_queries(nc, sems, wq_b, cos_sb, sin_sb, ident, ident_bf, qrT_high, qrT_low, qT_high, qT_low)
                self_maxima(nc, sems, sink, ident, kvT_high, qT_high, triangle_qk, ident_r, query_max, sink_exp)
                self_attention(nc, sems, ident, ident_r, ones_r, minus_r, triangle_kq, kv_high, kv_low, kvT_high, kvT_low,
                               query_max, sink_exp, qT_high, qT_low, sums, inverse)
                rotate_outputs(nc, sems, cos_sb, sin_sb, ident, ident_r, swap_r, qT_high, qT_low, inverse)
                grouped_projection(nc, sems, wo_a, ident_bf, qT_high, qT_low, ogT)
            sems.release()

            x2_sb = m.sb("x2", [P, QT, D])
            inputs = LinearInputs(nc, sems, m)
            output_projection(nc, sems, wo_b, ident_bf, ogT, x1, x2_sb,
                              meanwhile=lambda sp: inputs.load(sp, weight, bias, centroids, assignments))
            yT_high, yT_low = (m.sb(f"linear_yT_{p}", [P, KT, NQ], F32R) for p in ("high", "low"))
            layernorm_transposed(nc, sems, "ln2", x2_sb, ident, yT_high, yT_low)
            gated_linear(nc, sems, x2_sb, inputs, ident, ones, yT_high, yT_low, out)


_INS = ['x', 'ctx_4096', 'L0_xattn_Wq', 'L0_xattn_Wk', 'L0_xattn_Wv', 'L0_xattn_Wo', 'L0_xattn_q_norm_w', 'L0_xattn_k_norm_w',
        'L0_attn_wq_a', 'L0_attn_q_norm_w', 'L0_attn_wq_b', 'L0_attn_wkv', 'L0_attn_kv_norm_w', 'L0_attn_wo_a', 'L0_attn_wo_b',
        'L0_attn_attn_sink', 'L0_attn_cos', 'L0_attn_sin', 'L0_ffn_weight', 'L0_ffn_bias', 'L0_ffn_centroids', 'L0_ffn_assignments']


def kernel(**inputs):
    import numpy as _np
    import concourse.bacc as _bacc
    from concourse import mybir as _mybir
    from concourse.bass_utils import run_bass_kernel_spmd as _run

    nc = _bacc.Bacc("TRN2", target_bir_lowering=False, num_devices=1)
    arrays, args = {}, []
    for name in _INS:
        a = _np.ascontiguousarray(inputs[name])
        arrays[f"in_{name}_dram"] = a
        args.append(nc.dram_tensor(f"in_{name}_dram", a.shape, _mybir.dt.from_np(a.dtype), kind="ExternalInput").ap())
    args.append(nc.dram_tensor("out_dram", (1, NQ, D), F32, kind="ExternalOutput").ap())
    perceiver_kernel(nc, *args)
    return _run(nc, [arrays], core_ids=[0]).results[0]["out_dram"]
```
